# Optimizing a Trainium2 kernel written in Bass

```python
import numpy as np
import jax
import jax.numpy as jnp

def _softmax(x, axis=-1):
    return jax.nn.softmax(x, axis=axis)

def _gelu(x):
    return jax.nn.gelu(x, approximate=True)

def _silu(x):
    return jax.nn.silu(x)

def _sigmoid(x):
    return jax.nn.sigmoid(x)

def _layernorm(x, axis=-1, eps=1e-05):
    m = jnp.mean(x, axis=axis, keepdims=True)
    v = jnp.var(x, axis=axis, keepdims=True)
    return (x - m) / jnp.sqrt(v + eps)

def _scatter_add(tgt, idx, src, axis=0):
    return tgt.at[idx].add(src)

def _segment_sum(src, seg, n):
    return jax.ops.segment_sum(src, seg, n)
kernel_name = 'mk_gnn_resnorm_d2_gnn_r8_e44031'

def setup_inputs(seed: int=0):
    np.random.seed(seed)
    _w = jnp.asarray

    def _rec_inputs():
        import jax
        import jax.numpy as jnp
        _gk = jax.random.key(seed)
        x = -0.0001006 + 1 * jax.random.normal(jax.random.fold_in(_gk, 1), (6250, 96), jnp.float32)
        _s = jax.random.randint(jax.random.fold_in(_gk, 2), (100000,), 0, 6250, jnp.int32)
        _d = jax.random.randint(jax.random.fold_in(_gk, 3), (100000,), 0, 6250, jnp.int32)
        _loop = jnp.arange(6250, dtype=jnp.int32)
        src = jnp.concatenate([_s, _d, _loop])
        dst = jnp.concatenate([_d, _s, _loop])
        _o = jnp.argsort(dst, stable=True)
        src = src[_o]
        dst = dst[_o]
        edge_attr_32 = 0.000196303 + 1.00016 * jax.random.normal(jax.random.fold_in(_gk, 11), (206250, 32), jnp.float32)
        edge_attr_4 = 0.000714719 + 1.00021 * jax.random.normal(jax.random.fold_in(_gk, 12), (206250, 4), jnp.float32)
        return (x, src, dst, edge_attr_32, edge_attr_4)
    x, src, dst, edge_attr_32, edge_attr_4 = _rec_inputs()

    def _L0_gnn_setup():
        import jax, jax.numpy as jnp
        import numpy as np
        N_NODES = 6250
        N_EDGES = 100000
        IN_DIM = 96
        OUT_DIM = 96
        EDGE_DIM = 32
        BN_EPS = 1e-05
        key = jax.random.key(seed)
        ks = jax.random.split(key, 12)
        x = jax.random.normal(ks[0], (N_NODES, IN_DIM), dtype=jnp.float32)
        edge_index = jax.random.randint(ks[1], (2, N_EDGES), 0, N_NODES, dtype=jnp.int64)
        edge_attr = jax.random.normal(ks[2], (N_EDGES, EDGE_DIM), dtype=jnp.float32)
        We = jax.random.normal(ks[3], (EDGE_DIM, IN_DIM), dtype=jnp.float32) / np.sqrt(EDGE_DIM)
        be = jnp.zeros((IN_DIM,), dtype=jnp.float32)
        W1 = jax.random.normal(ks[4], (IN_DIM, OUT_DIM), dtype=jnp.float32) / np.sqrt(IN_DIM)
        b1 = jnp.zeros((OUT_DIM,), dtype=jnp.float32)
        W2 = jax.random.normal(ks[5], (OUT_DIM, OUT_DIM), dtype=jnp.float32) / np.sqrt(OUT_DIM)
        b2 = jnp.zeros((OUT_DIM,), dtype=jnp.float32)
        gamma = jnp.ones((OUT_DIM,), dtype=jnp.float32)
        beta = jnp.zeros((OUT_DIM,), dtype=jnp.float32)
        return {'x': x, 'edge_index': edge_index, 'edge_attr': edge_attr, 'We': We, 'be': be, 'W1': W1, 'b1': b1, 'W2': W2, 'b2': b2, 'gamma': gamma, 'beta': beta}
    _L0_gnn_all = _L0_gnn_setup()
    _L0_gnn_in = {k: v for k, v in _L0_gnn_all.items() if k in ('We', 'be', 'W1', 'b1', 'W2', 'b2', 'gamma', 'beta')}
    del _L0_gnn_all

    def _L1_gnn_setup():
        import jax, jax.numpy as jnp
        import numpy as np
        EPS = 1e-05

        def _mlp(h, W, b, gamma, beta):
            h = jax.nn.relu(h @ W + b)
            mu = jnp.mean(h, axis=0)
            var = jnp.mean(jnp.square(h - mu), axis=0)
            return gamma * (h - mu) * jax.lax.rsqrt(var + EPS) + beta
        key = jax.random.key(seed)
        ks = jax.random.split(key, 10)
        N, E, C_in, C_out, E_dim = (6250, 100000, 96, 96, 4)
        x = jax.random.normal(ks[0], (N, C_in), dtype=jnp.float32)
        edge_index = jax.random.randint(ks[1], (2, E), 0, N, dtype=jnp.int64)
        edge_attr = jax.random.normal(ks[2], (E, E_dim), dtype=jnp.float32)
        s = lambda fan_in: 1.0 / np.sqrt(fan_in)
        W_node = jax.random.uniform(ks[3], (C_in, C_out), jnp.float32, -s(C_in), s(C_in))
        b_node = jnp.zeros((C_out,), jnp.float32)
        g_node = jnp.ones((C_out,), jnp.float32)
        beta_node = jnp.zeros((C_out,), jnp.float32)
        W_edge = jax.random.uniform(ks[4], (E_dim, C_out), jnp.float32, -s(E_dim), s(E_dim))
        b_edge = jnp.zeros((C_out,), jnp.float32)
        g_edge = jnp.ones((C_out,), jnp.float32)
        beta_edge = jnp.zeros((C_out,), jnp.float32)
        M_in = 2 * C_in + C_out
        W_msg = jax.random.uniform(ks[5], (M_in, C_out), jnp.float32, -s(M_in), s(M_in))
        b_msg = jnp.zeros((C_out,), jnp.float32)
        g_msg = jnp.ones((C_out,), jnp.float32)
        beta_msg = jnp.zeros((C_out,), jnp.float32)
        return dict(x=x, edge_index=edge_index, edge_attr=edge_attr, W_node=W_node, b_node=b_node, g_node=g_node, beta_node=beta_node, W_edge=W_edge, b_edge=b_edge, g_edge=g_edge, beta_edge=beta_edge, W_msg=W_msg, b_msg=b_msg, g_msg=g_msg, beta_msg=beta_msg)
    _L1_gnn_all = _L1_gnn_setup()
    _L1_gnn_in = {k: v for k, v in _L1_gnn_all.items() if k in ('W_node', 'b_node', 'g_node', 'beta_node', 'W_edge', 'b_edge', 'g_edge', 'beta_edge', 'W_msg', 'b_msg', 'g_msg', 'beta_msg')}
    del _L1_gnn_all
    return {'x': x, 'src': src, 'dst': dst, 'edge_attr_32': edge_attr_32, 'edge_attr_4': edge_attr_4, 'L0_gnn_We': _L0_gnn_in['We'], 'L0_gnn_be': _L0_gnn_in['be'], 'L0_gnn_W1': _L0_gnn_in['W1'], 'L0_gnn_b1': _L0_gnn_in['b1'], 'L0_gnn_W2': _L0_gnn_in['W2'], 'L0_gnn_b2': _L0_gnn_in['b2'], 'L0_gnn_gamma': _L0_gnn_in['gamma'], 'L0_gnn_beta': _L0_gnn_in['beta'], 'L1_gnn_W_node': _L1_gnn_in['W_node'], 'L1_gnn_b_node': _L1_gnn_in['b_node'], 'L1_gnn_g_node': _L1_gnn_in['g_node'], 'L1_gnn_beta_node': _L1_gnn_in['beta_node'], 'L1_gnn_W_edge': _L1_gnn_in['W_edge'], 'L1_gnn_b_edge': _L1_gnn_in['b_edge'], 'L1_gnn_g_edge': _L1_gnn_in['g_edge'], 'L1_gnn_beta_edge': _L1_gnn_in['beta_edge'], 'L1_gnn_W_msg': _L1_gnn_in['W_msg'], 'L1_gnn_b_msg': _L1_gnn_in['b_msg'], 'L1_gnn_g_msg': _L1_gnn_in['g_msg'], 'L1_gnn_beta_msg': _L1_gnn_in['beta_msg']}

def reference(x, src, dst, edge_attr_32, edge_attr_4, L0_gnn_We, L0_gnn_be, L0_gnn_W1, L0_gnn_b1, L0_gnn_W2, L0_gnn_b2, L0_gnn_gamma, L0_gnn_beta, L1_gnn_W_node, L1_gnn_b_node, L1_gnn_g_node, L1_gnn_beta_node, L1_gnn_W_edge, L1_gnn_b_edge, L1_gnn_g_edge, L1_gnn_beta_edge, L1_gnn_W_msg, L1_gnn_b_msg, L1_gnn_g_msg, L1_gnn_beta_msg):
    import jax
    import jax.numpy as jnp

    def _L0_gnn_ref(x, edge_index, edge_attr, We, be, W1, b1, W2, b2, gamma, beta):
        import jax, jax.numpy as jnp
        import numpy as np
        N_NODES = 6250
        N_EDGES = 100000
        IN_DIM = 96
        OUT_DIM = 96
        EDGE_DIM = 32
        BN_EPS = 1e-05
        src = edge_index[0]
        dst = edge_index[1]
        msg = jax.nn.relu(x[src] + edge_attr @ We + be)
        aggr = jax.ops.segment_sum(msg, dst, num_segments=x.shape[0])
        h = x + aggr
        h = jax.nn.relu(h @ W1 + b1) @ W2 + b2
        mean = jnp.mean(h, axis=0)
        var = jnp.mean(jnp.square(h - mean), axis=0)
        h = (h - mean) * jax.lax.rsqrt(var + BN_EPS) * gamma + beta
        return jax.nn.relu(h)

    def _L1_gnn_ref(x, edge_index, edge_attr, W_node, b_node, g_node, beta_node, W_edge, b_edge, g_edge, beta_edge, W_msg, b_msg, g_msg, beta_msg):
        import jax, jax.numpy as jnp
        import numpy as np
        EPS = 1e-05

        def _mlp(h, W, b, gamma, beta):
            h = jax.nn.relu(h @ W + b)
            mu = jnp.mean(h, axis=0)
            var = jnp.mean(jnp.square(h - mu), axis=0)
            return gamma * (h - mu) * jax.lax.rsqrt(var + EPS) + beta
        node_feat = _mlp(x, W_node, b_node, g_node, beta_node)
        edge_feat = _mlp(edge_attr, W_edge, b_edge, g_edge, beta_edge)
        row, col = (edge_index[0], edge_index[1])
        message = jnp.concatenate([x[row], x[col], edge_feat], axis=1)
        message = _mlp(message, W_msg, b_msg, g_msg, beta_msg)
        agg = jax.ops.segment_sum(message, col, num_segments=node_feat.shape[0])
        return agg + node_feat
    edge_index = jnp.stack([src, dst])
    x = _layernorm(x + _L0_gnn_ref(x, edge_index, edge_attr_32, L0_gnn_We, L0_gnn_be, L0_gnn_W1, L0_gnn_b1, L0_gnn_W2, L0_gnn_b2, L0_gnn_gamma, L0_gnn_beta), axis=-1)
    x = _layernorm(x + _L1_gnn_ref(x, edge_index, edge_attr_4, L1_gnn_W_node, L1_gnn_b_node, L1_gnn_g_node, L1_gnn_beta_node, L1_gnn_W_edge, L1_gnn_b_edge, L1_gnn_g_edge, L1_gnn_beta_edge, L1_gnn_W_msg, L1_gnn_b_msg, L1_gnn_g_msg, L1_gnn_beta_msg), axis=-1)
    return x

_drawn_inputs = setup_inputs


def setup_inputs(seed=0):
    import zlib

    import numpy as np

    out = dict(_drawn_inputs(seed))
    spreads = {'L0_gnn_be': (0.0, 0.1),
     'L0_gnn_b1': (0.0, 0.8),
     'L0_gnn_b2': (0.0, 0.8),
     'L0_gnn_gamma': (1.0, 0.2),
     'L0_gnn_beta': (0.0, 0.1),
     'L1_gnn_b_node': (0.0, 0.8),
     'L1_gnn_g_node': (1.0, 0.6),
     'L1_gnn_beta_node': (0.0, 0.8),
     'L1_gnn_b_edge': (0.0, 0.1),
     'L1_gnn_g_edge': (1.0, 0.2),
     'L1_gnn_beta_edge': (0.0, 0.391),
     'L1_gnn_b_msg': (0.0, 0.1),
     'L1_gnn_g_msg': (1.0, 0.2),
     'L1_gnn_beta_msg': (0.0, 0.1)}
    factors = {}
    for name, (base, spread) in spreads.items():
        noise = np.random.default_rng([zlib.crc32(name.encode()), seed]).standard_normal(out[name].shape)
        drawn = base * np.exp(spread * noise) if base else spread * noise
        out[name] = jnp.asarray(drawn.astype(out[name].dtype))
    for name, factor in factors.items():
        out[name] = (out[name] * factor).astype(out[name].dtype)
    return out
```

```python
from contextlib import ExitStack

import concourse.bass as bass
from concourse import mybir

N = 6250
E = 206250
F = 96
D0 = 32
D1 = 4
P = 128
EPS = 1e-5
GROUP = 4
MACRO = GROUP * P
TILES = -(-E // P)
MACROS = -(-TILES // GROUP)
EPAD = MACROS * MACRO
SLOTS = 3
ROUNDS = (MACROS - 1) // SLOTS
WINDOW = 32
NODE_TILES = -(-N // P)
ROWS = (NODE_TILES + 1) * P
CHUNK = 512
CHUNKS = [(c, min(CHUNK, N - c)) for c in range(0, N, CHUNK)]
NC = len(CHUNKS)
TAIL = E - (TILES - 1) * P
assert MACROS == SLOTS * ROUNDS + 1 and TILES == MACROS * GROUP and ROWS >= N + 1 + P


def build(nc, x, x_t, src_tiles, dst_tiles, dst_first, dst_row, ea32_blocks, ea4_blocks,
          we_b, w1, w2, w_node, w_edge_b, w_msg, b_msg, node_vectors, out):
    fp32, i32 = mybir.dt.float32, mybir.dt.int32
    ALU, ACT, AX = mybir.AluOpType, mybir.ActivationFunctionType, mybir.AxisListType
    ds = bass.ds

    u_table = nc.dram_tensor("u_table", [ROWS, F], fp32, kind="Internal").ap()
    v_table = nc.dram_tensor("v_table", [ROWS, F], fp32, kind="Internal").ap()
    sum_table = [nc.dram_tensor(f"sum_table{n}", [ROWS, F + 1], fp32, kind="Internal").ap() for n in range(2)]

    ctx = ExitStack()
    with ctx:
        def sb(name, shape, dt=fp32):
            return ctx.enter_context(nc.sbuf_tensor(name, shape, dt))

        def sem(name):
            return ctx.enter_context(nc.semaphore(name))

        acc = sb("acc", [F + 1, ROWS])
        x1 = sb("x1", [F + 1, ROWS])
        work_a = sb("work_a", [P, ROWS])
        work_b = sb("work_b", [P, ROWS])
        dst_i = sb("dst_i", [P, TILES], i32)
        rel = sb("rel", [P, TILES])
        first_i = sb("first_i", [1, MACROS], i32)
        first_f = sb("first_f", [1, MACROS])
        first_all = sb("first_all", [P, MACROS])
        edge_sums = sb("edge_sums", [F, 2, MACROS])
        src_slot = [sb(f"src_slot{s}", [P, GROUP], i32) for s in range(SLOTS)]
        gath = [sb(f"gath{s}", [P, GROUP, F]) for s in range(SLOTS)]
        msg = [sb(f"msg{s}", [P, GROUP, F + 1]) for s in range(SLOTS)]
        msg_sq = [sb(f"msg_sq{s}", [P, GROUP, F]) for s in range(SLOTS)]
        onehot = [sb(f"onehot{s}", [P, GROUP, WINDOW]) for s in range(SLOTS)]
        ea32 = [sb(f"ea32_{s}", [D0 + 1, MACRO]) for s in range(SLOTS)]
        ea4 = [sb(f"ea4_{s}", [D1 + 1, MACRO]) for s in range(SLOTS)]
        edge_h = [sb(f"edge_h{s}", [F, MACRO]) for s in range(SLOTS)]
        dst_b = [sb(f"dst_b{s}", [WINDOW, MACRO], i32) for s in range(SLOTS)]
        onehot_t = [sb(f"onehot_t{s}", [WINDOW, MACRO]) for s in range(SLOTS)]
        v_win = [sb(f"v_win{s}", [WINDOW, F]) for s in range(SLOTS)]
        we_s = sb("we_s", [D0 + 1, F])
        w1_s = sb("w1_s", [F, F])
        w2_s = sb("w2_s", [F, F])
        wn_s = sb("wn_s", [F, F])
        wedge_s = sb("wedge_s", [D1 + 1, F])
        wmsg_s = sb("wmsg_s", [F, 3, F])
        bmsg_s = sb("bmsg_s", [1, F])
        vec = sb("vec", [F, 11])
        B1, B2, GAM0, BET0, BNODE, GNODE, BETNODE, GEDGE, BETEDGE, GMSG, BETMSG = range(11)
        wc_s = sb("wc_s", [F, F])
        uv_s = sb("uv_s", [F + 1, 2, F])
        ident = sb("ident", [P, P])
        before = sb("before", [P, P])
        mean_w = sb("mean_w", [F, F])
        ones = sb("ones", [P, P])
        tail_ones = sb("tail_ones", [P, 1])
        last_one = sb("last_one", [1, F + 1])
        spread = sb("spread", [F, F + 1])
        cols = sb("cols", [P, WINDOW])
        part = sb("part", [P, 1])
        dump = sb("dump", [P, 1])
        eps_s = sb("eps_s", [P, 1])
        in_window = sb("in_window", [P, 1])
        flag_f = sb("flag_f", [1, 1])
        flag_i = sb("flag_i", [1, 1], i32)
        chunk_sums = sb("chunk_sums", [F, NC])
        st = sb("st", [F, 32])
        scale_n = sb("scale_n", [F, F + 1])
        scale_m = sb("scale_m", [F, F + 1])
        mat_n = sb("mat_n", [F + 1, F])
        mat_m = sb("mat_m", [F + 1, F])
        bn6 = sb("bn6", [P, 2, GROUP, 6])
        mv = sb("mv", [P, 2, GROUP, 2])
        sd = sb("sd", [P, 2, GROUP])
        res = sb("res", [P, 2, GROUP, F])
        g_src = sb("g_src", [P, 1], i32)
        g_dst = sb("g_dst", [P, 1], i32)
        g_row = sb("g_row", [P, P], i32)
        g_dst_f = sb("g_dst_f", [P, 1])
        g_same = sb("g_same", [P, P])
        g_tmp = sb("g_tmp", [P, P])
        g_dup = sb("g_dup", [P, 1])
        g_isfirst = sb("g_isfirst", [P, 1])
        g_diff = sb("g_diff", [P, 1])
        g_to_f = sb("g_to_f", [P, 1])
        g_to = sb("g_to", [P, 1], i32)
        g_valid = sb("g_valid", [P, 1])
        g_cur = sb("g_cur", [P, F + 1])
        g_v = sb("g_v", [P, F])
        g_new = sb("g_new", [P, F + 1])

        bank = [ctx.enter_context(nc.psum_tensor(f"bank{i}", [P, 512], fp32)) for i in range(8)]
        pre_ps = [bank[s][:, 0:GROUP * F].rearrange("p (g f) -> p g f", g=GROUP) for s in range(SLOTS)]
        seg_ps = [bank[3 + s][:, 0:WINDOW] for s in range(SLOTS)]
        sq_ps = bank[6][0:F, 0:1]
        eh_ps = bank[7]

        loaded_idx = sem("loaded_idx")
        loaded_w = sem("loaded_w")
        loaded_x = sem("loaded_x")
        consts_ready = sem("consts_ready")
        pool_const = sem("pool_const")
        dve_step = sem("dve_step")
        first_ready = sem("first_ready")
        first_spread = sem("first_spread")
        window_counted = sem("window_counted")
        window_total = sem("window_total")
        flag_ready = sem("flag_ready")

        class Layer:
            def __init__(self, n):
                s = lambda name: sem(f"{name}_{n}")
                self.src_in = [s(f"src_in{h}") for h in range(SLOTS)]
                self.gathered = [s(f"gathered{h}") for h in range(SLOTS)]
                self.edges_in = [s(f"edges_in{h}") for h in range(SLOTS)]
                self.v_in = [s(f"v_in{h}") for h in range(SLOTS)]
                self.onehot_ready = s("onehot_ready")
                self.onehot_t_ready = s("onehot_t_ready")
                self.edge_mm = s("edge_mm")
                self.edge_relu = s("edge_relu")
                self.edge_sq = s("edge_sq")
                self.pre_mm = s("pre_mm")
                self.pre_ready = s("pre_ready")
                self.msg_ready = s("msg_ready")
                self.msg_sq_ready = s("msg_sq_ready")
                self.seg_mm = s("seg_mm")
                self.acc_added = s("acc_added")
                self.swept = s("swept")
                self.g_in = s("g_in")
                self.g_got = s("g_got")
                self.g_selected = s("g_selected")
                self.g_pre = s("g_pre")
                self.g_msg = s("g_msg")
                self.g_sum = s("g_sum")
                self.g_new = s("g_new")
                self.g_written = s("g_written")
                self.g_zero = s("g_zero")
                self.g_edge = s("g_edge")
                self.g_edge_relu = s("g_edge_relu")
                self.g_pmm = s("g_pmm")
                self.g_row_in = s("g_row_in")
                self.g_turned = s("g_turned")
                self.g_stored = s("g_stored")

        L = [Layer(0), Layer(1)]
        may_gather = sem("may_gather")
        h_ready = sem("h_ready")
        w1_mm = sem("w1_mm")
        r_ready = sem("r_ready")
        w2_mm = sem("w2_mm")
        h2_ready = sem("h2_ready")
        acc_cleared = sem("acc_cleared")
        mean0_ready = sem("mean0_ready")
        var0_ready = sem("var0_ready")
        sd0_ready = sem("sd0_ready")
        bn0_ready = sem("bn0_ready")
        y_ready = sem("y_ready")
        z_ready = sem("z_ready")
        mean_mm = sem("mean_mm")
        centred = sem("centred")
        csq_ready = sem("csq_ready")
        var_mm = sem("var_mm")
        csd_ready = sem("csd_ready")
        x1_ready = sem("x1_ready")
        evar_ready = sem("evar_ready")
        esd_ready = sem("esd_ready")
        eshift_ready = sem("eshift_ready")
        wc_ready = sem("wc_ready")
        uvw_mm = sem("uvw_mm")
        uvw_ready = sem("uvw_ready")
        uv_mm = sem("uv_mm")
        even_ready = sem("even_ready")
        odd_ready = sem("odd_ready")
        u_stored = sem("u_stored")
        v_stored = sem("v_stored")
        nf_mm = sem("nf_mm")
        nf_ready = sem("nf_ready")
        nmean_ready = sem("nmean_ready")
        nsq_ready = sem("nsq_ready")
        nf_row = sem("nf_row")
        msq_copied = sem("msq_copied")
        fvar_ready = sem("fvar_ready")
        fsd_ready = sem("fsd_ready")
        scales_ready = sem("scales_ready")
        mats_mm = sem("mats_mm")
        mats_ready = sem("mats_ready")
        fin_mm = sem("fin_mm")
        fin_var = sem("fin_var")
        fin_sd = sem("fin_sd")
        fin_ready = sem("fin_ready")
        out_stored = [sem(f"out_stored{s}") for s in range(2)]

        FIN = [(i, min(GROUP, NODE_TILES - i)) for i in range(0, NODE_TILES, GROUP)]
        UV_PAIRS = ROWS // P // 2
        STORE = 5
        rows_of = lambda i: min(P, N - i * P)

        def rows_ps(k, which):
            return bank[k % 3][:, 0:4 * F].rearrange("p (t k f) -> p t k f", t=2, k=2)[:, :, which, :]

        def staged(work, k):
            return work[:, 2 * k * F:2 * (k + 1) * F].rearrange("p (t f) -> p t f", t=2)

        def sweep(eng, step):
            for h in range(SLOTS):
                step(h, 0, h)
            with eng.Fori(1, ROUNDS) as q:
                for h in range(SLOTS):
                    step(q * SLOTS + h, q, h)
            step(MACROS - 1, ROUNDS, 0)

        def reused(q):
            return not (isinstance(q, int) and q == 0)

        def follows(m):
            return not (isinstance(m, int) and m == 0)

        block = ctx.enter_context(nc.Block())

        @block.sync
        def _(sp):
            sp.dma_start(first_i[:, :], dst_first).then_inc(loaded_idx, 16)
            sp.dma_start(dst_i[:, :], dst_tiles).then_inc(loaded_idx, 16)
            for to, of in ((we_s, we_b), (w1_s, w1), (w2_s, w2), (wn_s, w_node), (wedge_s, w_edge_b),
                           (bmsg_s, b_msg), (vec, node_vectors)):
                sp.dma_start(to[:, :], of).then_inc(loaded_w, 16)
            sp.dma_start(wmsg_s[:, :, :], w_msg.rearrange("(k p) f -> p k f", p=F)).then_inc(loaded_w, 16)
            sp.dma_start(x1[0:F, 0:N], x_t).then_inc(loaded_x, 16)

            def fast(n):
                s = L[n]

                def step(m, q, h):
                    if reused(q):
                        sp.wait_ge(s.gathered[h], q * (16 * GROUP))
                    sp.dma_start(src_slot[h][:, :], src_tiles[:, ds(m * GROUP, GROUP)]).then_inc(s.src_in[h], 16)
                    if n == 0:
                        if reused(q):
                            sp.wait_ge(s.edge_mm, m - (SLOTS - 1))
                        sp.dma_start(ea32[h][:, :], ea32_blocks[ds(m, 1), :, :].rearrange("a d e -> (a d) e")
                                     ).then_inc(s.edges_in[h], 16)
                    else:
                        if reused(q):
                            sp.wait_ge(s.pre_mm, m - (SLOTS - 1))
                        sp.dma_start(dst_b[h][:, :], dst_row[:, ds(m * MACRO, MACRO)].to_broadcast([WINDOW, MACRO])
                                     ).then_inc(s.edges_in[h], 16)
                    sp.dma_start(ea4[h][:, :], ea4_blocks[ds(m, 1), :, :].rearrange("a d e -> (a d) e")
                                 ).then_inc(s.edges_in[h], 16)
                    if n == 1:
                        base = sp.value_load(first_i[0:1, ds(m, 1)], min_val=0, max_val=N - 1)
                        sp.dma_start(v_win[h][:, :], v_table[ds(base, WINDOW), :]).then_inc(s.v_in[h], 16)

                sweep(sp, step)

            def general(n):
                s = L[n]
                sp.wait_ge(s.g_zero, 1)
                sp.dma_start(sum_table[n].rearrange("(p t) f -> p (t f)", p=P),
                             work_b[:, 0:ROWS // P * (F + 1)]).then_inc(s.g_written, 16)
                if n == 0:
                    def load_ea4(m):
                        sp.dma_start(ea4[0][:, :], ea4_blocks[ds(m, 1), :, :].rearrange("a d e -> (a d) e")
                                     ).then_inc(s.edges_in[0], 16)

                    load_ea4(0)
                    with sp.Fori(1, MACROS) as m:
                        sp.wait_ge(s.edge_mm, m)
                        load_ea4(m)
                    sp.wait_ge(s.edge_mm, MACROS)
                with sp.Fori(0, MACROS) as m:
                    for g in range(GROUP):
                        sp.wait_ge(s.g_written, m * (16 * GROUP) + 16 * (g + 1))
                        sp.dma_start(g_src[:, :], src_tiles[:, ds(m * GROUP + g, 1)], allow_slow_non_contiguous=True).then_inc(s.g_in, 16)
                        sp.dma_start(g_dst[:, :], dst_tiles[:, ds(m * GROUP + g, 1)], allow_slow_non_contiguous=True).then_inc(s.g_in, 16)
                        sp.dma_start(g_row[:, :], dst_row[:, ds(m * MACRO + g * P, P)].to_broadcast([P, P])
                                     ).then_inc(s.g_in, 16)
                        if n == 0:
                            sp.dma_start(ea32[0][:, 0:P], ea32_blocks[ds(m, 1), :, g * P:(g + 1) * P]
                                         .rearrange("a d e -> (a d) e")).then_inc(s.g_in, 16)
                        else:
                            sp.dma_start(ea4[0][:, 0:P], ea4_blocks[ds(m, 1), :, g * P:(g + 1) * P]
                                         .rearrange("a d e -> (a d) e")).then_inc(s.g_in, 16)
                sp.wait_ge(s.g_written, 16 * (TILES + 1))
                for i in range(ROWS // P):
                    if i:
                        sp.wait_ge(s.g_turned, i)
                    sp.dma_start(g_cur[:, :], sum_table[n][i * P:(i + 1) * P, :]).then_inc(s.g_row_in, 16)

            sp.wait_ge(flag_ready, 1)
            ordered = sp.value_load(flag_i[0:1, 0:1], min_val=0, max_val=1)
            with sp.If(ordered == 1):
                fast(0)
            with sp.Else():
                general(0)
            sp.wait_ge(L[0].swept, 1)

            for k in range(UV_PAIRS // STORE):
                t0, t1 = 2 * STORE * k, 2 * STORE * (k + 1)
                pairs = STORE * (k + 1)
                sp.wait_ge(even_ready, (pairs + 1) // 2)
                sp.wait_ge(odd_ready, pairs // 2)
                for work, table, stored in ((work_a, u_table, u_stored), (work_b, v_table, v_stored)):
                    sp.dma_start(table[t0 * P:t1 * P, :].rearrange("(t p) f -> p t f", p=P),
                                 work[:, t0 * F:t1 * F].rearrange("p (t f) -> p t f", f=F)).then_inc(stored, 16)
            sp.wait_ge(v_stored, 16 * (UV_PAIRS // STORE))

            sp.wait_ge(flag_ready, 1)
            ordered = sp.value_load(flag_i[0:1, 0:1], min_val=0, max_val=1)
            with sp.If(ordered == 1):
                fast(1)
            with sp.Else():
                general(1)
            sp.wait_ge(L[1].swept, 1)

            for k, (t0, nt) in enumerate(FIN):
                sp.wait_ge(fin_ready, k + 1)
                for i in range(nt):
                    r = rows_of(t0 + i)
                    sp.dma_start(out[(t0 + i) * P:(t0 + i) * P + r, :], res[0:r, k % 2, i, :]
                                 ).then_inc(out_stored[k % 2], 16)
            for s2 in range(2):
                sp.wait_ge(out_stored[s2], 16 * sum(nt for k, (_, nt) in enumerate(FIN) if k % 2 == s2))

        @block.gpsimd
        def _(pool):
            nc.gpsimd.iota(cols[:, :], [[1, WINDOW]], base=0, channel_multiplier=0,
                           allow_small_or_imprecise_dtypes=True).then_inc(pool_const, 1)
            nc.gpsimd.iota(part[:, :], [[0, 1]], base=0, channel_multiplier=1,
                           allow_small_or_imprecise_dtypes=True).then_inc(pool_const, 1)
            nc.gpsimd.iota(dump[:, :], [[0, 1]], base=N + 1, channel_multiplier=1,
                           allow_small_or_imprecise_dtypes=True).then_inc(pool_const, 1)
            nc.gpsimd.memset(ones[:, :], 1.0).then_inc(pool_const, 1)
            pool.wait_ge(pool_const, 4)
            nc.gpsimd.affine_select(out=ident[:, :], in_=ones[:, :], compare_op=ALU.is_equal, fill=0.0, base=0,
                                    pattern=[[1, P]], channel_multiplier=-1).then_inc(pool_const, 1)
            nc.gpsimd.affine_select(out=before[:, :], in_=ones[:, :], compare_op=ALU.is_gt, fill=0.0, base=0,
                                    pattern=[[-1, P]], channel_multiplier=1).then_inc(pool_const, 1)
            nc.gpsimd.affine_select(out=tail_ones[:, :], in_=ones[:, 0:1], compare_op=ALU.is_gt, fill=0.0, base=TAIL,
                                    pattern=[[0, 1]], channel_multiplier=-1).then_inc(pool_const, 1)
            nc.gpsimd.affine_select(out=last_one[:, :], in_=ones[0:1, 0:F + 1], compare_op=ALU.is_equal, fill=0.0,
                                    base=-F, pattern=[[1, F + 1]], channel_multiplier=0).then_inc(pool_const, 1)
            pool.wait_ge(pool_const, 8)

            def fast(n, table):
                s = L[n]

                def step(m, q, h):
                    pool.wait_ge(s.src_in[h], (q + 1) * 16)
                    if reused(q):
                        pool.wait_ge(s.msg_ready, m - (SLOTS - 1))
                    pool.sem_inc(may_gather, 1)
                    for g in range(GROUP):
                        nc.gpsimd.indirect_dma_start(
                            out=gath[h][:, g, :], out_offset=None, in_=table,
                            in_offset=bass.IndirectOffsetOnAxis(ap=src_slot[h][:, g:g + 1], axis=0),
                        ).then_inc(s.gathered[h], 16)

                sweep(pool, step)

            def general(n, table):
                s = L[n]
                got = 16 * (2 + n)
                with pool.Fori(0, TILES) as t:
                    pool.wait_ge(s.g_in, (t + 1) * 64)
                    pool.sem_inc(may_gather, 1)
                    nc.gpsimd.indirect_dma_start(
                        out=gath[0][:, 0, :], out_offset=None, in_=table,
                        in_offset=bass.IndirectOffsetOnAxis(ap=g_src[:, 0:1], axis=0)).then_inc(s.g_got, 16)
                    nc.gpsimd.indirect_dma_start(
                        out=g_cur[:, :], out_offset=None, in_=sum_table[n],
                        in_offset=bass.IndirectOffsetOnAxis(ap=g_dst[:, 0:1], axis=0)).then_inc(s.g_got, 16)
                    if n == 1:
                        nc.gpsimd.indirect_dma_start(
                            out=g_v[:, :], out_offset=None, in_=v_table,
                            in_offset=bass.IndirectOffsetOnAxis(ap=g_dst[:, 0:1], axis=0)).then_inc(s.g_got, 16)
                    pool.wait_ge(s.g_new, t + 1)
                    pool.sem_inc(may_gather, 1)
                    nc.gpsimd.indirect_dma_start(
                        out=sum_table[n], out_offset=bass.IndirectOffsetOnAxis(ap=g_to[:, 0:1], axis=0),
                        in_=g_new[:, :], in_offset=None).then_inc(s.g_written, 16)

            pool.wait_ge(flag_ready, 1)
            ordered = pool.value_load(flag_i[0:1, 0:1], min_val=0, max_val=1)
            with pool.If(ordered == 1):
                fast(0, x)
            with pool.Else():
                general(0, x)
            pool.wait_ge(u_stored, 16 * (UV_PAIRS // STORE))
            pool.wait_ge(v_stored, 16 * (UV_PAIRS // STORE))
            ordered = pool.value_load(flag_i[0:1, 0:1], min_val=0, max_val=1)
            with pool.If(ordered == 1):
                fast(1, u_table)
            with pool.Else():
                general(1, u_table)

        @block.scalar
        def _(act):
            def fast(n):
                s = L[n]

                def step(m, q, h):
                    act.wait_ge(s.edge_mm, m + 1)
                    if reused(q) and n == 1:
                        act.wait_ge(s.pre_mm, m - (SLOTS - 1))
                    if n == 0:
                        nc.scalar.activation(edge_h[h][:, :], eh_ps[0:F, :], ACT.Relu,
                                             accum_out=edge_sums[:, 0, ds(m, 1)]).then_inc(s.edge_relu, 1)
                        act.wait_ge(s.edge_relu, m + 1)
                        nc.scalar.activation(edge_h[h][:, :], edge_h[h][:, :], ACT.Square,
                                             accum_out=edge_sums[:, 1, ds(m, 1)]).then_inc(s.edge_sq, 1)
                    else:
                        nc.scalar.activation(edge_h[h][:, :], eh_ps[0:F, :], ACT.Relu).then_inc(s.edge_relu, 1)
                    act.wait_ge(s.pre_ready, m + 1)
                    if reused(q):
                        act.wait_ge(s.seg_mm, m - (SLOTS - 1))
                    nc.scalar.activation(msg[h][:, :, 0:F], gath[h][:, :, :], ACT.Relu).then_inc(s.msg_ready, 1)
                    if n == 1:
                        act.wait_ge(s.msg_ready, m + 1)
                        nc.scalar.activation(msg_sq[h][:, :, :], msg[h][:, :, 0:F], ACT.Square
                                             ).then_inc(s.msg_sq_ready, 1)

                sweep(act, step)

            def general(n):
                s = L[n]
                if n == 0:
                    with act.Fori(0, MACROS) as m:
                        act.wait_ge(s.edge_mm, m + 1)
                        nc.scalar.activation(edge_h[0][:, :], eh_ps[0:F, :], ACT.Relu,
                                             accum_out=edge_sums[:, 0, ds(m, 1)]).then_inc(s.edge_relu, 1)
                        act.wait_ge(s.edge_relu, m + 1)
                        nc.scalar.activation(edge_h[0][:, :], edge_h[0][:, :], ACT.Square,
                                             accum_out=edge_sums[:, 1, ds(m, 1)]).then_inc(s.edge_sq, 1)
                with act.Fori(0, TILES) as t:
                    if n == 1:
                        act.wait_ge(s.g_edge, t + 1)
                        nc.scalar.activation(edge_h[0][:, 0:P], eh_ps[0:F, 0:P], ACT.Relu).then_inc(s.g_edge_relu, 1)
                    act.wait_ge(s.g_pre, t + 1)
                    nc.scalar.activation(msg[0][:, 0, 0:F], gath[0][:, 0, :], ACT.Relu).then_inc(s.msg_ready, 1)
                    act.wait_ge(s.msg_ready, t + 1)
                    if n == 1:
                        nc.scalar.activation(msg_sq[0][:, 0, :], msg[0][:, 0, 0:F], ACT.Square).then_inc(s.g_msg, 1)
                    else:
                        nc.scalar.activation(gath[0][:, 1, :], gath[0][:, 0, :], ACT.Copy).then_inc(s.g_msg, 1)

            act.wait_ge(flag_ready, 1)
            ordered = act.value_load(flag_i[0:1, 0:1], min_val=0, max_val=1)
            with act.If(ordered == 1):
                fast(0)
            with act.Else():
                general(0)
            act.wait_ge(L[0].swept, 1)

            act.wait_ge(loaded_w, 16 * 8)

            def mlp_out(c):
                o, w = CHUNKS[c]
                act.wait_ge(w2_mm, c + 1)
                nc.scalar.activation(work_a[0:F, o:o + w], bank[4 + c % 2][0:F, 0:w], ACT.Identity,
                                     bias=vec[:, B2:B2 + 1], accum_out=chunk_sums[:, c:c + 1]).then_inc(h2_ready, 1)

            for c, (o, w) in enumerate(CHUNKS):
                act.wait_ge(w1_mm, c + 1)
                nc.scalar.activation(work_b[0:F, o:o + w], bank[c % 2][0:F, 0:w], ACT.Relu,
                                     bias=vec[:, B1:B1 + 1]).then_inc(r_ready, 1)
                if c:
                    mlp_out(c - 1)
            mlp_out(NC - 1)
            act.wait_ge(mean0_ready, 1)
            act.wait_ge(h2_ready, NC)
            nc.scalar.activation(work_b[0:F, 0:N], work_a[0:F, 0:N], ACT.Square, bias=st[:, 1:2],
                                 accum_out=st[:, 2:3]).then_inc(var0_ready, 1)
            act.wait_ge(var0_ready, 1)
            nc.scalar.activation(st[:, 3:4], st[:, 2:3], ACT.Sqrt, scale=1.0 / N, bias=eps_s[0:F, :]).then_inc(sd0_ready, 1)
            act.wait_ge(evar_ready, 1)
            nc.scalar.activation(st[:, 14:15], st[:, 13:14], ACT.Sqrt, bias=eps_s[0:F, :]).then_inc(esd_ready, 1)
            act.wait_ge(bn0_ready, 1)
            for c, (o, w) in enumerate(CHUNKS):
                nc.scalar.activation(work_b[0:F, o:o + w], work_a[0:F, o:o + w], ACT.Relu, scale=st[:, 5:6],
                                     bias=st[:, 6:7]).then_inc(y_ready, 1)

            def root(c):
                o, w = CHUNKS[c]
                act.wait_ge(var_mm, c + 1)
                nc.scalar.activation(work_b[0:F, o:o + w], bank[4 + c % 2][0:F, 0:w], ACT.Sqrt,
                                     bias=eps_s[0:F, :]).then_inc(csd_ready, 1)

            for c, (o, w) in enumerate(CHUNKS):
                act.wait_ge(centred, c + 1)
                nc.scalar.activation(work_b[0:F, o:o + w], x1[0:F, o:o + w], ACT.Square).then_inc(csq_ready, 1)
                if c:
                    root(c - 1)
            root(NC - 1)

            act.wait_ge(x1_ready, NC)
            for k in range(0, UV_PAIRS, 2):
                act.wait_ge(uv_mm, k + 1)
                nc.scalar.activation(staged(work_a, k), rows_ps(k, 0), ACT.Copy)
                nc.scalar.activation(staged(work_b, k), rows_ps(k, 1), ACT.Copy).then_inc(even_ready, 1)

            act.wait_ge(u_stored, 16 * (UV_PAIRS // STORE))
            for c, (o, w) in enumerate(CHUNKS):
                act.wait_ge(nf_mm, c + 1)
                nc.scalar.activation(work_a[0:F, o:o + w], bank[4 + c % 2][0:F, 0:w], ACT.Relu,
                                     bias=vec[:, BNODE:BNODE + 1], accum_out=chunk_sums[:, c:c + 1]).then_inc(nf_ready, 1)
            act.wait_ge(v_stored, 16 * (UV_PAIRS // STORE))
            act.wait_ge(nmean_ready, 1)
            nc.scalar.activation(work_b[0:F, 0:N], work_a[0:F, 0:N], ACT.Square, bias=st[:, 17:18],
                                 accum_out=st[:, 18:19]).then_inc(nsq_ready, 1)

            with act.If(ordered == 1):
                fast(1)
            with act.Else():
                general(1)
            act.wait_ge(L[1].swept, 1)

            act.wait_ge(fvar_ready, 1)
            nc.scalar.activation(st[:, 19:20], st[:, 18:19], ACT.Sqrt, scale=1.0 / N, bias=eps_s[0:F, :]).then_inc(fsd_ready, 1)
            nc.scalar.activation(st[:, 26:27], st[:, 25:26], ACT.Sqrt, bias=eps_s[0:F, :]).then_inc(fsd_ready, 1)
            for k, (t0, nt) in enumerate(FIN):
                act.wait_ge(fin_var, k + 1)
                nc.scalar.activation(sd[:, k % 2, 0:nt], mv[:, k % 2, 0:nt, 1], ACT.Sqrt,
                                     bias=eps_s[:, :]).then_inc(fin_sd, 1)

        @block.vector
        def _(dve):
            chain = [0]

            def link(ins):
                chain[0] += 1
                ins.then_inc(dve_step, 1)
                dve.wait_ge(dve_step, chain[0])

            link(nc.vector.memset(mean_w[:, :], 1.0 / F))
            link(nc.vector.memset(eps_s[:, :], EPS))
            link(nc.vector.memset(spread[:, :], 0.0))
            link(nc.vector.memset(x1[:, N:ROWS], 0.0))
            link(nc.vector.memset(x1[F:F + 1, :], 1.0))
            for s in range(SLOTS):
                link(nc.vector.memset(msg[s][:, :, F:F + 1], 1.0))
            nc.vector.memset(acc[:, :], 0.0).then_inc(L[0].acc_added, 1)

            dve.wait_ge(loaded_idx, 32)
            dve.wait_ge(pool_const, 8)
            nc.vector.tensor_copy(first_f[:, :], first_i[:, :]).then_inc(first_ready, 1)
            dve.wait_ge(first_spread, 1)
            link(nc.vector.tensor_copy(first_all[:, :], bank[0][:, 0:MACROS]))
            link(nc.vector.tensor_tensor(rel[:, :].rearrange("p (m g) -> p m g", g=GROUP),
                                         dst_i[:, :].rearrange("p (m g) -> p m g", g=GROUP),
                                         first_all[:, :].unsqueeze(2).to_broadcast([P, MACROS, GROUP]), ALU.subtract))
            link(nc.vector.tensor_scalar(work_a[:, 0:TILES], rel[:, :], 0.0, None, ALU.is_ge))
            nc.vector.scalar_tensor_tensor(work_b[:, 0:TILES], rel[:, :], float(WINDOW), work_a[:, 0:TILES], ALU.is_lt,
                                           ALU.mult, accum_out=in_window[:, :]).then_inc(window_counted, 1)
            dve.wait_ge(window_total, 1)
            link(nc.vector.tensor_scalar(flag_f[:, :], bank[1][0:1, 0:1], float(EPAD), None, ALU.is_equal))
            dve.wait_ge(window_counted, 1)
            nc.vector.tensor_copy(flag_i[:, :], flag_f[:, :]).then_inc(flag_ready, 1)
            dve.wait_ge(flag_ready, 1)
            ordered = dve.value_load(flag_i[0:1, 0:1], min_val=0, max_val=1)

            def fast(n):
                s = L[n]
                height = F + 1 if n == 0 else F

                def add_window(m, h):
                    dve.wait_ge(s.seg_mm, m + 1)
                    base = dve.value_load(first_i[0:1, ds(m, 1)], min_val=0, max_val=N - 1)
                    dve.wait_ge(s.acc_added, m + 1)
                    at = acc[0:height, ds(base, WINDOW)]
                    nc.vector.tensor_tensor(at, at, seg_ps[h][0:height, :], ALU.add).then_inc(s.acc_added, 1)

                def step(m, q, h):
                    if reused(q):
                        dve.wait_ge(s.seg_mm, m - (SLOTS - 1))
                    nc.vector.tensor_tensor(
                        onehot[h][:, :, :], rel[:, ds(m * GROUP, GROUP)].unsqueeze(2).to_broadcast([P, GROUP, WINDOW]),
                        cols[:, :].unsqueeze(1).to_broadcast([P, GROUP, WINDOW]), ALU.is_equal).then_inc(s.onehot_ready, 1)
                    if n == 1:
                        dve.wait_ge(s.edges_in[h], (q + 1) * 32)
                        if reused(q):
                            dve.wait_ge(s.pre_mm, m - (SLOTS - 1))
                        nc.vector.tensor_scalar(onehot_t[h][:, :], dst_b[h][:, :], first_all[0:WINDOW, ds(m, 1)],
                                                part[0:WINDOW, :], ALU.subtract, ALU.is_equal).then_inc(s.onehot_t_ready, 1)
                    dve.wait_ge(s.pre_mm, m + 1)
                    dve.wait_ge(s.gathered[h], (q + 1) * (16 * GROUP))
                    nc.vector.tensor_tensor(gath[h][:, :, :], gath[h][:, :, :], pre_ps[h], ALU.add).then_inc(s.pre_ready, 1)
                    if follows(m):
                        add_window(m - 1, (h - 1) % SLOTS)

                sweep(dve, step)
                add_window(MACROS - 1, 0)
                dve.wait_ge(s.edge_relu, MACROS)
                dve.wait_ge(s.msg_ready, MACROS)
                if n == 0:
                    dve.wait_ge(s.edge_sq, MACROS)
                else:
                    dve.wait_ge(s.msg_sq_ready, MACROS)
                    dve.wait_ge(s.onehot_t_ready, MACROS)
                    for h in range(SLOTS):
                        dve.wait_ge(s.v_in[h], 16 * (ROUNDS + (h == 0)))
                for h in range(SLOTS):
                    dve.wait_ge(s.src_in[h], 16 * (ROUNDS + (h == 0)))
                    dve.wait_ge(s.edges_in[h], 32 * (ROUNDS + (h == 0)))
                dve.wait_ge(s.acc_added, MACROS + 1)

            def general(n):
                s = L[n]
                dve.wait_ge(s.acc_added, 1)
                nc.vector.memset(work_b[:, :], 0.0).then_inc(s.g_zero, 1)
                own = sem(f"g_dve_{n}")
                STEPS = 7
                with dve.Fori(0, TILES) as t:
                    def then(k, ins):
                        ins.then_inc(own, 1)
                        dve.wait_ge(own, t * STEPS + k)
                    dve.wait_ge(s.g_in, (t + 1) * 64)
                    then(1, nc.vector.tensor_copy(g_dst_f[:, :], g_dst[:, :]))
                    then(2, nc.vector.tensor_scalar(g_same[:, :], g_row[:, :], g_dst_f[:, :], None, ALU.is_equal))
                    then(3, nc.vector.tensor_tensor(g_tmp[:, :], g_same[:, :], before[:, :], ALU.mult))
                    then(4, nc.vector.tensor_reduce(g_dup[:, :], g_tmp[:, :], AX.X, ALU.add))
                    then(5, nc.vector.tensor_scalar(g_isfirst[:, :], g_dup[:, :], 0.0, None, ALU.is_equal))
                    then(6, nc.vector.tensor_tensor(g_diff[:, :], g_dst_f[:, :], dump[:, :], ALU.subtract))
                    then(7, nc.vector.scalar_tensor_tensor(g_to_f[:, :], g_diff[:, :], g_isfirst[:, :], dump[:, :],
                                                           ALU.mult, ALU.add))
                    nc.vector.tensor_copy(g_to[:, :], g_to_f[:, :]).then_inc(s.g_selected, 1)
                    nc.vector.tensor_scalar(g_valid[:, :], g_dst_f[:, :], float(N), None, ALU.is_lt).then_inc(s.g_selected, 1)
                    dve.wait_ge(s.g_pmm, t + 1)
                    dve.wait_ge(s.g_got, (t + 1) * (16 * (2 + n)))
                    if n == 1:
                        nc.vector.tensor_tensor(g_v[:, :], g_v[:, :], pre_ps[0][:, 0, :], ALU.add).then_inc(s.onehot_ready, 1)
                        dve.wait_ge(s.onehot_ready, t + 1)
                        nc.vector.tensor_tensor(gath[0][:, 0, :], gath[0][:, 0, :], g_v[:, :], ALU.add).then_inc(s.g_pre, 1)
                    else:
                        nc.vector.tensor_tensor(gath[0][:, 0, :], gath[0][:, 0, :], pre_ps[0][:, 0, :], ALU.add
                                                ).then_inc(s.g_pre, 1)
                    dve.wait_ge(s.g_sum, t + 1)
                    nc.vector.tensor_tensor(g_new[:, :], g_cur[:, :], bank[3][:, 0:F + 1], ALU.add).then_inc(s.g_new, 1)
                height = F + 1 if n == 0 else F
                for i in range(ROWS // P):
                    dve.wait_ge(s.g_turned, i + 1)
                    nc.vector.tensor_copy(acc[0:height, i * P:(i + 1) * P], bank[i % 2][0:height, 0:P]).then_inc(s.g_stored, 1)
                dve.wait_ge(s.g_stored, ROWS // P)
                dve.wait_ge(s.g_msg, TILES)
                dve.wait_ge(s.g_selected, 2 * TILES)
                dve.wait_ge(s.g_written, 16 * (TILES + 1))
                dve.wait_ge(s.g_row_in, 16 * (ROWS // P))
                if n == 0:
                    dve.wait_ge(s.edges_in[0], 16 * MACROS)
                    dve.wait_ge(s.edge_sq, MACROS)
                else:
                    dve.wait_ge(s.g_edge_relu, TILES)

            with dve.If(ordered == 1):
                fast(0)
            with dve.Else():
                general(0)
            nc.vector.memset(st[:, :], 0.0).then_inc(L[0].swept, 1)
            dve.wait_ge(L[0].swept, 1)

            dve.wait_ge(loaded_x, 16)
            for c, (o, w) in enumerate(CHUNKS):
                nc.vector.tensor_tensor(work_a[0:F, o:o + w], x1[0:F, o:o + w], acc[0:F, o:o + w], ALU.add
                                        ).then_inc(h_ready, 1)
            dve.wait_ge(h_ready, NC)
            nc.vector.memset(acc[0:F, :], 0.0).then_inc(L[1].acc_added, 1)
            link(nc.vector.tensor_reduce(st[:, 8:9], edge_sums[:, 0, :], AX.X, ALU.add))
            link(nc.vector.tensor_reduce(st[:, 9:10], edge_sums[:, 1, :], AX.X, ALU.add))
            link(nc.vector.tensor_scalar(st[:, 10:12], st[:, 8:10], 1.0 / E, None, ALU.mult))
            link(nc.vector.tensor_tensor(st[:, 12:13], st[:, 10:11], st[:, 10:11], ALU.mult))
            nc.vector.tensor_tensor(st[:, 13:14], st[:, 11:12], st[:, 12:13], ALU.subtract).then_inc(evar_ready, 1)
            dve.wait_ge(h2_ready, NC)
            link(nc.vector.tensor_reduce(st[:, 0:1], chunk_sums[:, :], AX.X, ALU.add))
            nc.vector.tensor_scalar(st[:, 1:2], st[:, 0:1], -1.0 / N, None, ALU.mult).then_inc(mean0_ready, 1)
            dve.wait_ge(mean0_ready, 1)
            dve.wait_ge(sd0_ready, 1)
            link(nc.vector.reciprocal(st[:, 4:5], st[:, 3:4]))
            link(nc.vector.tensor_tensor(st[:, 5:6], st[:, 4:5], vec[:, GAM0:GAM0 + 1], ALU.mult))
            nc.vector.scalar_tensor_tensor(st[:, 6:7], st[:, 1:2], st[:, 5:6], vec[:, BET0:BET0 + 1],
                                           ALU.mult, ALU.add).then_inc(bn0_ready, 1)
            dve.wait_ge(esd_ready, 1)
            link(nc.vector.reciprocal(st[:, 15:16], st[:, 14:15]))
            link(nc.vector.tensor_tensor(st[:, 16:17], st[:, 15:16], vec[:, GEDGE:GEDGE + 1], ALU.mult))
            nc.vector.tensor_scalar(wc_s[:, :], wmsg_s[:, 2, :], st[:, 16:17], None, ALU.mult).then_inc(wc_ready, 1)
            link(nc.vector.tensor_tensor(st[:, 27:28], st[:, 10:11], st[:, 16:17], ALU.mult))
            nc.vector.tensor_tensor(spread[:, F:F + 1], vec[:, BETEDGE:BETEDGE + 1], st[:, 27:28], ALU.subtract
                                    ).then_inc(eshift_ready, 1)
            dve.wait_ge(uvw_mm, 1)
            nc.vector.tensor_copy(uv_s[:, :, :], bank[3][0:F + 1, 0:2 * F].rearrange("p (k f) -> p k f", k=2)
                                  ).then_inc(uvw_ready, 1)

            dve.wait_ge(bn0_ready, 1)
            for c, (o, w) in enumerate(CHUNKS):
                dve.wait_ge(y_ready, c + 1)
                nc.vector.tensor_tensor(work_a[0:F, o:o + w], work_b[0:F, o:o + w], x1[0:F, o:o + w], ALU.add
                                        ).then_inc(z_ready, 1)

            def normalise(c):
                o, w = CHUNKS[c]
                dve.wait_ge(csd_ready, c + 1)
                link(nc.vector.reciprocal(work_b[0:F, o:o + w], work_b[0:F, o:o + w]))
                nc.vector.tensor_tensor(x1[0:F, o:o + w], x1[0:F, o:o + w], work_b[0:F, o:o + w], ALU.mult
                                        ).then_inc(x1_ready, 1)

            dve.wait_ge(z_ready, NC)
            for c, (o, w) in enumerate(CHUNKS):
                dve.wait_ge(mean_mm, c + 1)
                nc.vector.tensor_tensor(x1[0:F, o:o + w], work_a[0:F, o:o + w], bank[c % 2][0:F, 0:w], ALU.subtract
                                        ).then_inc(centred, 1)
                if c:
                    normalise(c - 1)
            normalise(NC - 1)
            dve.wait_ge(x1_ready, NC)

            for k in range(1, UV_PAIRS, 2):
                dve.wait_ge(uv_mm, k + 1)
                nc.vector.tensor_copy(staged(work_a, k), rows_ps(k, 0))
                nc.vector.tensor_copy(staged(work_b, k), rows_ps(k, 1)).then_inc(odd_ready, 1)
            dve.wait_ge(u_stored, 16 * (UV_PAIRS // STORE))
            nc.vector.memset(work_a[0:F, N:ROWS], 0.0).then_inc(nf_row, 1)
            nc.vector.memset(work_a[F:F + 1, 0:ROWS], 1.0).then_inc(nf_row, 1)
            dve.wait_ge(nf_ready, NC)
            link(nc.vector.tensor_reduce(st[:, 20:21], chunk_sums[:, :], AX.X, ALU.add))
            nc.vector.tensor_scalar(st[:, 17:18], st[:, 20:21], -1.0 / N, None, ALU.mult).then_inc(nmean_ready, 1)
            dve.wait_ge(nsq_ready, 1)

            with dve.If(ordered == 1):
                fast(1)
            with dve.Else():
                general(1)
            nc.vector.tensor_copy(st[:, 21:22], sq_ps).then_inc(L[1].swept, 1)
            dve.wait_ge(L[1].swept, 1)

            link(nc.vector.tensor_reduce(st[:, 22:23], acc[0:F, 0:N], AX.X, ALU.add))
            link(nc.vector.tensor_scalar(st[:, 23:24], st[:, 22:23], -1.0 / E, None, ALU.mult))
            link(nc.vector.tensor_tensor(st[:, 24:25], st[:, 23:24], st[:, 23:24], ALU.mult))
            nc.vector.scalar_tensor_tensor(st[:, 25:26], st[:, 21:22], 1.0 / E, st[:, 24:25],
                                           ALU.mult, ALU.subtract).then_inc(fvar_ready, 1)
            dve.wait_ge(fvar_ready, 1)
            dve.wait_ge(fsd_ready, 2)
            link(nc.vector.reciprocal(st[:, 28:29], st[:, 19:20]))
            link(nc.vector.reciprocal(st[:, 29:30], st[:, 26:27]))
            link(nc.vector.tensor_tensor(st[:, 28:29], st[:, 28:29], vec[:, GNODE:GNODE + 1], ALU.mult))
            link(nc.vector.tensor_tensor(st[:, 29:30], st[:, 29:30], vec[:, GMSG:GMSG + 1], ALU.mult))
            link(nc.vector.tensor_scalar(scale_n[:, 0:F], ident[0:F, 0:F], st[:, 28:29], None, ALU.mult))
            link(nc.vector.tensor_scalar(scale_m[:, 0:F], ident[0:F, 0:F], st[:, 29:30], None, ALU.mult))
            link(nc.vector.scalar_tensor_tensor(scale_n[:, F:F + 1], st[:, 17:18], st[:, 28:29],
                                                vec[:, BETNODE:BETNODE + 1], ALU.mult, ALU.add))
            nc.vector.scalar_tensor_tensor(scale_m[:, F:F + 1], st[:, 23:24], st[:, 29:30], vec[:, BETMSG:BETMSG + 1],
                                           ALU.mult, ALU.add).then_inc(scales_ready, 1)
            dve.wait_ge(mats_mm, 1)
            link(nc.vector.tensor_copy(mat_n[:, :], bank[0][0:F + 1, 0:F]))
            nc.vector.tensor_copy(mat_m[:, :], bank[1][0:F + 1, 0:F]).then_inc(mats_ready, 1)

            for k, (t0, nt) in enumerate(FIN):
                b = k % 2
                ps = bank[k % 4][:, 0:GROUP * F].rearrange("p (g f) -> p g f", g=GROUP)
                dve.wait_ge(fin_mm, k + 1)
                for i in range(nt):
                    last = nc.vector.bn_stats(bn6[:, b, i, :], ps[:, i, :])
                link(last)
                for i in range(nt):
                    last = nc.vector.bn_aggr(mv[:, b, i, :], bn6[:, b, i, :])
                last.then_inc(fin_var, 1)
                dve.wait_ge(fin_var, k + 1)
                dve.wait_ge(fin_sd, k + 1)
                link(nc.vector.reciprocal(sd[:, b, 0:nt], sd[:, b, 0:nt]))
                if k >= 2:
                    dve.wait_ge(out_stored[b], 16 * GROUP * (k // 2))
                for i in range(nt):
                    last = nc.vector.tensor_scalar(res[:, b, i, :], ps[:, i, :], mv[:, b, i, 0:1], sd[:, b, i:i + 1],
                                                   ALU.subtract, ALU.mult)
                last.then_inc(fin_ready, 1)

        @block.tensor
        def _(pe):
            pe.wait_ge(pool_const, 8)
            pe.wait_ge(first_ready, 1)
            nc.tensor.matmul(bank[0][:, 0:MACROS], ones[0:1, :], first_f[:, :], start=True, stop=True).then_inc(first_spread, 1)
            pe.wait_ge(window_counted, 1)
            nc.tensor.matmul(bank[1][0:1, 0:1], in_window[:, :], ones[:, 0:1], start=True, stop=True).then_inc(window_total, 1)
            pe.wait_ge(loaded_w, 16 * 8)

            def fast(n):
                s = L[n]
                height = F + 1 if n == 0 else F

                def segments(m, h, last):
                    pe.wait_ge(s.msg_ready if n == 0 else s.msg_sq_ready, m + 1)
                    pe.wait_ge(s.onehot_ready, m + 1)
                    if not isinstance(m, int) or m >= SLOTS:
                        pe.wait_ge(s.acc_added, m - (SLOTS - 2))
                    if n == 1:
                        for g in range(GROUP):
                            real = tail_ones if last and g == GROUP - 1 else ones
                            nc.tensor.matmul(sq_ps, msg_sq[h][:, g, :], real[:, 0:1], start=(isinstance(m, int) and m == 0 and g == 0),
                                             stop=(last and g == GROUP - 1), skip_group_check=True)
                    for g in range(GROUP):
                        mm = nc.tensor.matmul(seg_ps[h][0:height, :], msg[h][:, g, 0:height], onehot[h][:, g, :],
                                              start=(g == 0), stop=(g == GROUP - 1), skip_group_check=True)
                    mm.then_inc(s.seg_mm, 1)

                def edge_features(m, q, h):
                    if follows(m):
                        pe.wait_ge(s.edge_relu, m)
                    nc.tensor.matmul(eh_ps[0:F, :], wedge_s[:, :], ea4[h][:, :], start=True, stop=True).then_inc(s.edge_mm, 1)

                def step(m, q, h):
                    pe.wait_ge(s.edges_in[h], (q + 1) * 32)
                    if n == 1:
                        edge_features(m, q, h)
                        if follows(m):
                            segments(m - 1, (h - 1) % SLOTS, False)
                    if reused(q):
                        pe.wait_ge(s.pre_ready, m - (SLOTS - 1))
                    if n == 1:
                        pe.wait_ge(s.edge_relu, m + 1)
                        pe.wait_ge(s.onehot_t_ready, m + 1)
                        pe.wait_ge(s.v_in[h], (q + 1) * 16)
                    for g in range(GROUP):
                        tile = slice(g * P, (g + 1) * P)
                        if n == 0:
                            mm = nc.tensor.matmul(pre_ps[h][:, g, :], ea32[h][:, tile], we_s[:, :], start=True, stop=True)
                        else:
                            nc.tensor.matmul(pre_ps[h][:, g, :], edge_h[h][:, tile], wc_s[:, :], start=True, stop=False)
                            mm = nc.tensor.matmul(pre_ps[h][:, g, :], onehot_t[h][:, tile], v_win[h][:, :],
                                                  start=False, stop=True)
                    mm.then_inc(s.pre_mm, 1)
                    if n == 0:
                        edge_features(m, q, h)
                        if follows(m):
                            segments(m - 1, (h - 1) % SLOTS, False)

                sweep(pe, step)
                segments(MACROS - 1, 0, True)

            def general(n):
                s = L[n]
                if n == 0:
                    def edge_features(m):
                        pe.wait_ge(s.edges_in[0], (m + 1) * 16)
                        nc.tensor.matmul(eh_ps[0:F, :], wedge_s[:, :], ea4[0][:, :], start=True, stop=True
                                         ).then_inc(s.edge_mm, 1)

                    edge_features(0)
                    with pe.Fori(1, MACROS) as m:
                        pe.wait_ge(s.edge_sq, m)
                        edge_features(m)
                else:
                    pe.wait_ge(s.g_zero, 1)
                    nc.tensor.matmul(sq_ps, work_b[:, 0:F], ones[:, 0:1], start=True, stop=False, skip_group_check=True)
                with pe.Fori(0, TILES) as t:
                    pe.wait_ge(s.g_in, (t + 1) * 64)
                    if n == 0:
                        nc.tensor.matmul(pre_ps[0][:, 0, :], ea32[0][:, 0:P], we_s[:, :], start=True, stop=True
                                         ).then_inc(s.g_pmm, 1)
                    else:
                        nc.tensor.matmul(eh_ps[0:F, 0:P], wedge_s[:, :], ea4[0][:, 0:P], start=True, stop=True
                                         ).then_inc(s.g_edge, 1)
                        pe.wait_ge(s.g_edge_relu, t + 1)
                        nc.tensor.matmul(pre_ps[0][:, 0, :], edge_h[0][:, 0:P], wc_s[:, :], start=True, stop=True
                                         ).then_inc(s.g_pmm, 1)
                    pe.wait_ge(s.g_msg, t + 1)
                    pe.wait_ge(s.g_selected, (t + 1) * 2)
                    if n == 1:
                        nc.tensor.matmul(sq_ps, msg_sq[0][:, 0, :], g_valid[:, :], start=False, stop=False,
                                         skip_group_check=True)
                    nc.tensor.matmul(bank[3][:, 0:F + 1], g_same[:, :], msg[0][:, 0, :], start=True, stop=True
                                     ).then_inc(s.g_sum, 1)
                if n == 1:
                    nc.tensor.matmul(sq_ps, work_b[:, 0:F], ones[:, 0:1], start=False, stop=True, skip_group_check=True)
                for i in range(ROWS // P):
                    pe.wait_ge(s.g_row_in, 16 * (i + 1))
                    if i >= 2:
                        pe.wait_ge(s.g_stored, i - 1)
                    nc.tensor.matmul(bank[i % 2][0:F + 1, 0:P], g_cur[:, :], ident[:, :], start=True, stop=True
                                     ).then_inc(s.g_turned, 1)

            pe.wait_ge(flag_ready, 1)
            ordered = pe.value_load(flag_i[0:1, 0:1], min_val=0, max_val=1)
            with pe.If(ordered == 1):
                fast(0)
            with pe.Else():
                general(0)
            pe.wait_ge(L[0].swept, 1)

            def mlp_second(c):
                o, w = CHUNKS[c]
                pe.wait_ge(r_ready, c + 1)
                if c >= 2:
                    pe.wait_ge(h2_ready, c - 1)
                nc.tensor.matmul(bank[4 + c % 2][0:F, 0:w], w2_s[:, :], work_b[0:F, o:o + w], start=True, stop=True
                                 ).then_inc(w2_mm, 1)

            for c, (o, w) in enumerate(CHUNKS):
                pe.wait_ge(h_ready, c + 1)
                if c >= 2:
                    pe.wait_ge(r_ready, c - 1)
                nc.tensor.matmul(bank[c % 2][0:F, 0:w], w1_s[:, :], work_a[0:F, o:o + w], start=True, stop=True
                                 ).then_inc(w1_mm, 1)
                if c:
                    mlp_second(c - 1)
            mlp_second(NC - 1)
            pe.wait_ge(eshift_ready, 1)
            nc.tensor.matmul(bank[3][0:F + 1, 0:F], ident[0:F, 0:F + 1], wmsg_s[:, 0, :], start=True, stop=True)
            v_part = bank[3][0:F + 1, F:2 * F]
            nc.tensor.matmul(v_part, ident[0:F, 0:F + 1], wmsg_s[:, 1, :], start=True, stop=False)
            nc.tensor.matmul(v_part, spread[:, :], wmsg_s[:, 2, :], start=False, stop=False)
            nc.tensor.matmul(v_part, last_one[:, :], bmsg_s[:, :], start=False, stop=True).then_inc(uvw_mm, 1)

            def variances(c):
                o, w = CHUNKS[c]
                pe.wait_ge(csq_ready, c + 1)
                if c >= 2:
                    pe.wait_ge(csd_ready, c - 1)
                nc.tensor.matmul(bank[4 + c % 2][0:F, 0:w], mean_w[:, :], work_b[0:F, o:o + w], start=True, stop=True
                                 ).then_inc(var_mm, 1)

            for c, (o, w) in enumerate(CHUNKS):
                pe.wait_ge(z_ready, c + 1)
                if c >= 2:
                    pe.wait_ge(centred, c - 1)
                nc.tensor.matmul(bank[c % 2][0:F, 0:w], mean_w[:, :], work_a[0:F, o:o + w], start=True, stop=True
                                 ).then_inc(mean_mm, 1)
                if c:
                    variances(c - 1)
            variances(NC - 1)

            pe.wait_ge(uvw_ready, 1)
            pe.wait_ge(x1_ready, NC)
            for k in range(UV_PAIRS):
                if k >= 3:
                    ready = odd_ready if k % 2 == 0 else even_ready
                    pe.wait_ge(ready, (k - 3) // 2 + 1)
                for t in range(2):
                    mm = nc.tensor.matmul(bank[k % 3][:, t * 2 * F:(t + 1) * 2 * F], x1[:, (2 * k + t) * P:(2 * k + t + 1) * P],
                                          uv_s[:, :, :].rearrange("p k f -> p (k f)"), start=True, stop=True)
                mm.then_inc(uv_mm, 1)
            for c, (o, w) in enumerate(CHUNKS):
                if c >= 2:
                    pe.wait_ge(nf_ready, c - 1)
                nc.tensor.matmul(bank[4 + c % 2][0:F, 0:w], wn_s[:, :], x1[0:F, o:o + w], start=True, stop=True
                                 ).then_inc(nf_mm, 1)
            pe.wait_ge(even_ready, (UV_PAIRS + 1) // 2)
            pe.wait_ge(odd_ready, UV_PAIRS // 2)
            pe.wait_ge(nf_ready, NC)
            pe.wait_ge(L[1].acc_added, 1)

            with pe.If(ordered == 1):
                fast(1)
            with pe.Else():
                general(1)
            pe.wait_ge(L[1].swept, 1)

            pe.wait_ge(scales_ready, 1)
            nc.tensor.matmul(bank[0][0:F + 1, 0:F], scale_n[:, :], ident[0:F, 0:F], start=True, stop=True)
            nc.tensor.matmul(bank[1][0:F + 1, 0:F], scale_m[:, :], ident[0:F, 0:F], start=True, stop=True).then_inc(mats_mm, 1)
            pe.wait_ge(mats_ready, 1)
            pe.wait_ge(nf_row, 2)
            for k, (t0, nt) in enumerate(FIN):
                if k >= 4:
                    pe.wait_ge(fin_ready, k - 3)
                for i in range(nt):
                    nodes = slice((t0 + i) * P, (t0 + i + 1) * P)
                    to = bank[k % 4][:, i * F:(i + 1) * F]
                    nc.tensor.matmul(to, acc[:, nodes], mat_m[:, :], start=True, stop=False)
                    nc.tensor.matmul(to, work_a[0:F + 1, nodes], mat_n[:, :], start=False, stop=False)
                    mm = nc.tensor.matmul(to, x1[0:F, nodes], ident[0:F, 0:F], start=False, stop=True)
                mm.then_inc(fin_mm, 1)


def kernel(**inputs):
    import numpy as np
    import concourse.bacc as bacc
    from concourse import mybir as _mybir
    from concourse.bass_utils import run_bass_kernel_spmd

    a = {k: np.asarray(v) for k, v in inputs.items()}

    def padded(v, fill):
        out = np.full((EPAD,) + v.shape[1:], fill, v.dtype)
        out[:E] = v
        return out

    def blocks(v):
        out = np.zeros((MACROS, v.shape[1] + 1, MACRO), v.dtype)
        out[:, :-1, :] = padded(v, 0).reshape(MACROS, MACRO, -1).transpose(0, 2, 1)
        out[:, -1, :] = (np.arange(EPAD) < E).reshape(MACROS, MACRO)
        return out

    src, dst = padded(a["src"], 0), padded(a["dst"], N)
    vectors = ["L0_gnn_b1", "L0_gnn_b2", "L0_gnn_gamma", "L0_gnn_beta", "L1_gnn_b_node", "L1_gnn_g_node",
               "L1_gnn_beta_node", "L1_gnn_g_edge", "L1_gnn_beta_edge", "L1_gnn_g_msg", "L1_gnn_beta_msg"]
    arrays = {
        "x": a["x"],
        "x_t": a["x"].T,
        "src_tiles": src.reshape(TILES, P).T,
        "dst_tiles": dst.reshape(TILES, P).T,
        "dst_first": dst[::MACRO].reshape(1, MACROS),
        "dst_row": dst.reshape(1, EPAD),
        "ea32_blocks": blocks(a["edge_attr_32"]),
        "ea4_blocks": blocks(a["edge_attr_4"]),
        "we_b": np.concatenate([a["L0_gnn_We"], a["L0_gnn_be"][None]]),
        "w1": a["L0_gnn_W1"],
        "w2": a["L0_gnn_W2"],
        "w_node": a["L1_gnn_W_node"],
        "w_edge_b": np.concatenate([a["L1_gnn_W_edge"], a["L1_gnn_b_edge"][None]]),
        "w_msg": a["L1_gnn_W_msg"],
        "b_msg": a["L1_gnn_b_msg"][None],
        "node_vectors": np.stack([a[n] for n in vectors], axis=1),
    }
    arrays = {k: np.ascontiguousarray(v) for k, v in arrays.items()}
    nc = bacc.Bacc("TRN2", target_bir_lowering=False, num_devices=1)
    args = [nc.dram_tensor(k, v.shape, _mybir.dt.from_np(v.dtype), kind="ExternalInput").ap() for k, v in arrays.items()]
    out = nc.dram_tensor("out", (N, F), _mybir.dt.float32, kind="ExternalOutput").ap()
    build(nc, *args, out)
    r = run_bass_kernel_spmd(nc, [arrays], core_ids=[0])
    return r.results[0]["out"]
```

```python
from contextlib import ExitStack

import concourse.bass as bass
from concourse import mybir

N = 6250
E = 206250
F = 96
D0 = 32
D1 = 4
P = 128
EPS = 1e-5
GROUP = 4
MACRO = GROUP * P
TILES = -(-E // P)
MACROS = -(-TILES // GROUP)
SLOTS = 3
UNROLL = 2 * SLOTS
ROUNDS = (MACROS - 1) // UNROLL
UNIT = SLOTS * MACRO
EPAD = -(-MACROS // SLOTS) * UNIT
PARTS = 3
SPLIT = (D1 + 1) * EPAD // P // 2
WINDOW = 32
NODE_TILES = -(-N // P)
ROWS = (NODE_TILES + 1) * P
CHUNK = 512
CHUNKS = [(c, min(CHUNK, N - c)) for c in range(0, N, CHUNK)]
NC = len(CHUNKS)
TAIL = E - (TILES - 1) * P
assert MACROS == UNROLL * ROUNDS + 1 and TILES == MACROS * GROUP and ROWS >= N + 1 + P
assert 2 * P * SPLIT == (D1 + 1) * EPAD


def build(nc, x, x_t, src_tiles, dst_tiles, dst_first, dst_row, ea32_blocks, ea4_rows,
          we_b, w1, w2, w_node, w_edge_b, w_msg, b_msg, node_vectors, out):
    fp32, i32, bf16 = mybir.dt.float32, mybir.dt.int32, mybir.dt.bfloat16
    ALU, ACT, AX = mybir.AluOpType, mybir.ActivationFunctionType, mybir.AxisListType
    ds = bass.ds

    u_table = nc.dram_tensor("u_table", [ROWS, F], fp32, kind="Internal").ap()
    v_table = nc.dram_tensor("v_table", [ROWS, F], fp32, kind="Internal").ap()
    ea4_parts = nc.dram_tensor("ea4_parts", [PARTS * (D1 + 1), EPAD], bf16, kind="Internal").ap()
    v_parts = nc.dram_tensor("v_parts", [PARTS, ROWS, F], bf16, kind="Internal").ap()
    sum_table = [nc.dram_tensor(f"sum_table{n}", [ROWS, F + 1], fp32, kind="Internal").ap() for n in range(2)]

    ctx = ExitStack()
    with ctx:
        def sb(name, shape, dt=fp32):
            return ctx.enter_context(nc.sbuf_tensor(name, shape, dt))

        def sem(name):
            return ctx.enter_context(nc.semaphore(name))

        UV_PAIRS = ROWS // P // 2
        STORE = 5
        STORES = UV_PAIRS // STORE

        acc = sb("acc", [F + 1, ROWS])
        x1 = sb("x1", [P, ROWS])
        work_a = sb("work_a", [P, ROWS])
        work_b = sb("work_b", [P, ROWS])
        dst_i = sb("dst_i", [P, EPAD // P], i32)
        rel = sb("rel", [P, TILES])
        first_i = sb("first_i", [1, MACROS], i32)
        first_f = sb("first_f", [1, MACROS])
        first_all = sb("first_all", [P, MACROS])
        edge_sums = sb("edge_sums", [F, 2, MACROS])
        sq_sum = sb("sq_sum", [P, GROUP, F])
        src_in = [sb(f"src_in{s}", [P, SLOTS * GROUP], i32) for s in range(2)]
        ea4 = [sb(f"ea4_{s}", [PARTS * PARTS * (D1 + 1), UNIT], bf16) for s in range(2)]
        dst_b = [sb(f"dst_b{s}", [P, max(UNIT, TILES)], i32) for s in range(2)]
        gath = [sb(f"gath{s}", [P, GROUP, F]) for s in range(SLOTS)]
        msg = [sb(f"msg{s}", [P, GROUP, F + 1]) for s in range(SLOTS)]
        msg_sq = [sb(f"msg_sq{s}", [P, GROUP, F]) for s in range(SLOTS)]
        onehot = [sb(f"onehot{s}", [P, GROUP, WINDOW]) for s in range(SLOTS)]
        ea32 = [sb(f"ea32_{s}", [D0 + 1, MACRO]) for s in range(SLOTS)]
        edge_h = [sb(f"edge_h{s}", [F, MACRO]) for s in range(2)]
        onehot_t = [sb(f"onehot_t{s}", [PARTS * WINDOW, MACRO], bf16) for s in range(SLOTS)]
        v_win = [sb(f"v_win{s}", [PARTS * WINDOW, F], bf16) for s in range(SLOTS)]
        we_s = sb("we_s", [D0 + 1, F])
        w1_s = sb("w1_s", [F, F])
        w2_s = sb("w2_s", [F, F])
        wn_s = sb("wn_s", [F, F])
        KE = PARTS * PARTS * (D1 + 1)
        wedge_f = sb("wedge_f", [KE, F])
        wedge_p = [sb(f"wedge_p{i}", [KE, F], bf16) for i in range(PARTS)]
        wedge_s = sb("wedge_s", [KE, F], bf16)
        third = sb("third", [KE, PARTS])
        wmsg_s = sb("wmsg_s", [F, 3, F])
        bmsg_s = sb("bmsg_s", [1, F])
        vec = sb("vec", [F, 11])
        B1, B2, GAM0, BET0, BNODE, GNODE, BETNODE, GEDGE, BETEDGE, GMSG, BETMSG = range(11)
        wc_s = sb("wc_s", [F, F])
        uv_s = sb("uv_s", [F + 1, 2, F])
        ident = sb("ident", [P, P])
        before = sb("before", [P, P])
        mean_w = sb("mean_w", [F, F])
        ones = sb("ones", [P, P])
        last_one = sb("last_one", [1, F + 1])
        spread = sb("spread", [F, F + 1])
        cols = sb("cols", [P, WINDOW])
        part = sb("part", [P, 1])
        part_w = sb("part_w", [P, 1])
        dump = sb("dump", [P, 1])
        eps_s = sb("eps_s", [P, 1])
        in_window = sb("in_window", [P, 1])
        flag_f = sb("flag_f", [1, 1])
        flag_i = sb("flag_i", [1, 1], i32)
        chunk_sums = sb("chunk_sums", [F, NC])
        st = sb("st", [F, 32])
        scale_n = sb("scale_n", [F, F + 1])
        scale_m = sb("scale_m", [F, F + 1])
        mat_n = sb("mat_n", [F + 1, F])
        mat_m = sb("mat_m", [F + 1, F])
        bn6 = sb("bn6", [P, 2, GROUP, 6])
        mv = sb("mv", [P, 2, GROUP, 2])
        sd = sb("sd", [P, 2, GROUP])
        res = sb("res", [P, 2, GROUP, F])
        SC = 2 * STORE * F
        v_rest = sb("v_rest", [P, 2, SC])
        v_bf = sb("v_bf", [P, 2, PARTS, SC], bf16)
        g_src = sb("g_src", [P, 1], i32)
        g_dst = sb("g_dst", [P, 1], i32)
        g_row = sb("g_row", [P, P], i32)
        g_dst_f = sb("g_dst_f", [P, 1])
        g_same = sb("g_same", [P, P])
        g_tmp = sb("g_tmp", [P, P])
        g_dup = sb("g_dup", [P, 1])
        g_isfirst = sb("g_isfirst", [P, 1])
        g_diff = sb("g_diff", [P, 1])
        g_to_f = sb("g_to_f", [P, 1])
        g_to = sb("g_to", [P, 1], i32)
        g_valid = sb("g_valid", [P, 1])
        g_cur = sb("g_cur", [P, F + 1])
        g_v = sb("g_v", [P, F])
        g_new = sb("g_new", [P, F + 1])

        bank = [ctx.enter_context(nc.psum_tensor(f"bank{i}", [P, 512], fp32)) for i in range(8)]
        pre_ps = [bank[s][:, 0:GROUP * F].rearrange("p (g f) -> p g f", g=GROUP) for s in range(SLOTS)]
        seg_ps = [bank[3 + s][:, 0:WINDOW] for s in range(SLOTS)]
        eh_ps = [bank[6 + s] for s in range(2)]

        loaded_idx = sem("loaded_idx")
        loaded_w = sem("loaded_w")
        loaded_wedge = sem("loaded_wedge")
        loaded_x = sem("loaded_x")
        x1_padded = sem("x1_padded")
        consts_ready = sem("consts_ready")
        pool_const = sem("pool_const")
        dve_step = sem("dve_step")
        first_ready = sem("first_ready")
        first_spread = sem("first_spread")
        window_counted = sem("window_counted")
        window_total = sem("window_total")
        flag_ready = sem("flag_ready")
        attr_in = [sem(f"attr_in{k}") for k in range(2)]
        part_ready = [sem(f"part_ready{k}") for k in range(2)]
        rest_ready = [sem(f"rest_ready{k}") for k in range(2)]
        parts_stored = sem("parts_stored")
        wedge_part = sem("wedge_part")
        wedge_ready = sem("wedge_ready")
        v_part = sem("v_part")
        v_left = sem("v_left")
        vp_stored = [sem(f"vp_stored{k}") for k in range(2)]

        class Layer:

            def __init__(self, n):
                s = lambda name: sem(f"{name}_{n}")
                self.src_in = [s(f"src_in{h}") for h in range(2)]
                self.gathered = [s(f"gathered{h}") for h in range(SLOTS)]
                self.ea4_in = [s(f"ea4_in{h}") for h in range(2)]
                self.onehot_ready = s("onehot_ready")
                self.edge_mm = s("edge_mm")
                self.edge_relu = s("edge_relu")
                self.pre_mm = s("pre_mm")
                self.pre_ready = s("pre_ready")
                self.msg_ready = s("msg_ready")
                self.seg_mm = s("seg_mm")
                self.acc_added = s("acc_added")
                self.swept = s("swept")
                if n == 0:
                    self.ea32_in = [s(f"ea32_in{h}") for h in range(SLOTS)]
                    self.edge_sq = s("edge_sq")
                else:
                    self.dst_in = [s(f"dst_in{h}") for h in range(2)]
                    self.v_in = [s(f"v_in{h}") for h in range(SLOTS)]
                    self.onehot_t_ready = s("onehot_t_ready")
                    self.msg_sq_ready = s("msg_sq_ready")
                    self.sq_added = s("sq_added")
                self.g_in = s("g_in")
                self.g_got = s("g_got")
                self.g_selected = s("g_selected")
                self.g_sum = s("g_sum")
                self.g_new = s("g_new")
                self.g_cleared = s("g_cleared")
                self.g_written = s("g_written")
                self.g_zero = s("g_zero")
                self.g_row_in = s("g_row_in")
                self.g_turned = s("g_turned")
                self.g_stored = s("g_stored")
                if n == 1:
                    self.g_got_v = s("g_got_v")

        L = [Layer(0), Layer(1)]
        G_LOADS = (4, 3 + PARTS)
        may_load = sem("may_load")
        may_gather = sem("may_gather")
        h_ready = sem("h_ready")
        w1_mm = sem("w1_mm")
        r_ready = sem("r_ready")
        w2_mm = sem("w2_mm")
        h2_ready = sem("h2_ready")
        acc_cleared = sem("acc_cleared")
        mean0_ready = sem("mean0_ready")
        var0_ready = sem("var0_ready")
        sd0_ready = sem("sd0_ready")
        bn0_ready = sem("bn0_ready")
        y_ready = sem("y_ready")
        z_ready = sem("z_ready")
        mean_mm = sem("mean_mm")
        centred = sem("centred")
        csq_ready = sem("csq_ready")
        var_mm = sem("var_mm")
        csd_ready = sem("csd_ready")
        x1_ready = sem("x1_ready")
        evar_ready = sem("evar_ready")
        esd_ready = sem("esd_ready")
        eshift_ready = sem("eshift_ready")
        wc_ready = sem("wc_ready")
        uvw_mm = sem("uvw_mm")
        uvw_ready = sem("uvw_ready")
        uv_mm = sem("uv_mm")
        even_ready = sem("even_ready")
        odd_ready = sem("odd_ready")
        u_stored = sem("u_stored")
        v_stored = sem("v_stored")
        nf_mm = sem("nf_mm")
        nf_ready = sem("nf_ready")
        nmean_ready = sem("nmean_ready")
        nsq_ready = sem("nsq_ready")
        nf_row = sem("nf_row")
        sq_total = sem("sq_total")
        fvar_ready = sem("fvar_ready")
        fsd_ready = sem("fsd_ready")
        scales_ready = sem("scales_ready")
        mats_mm = sem("mats_mm")
        mats_ready = sem("mats_ready")
        fin_mm = sem("fin_mm")
        fin_var = sem("fin_var")
        fin_sd = sem("fin_sd")
        fin_ready = sem("fin_ready")
        out_stored = [sem(f"out_stored{s}") for s in range(2)]

        x1_bf = x1[:, :].bitcast(bf16)
        a_bf, b_bf = work_a[:, :].bitcast(bf16), work_b[:, :].bitcast(bf16)
        split_parts = [[a_bf[:, 2 * SPLIT:3 * SPLIT], x1_bf[:, 0:SPLIT], x1_bf[:, SPLIT:2 * SPLIT]],
                       [b_bf[:, 2 * SPLIT:3 * SPLIT], x1_bf[:, 2 * SPLIT:3 * SPLIT], a_bf[:, 0:SPLIT]]]

        FIN = [(i, min(GROUP, NODE_TILES - i)) for i in range(0, NODE_TILES, GROUP)]
        rows_of = lambda i: min(P, N - i * P)

        def rows_ps(k, which):
            return bank[k % 3][:, 0:4 * F].rearrange("p (t k f) -> p t k f", t=2, k=2)[:, :, which, :]

        def staged(work, k):
            return work[:, 2 * k * F:2 * (k + 1) * F].rearrange("p (t f) -> p t f", t=2)

        def sweep(eng, step):
            for h in range(UNROLL):
                step(h, 0, h)
            with eng.Fori(1, ROUNDS) as q:
                for h in range(UNROLL):
                    step(q * UNROLL + h, q, h)
            step(MACROS - 1, ROUNDS, 0)

        def past(m, k):
            return not (isinstance(m, int) and m < k)

        def is_last(m):
            return isinstance(m, int) and m == MACROS - 1

        def slot_uses(q, h):
            return q * 2 + (h // SLOTS + 1)

        def unit_of(q, h):
            return h // SLOTS % 2, q + (h // UNROLL + 1), h % SLOTS

        block = ctx.enter_context(nc.Block())

        @block.sync
        def _(sp):
            sp.dma_start(first_i[:, :], dst_first).then_inc(loaded_idx, 16)
            sp.dma_start(dst_i[:, :], dst_tiles).then_inc(loaded_idx, 16)
            for to, of in ((we_s, we_b), (w1_s, w1), (w2_s, w2), (wn_s, w_node),
                           (bmsg_s, b_msg), (vec, node_vectors)):
                sp.dma_start(to[:, :], of).then_inc(loaded_w, 16)
            sp.dma_start(wmsg_s[:, :, :], w_msg.rearrange("(k p) f -> p k f", p=F)).then_inc(loaded_w, 16)
            for i in range(PARTS * PARTS):
                sp.dma_start(wedge_f[i * (D1 + 1):(i + 1) * (D1 + 1), :], w_edge_b).then_inc(loaded_wedge, 16)
            attr = ea4_rows.rearrange("d e -> (d e)").rearrange("(p k c) -> p k c", p=P, k=2)
            attr_parts = ea4_parts.rearrange("(i d) e -> i (d e)", i=PARTS).rearrange("i (p k c) -> i p k c", p=P, k=2)
            for k, work in enumerate((work_a, work_b)):
                sp.dma_start(work[:, 0:SPLIT], attr[:, k, :]).then_inc(attr_in[k], 16)
            for k in range(2):
                for i in range(PARTS):
                    sp.wait_ge(part_ready[k], i + 1)
                    sp.dma_start(attr_parts[i, :, k, :], split_parts[k][i]).then_inc(parts_stored, 16)
            sp.wait_ge(parts_stored, 16 * 2 * PARTS)
            sp.dma_start(x1[0:F, 0:N], x_t).then_inc(loaded_x, 16)
            sp.wait_ge(x1_padded, 1)

            def fast(n):
                s = L[n]

                def load_unit(m, q, h):
                    u = h // SLOTS % 2
                    if past(m, UNROLL):
                        sp.wait_ge(s.pre_ready, m - SLOTS)
                    sp.dma_start(src_in[u][:, :], src_tiles[:, ds(m * GROUP, SLOTS * GROUP)]).then_inc(s.src_in[u], 16)
                    if past(m, UNROLL):
                        sp.wait_ge(s.edge_mm, m - SLOTS)
                    for i in range(PARTS):
                        rows = slice(i * PARTS * (D1 + 1), (i + 1) * PARTS * (D1 + 1))
                        sp.dma_start(ea4[u][rows, :], ea4_parts[:, ds(m * MACRO, UNIT)]).then_inc(s.ea4_in[u], 16)
                    if n == 1:
                        if past(m, UNROLL):
                            sp.wait_ge(s.onehot_t_ready, m - SLOTS)
                            sp.sem_inc(may_load, 1)
                        sp.dma_start(dst_b[u][0:PARTS * WINDOW, 0:UNIT],
                                     dst_row[:, ds(m * MACRO, UNIT)].to_broadcast([PARTS * WINDOW, UNIT])
                                     ).then_inc(s.dst_in[u], 16)

                def step(m, q, h):
                    if h % SLOTS == 0:
                        load_unit(m, q, h)
                    c = h % SLOTS
                    if past(m, SLOTS):
                        sp.wait_ge(s.pre_mm, m - (SLOTS - 1))
                        sp.sem_inc(may_load, 1)
                    if n == 0:
                        sp.dma_start(ea32[c][:, :], ea32_blocks[ds(m, 1), :, :].rearrange("a d e -> (a d) e")
                                     ).then_inc(s.ea32_in[c], 16)
                    else:
                        base = sp.value_load(first_i[0:1, ds(m, 1)], min_val=0, max_val=N - 1)
                        for i in range(PARTS):
                            sp.dma_start(v_win[c][i * WINDOW:(i + 1) * WINDOW, :], v_parts[i, ds(base, WINDOW), :]
                                         ).then_inc(s.v_in[c], 16)

                sweep(sp, step)

            def general(n):
                s = L[n]
                sp.wait_ge(s.g_zero, 1)
                sp.dma_start(sum_table[n].rearrange("(p t) f -> p (t f)", p=P),
                             work_b[:, 0:ROWS // P * (F + 1)]).then_inc(s.g_cleared, 16)
                sp.wait_ge(s.g_cleared, 16)
                if n == 0:
                    def load_ea4(m):
                        for i in range(PARTS):
                            rows = slice(i * PARTS * (D1 + 1), (i + 1) * PARTS * (D1 + 1))
                            sp.dma_start(ea4[0][rows, 0:MACRO], ea4_parts[:, ds(m * MACRO, MACRO)]).then_inc(s.ea4_in[0], 16)

                    load_ea4(0)
                    with sp.Fori(1, MACROS) as m:
                        sp.wait_ge(s.edge_mm, m)
                        load_ea4(m)
                    sp.wait_ge(s.edge_mm, MACROS)
                with sp.Fori(0, MACROS) as m:
                    for g in range(GROUP):
                        sp.dma_start(g_src[:, :], src_tiles[:, ds(m * GROUP + g, 1)], allow_slow_non_contiguous=True).then_inc(s.g_in, 16)
                        sp.dma_start(g_dst[:, :], dst_tiles[:, ds(m * GROUP + g, 1)], allow_slow_non_contiguous=True).then_inc(s.g_in, 16)
                        sp.dma_start(g_row[:, :], dst_row[:, ds(m * MACRO + g * P, P)].to_broadcast([P, P])
                                     ).then_inc(s.g_in, 16)
                        if n == 0:
                            sp.dma_start(ea32[0][:, 0:P], ea32_blocks[ds(m, 1), :, g * P:(g + 1) * P]
                                         .rearrange("a d e -> (a d) e")).then_inc(s.g_in, 16)
                        else:
                            for i in range(PARTS):
                                rows = slice(i * PARTS * (D1 + 1), (i + 1) * PARTS * (D1 + 1))
                                sp.dma_start(ea4[0][rows, 0:P], ea4_parts[:, ds(m * MACRO + g * P, P)]).then_inc(s.g_in, 16)
                        sp.wait_ge(s.g_written, m * (16 * GROUP) + 16 * (g + 1))
                        sp.sem_inc(may_load, 1)
                sp.wait_ge(s.g_written, 16 * TILES)
                for i in range(ROWS // P):
                    if i:
                        sp.wait_ge(s.g_turned, i)
                    sp.dma_start(g_cur[:, :], sum_table[n][i * P:(i + 1) * P, :]).then_inc(s.g_row_in, 16)

            sp.wait_ge(flag_ready, 1)
            ordered = sp.value_load(flag_i[0:1, 0:1], min_val=0, max_val=1)
            with sp.If(ordered == 1):
                fast(0)
            with sp.Else():
                general(0)
            sp.wait_ge(L[0].swept, 1)

            for k in range(STORES):
                t0, t1 = 2 * STORE * k, 2 * STORE * (k + 1)
                pairs = STORE * (k + 1)
                sp.wait_ge(even_ready, (pairs + 1) // 2)
                sp.wait_ge(odd_ready, pairs // 2)
                for work, table, stored in ((work_a, u_table, u_stored), (work_b, v_table, v_stored)):
                    sp.dma_start(table[t0 * P:t1 * P, :].rearrange("(t p) f -> p t f", p=P),
                                 work[:, t0 * F:t1 * F].rearrange("p (t f) -> p t f", f=F)).then_inc(stored, 16)
                for i in range(PARTS):
                    sp.wait_ge(v_part, PARTS * k + i + 1)
                    sp.dma_start(v_parts[i, t0 * P:t1 * P, :].rearrange("(t p) f -> p t f", p=P),
                                 v_bf[:, k % 2, i, :].rearrange("p (t f) -> p t f", f=F)).then_inc(vp_stored[k % 2], 16)
            for k in range(2):
                sp.wait_ge(vp_stored[k], 16 * PARTS * ((STORES + 1 - k) // 2))

            sp.wait_ge(flag_ready, 1)
            ordered = sp.value_load(flag_i[0:1, 0:1], min_val=0, max_val=1)
            with sp.If(ordered == 1):
                fast(1)
            with sp.Else():
                general(1)
            sp.wait_ge(L[1].swept, 1)

            for k, (t0, nt) in enumerate(FIN):
                sp.wait_ge(fin_ready, k + 1)
                for i in range(nt):
                    r = rows_of(t0 + i)
                    sp.dma_start(out[(t0 + i) * P:(t0 + i) * P + r, :], res[0:r, k % 2, i, :]
                                 ).then_inc(out_stored[k % 2], 16)
            for s2 in range(2):
                sp.wait_ge(out_stored[s2], 16 * sum(nt for k, (_, nt) in enumerate(FIN) if k % 2 == s2))

        @block.gpsimd
        def _(pool):
            nc.gpsimd.iota(cols[:, :], [[1, WINDOW]], base=0, channel_multiplier=0,
                           allow_small_or_imprecise_dtypes=True).then_inc(pool_const, 1)
            nc.gpsimd.iota(part[:, :], [[0, 1]], base=0, channel_multiplier=1,
                           allow_small_or_imprecise_dtypes=True).then_inc(pool_const, 1)
            nc.gpsimd.iota(dump[:, :], [[0, 1]], base=N + 1, channel_multiplier=1,
                           allow_small_or_imprecise_dtypes=True).then_inc(pool_const, 1)
            nc.gpsimd.memset(ones[:, :], 1.0).then_inc(pool_const, 1)
            pool.wait_ge(pool_const, 4)
            nc.gpsimd.affine_select(out=ident[:, :], in_=ones[:, :], compare_op=ALU.is_equal, fill=0.0, base=0,
                                    pattern=[[1, P]], channel_multiplier=-1).then_inc(pool_const, 1)
            nc.gpsimd.affine_select(out=before[:, :], in_=ones[:, :], compare_op=ALU.is_gt, fill=0.0, base=0,
                                    pattern=[[-1, P]], channel_multiplier=1).then_inc(pool_const, 1)
            nc.gpsimd.affine_select(out=last_one[:, :], in_=ones[0:1, 0:F + 1], compare_op=ALU.is_equal, fill=0.0,
                                    base=-F, pattern=[[1, F + 1]], channel_multiplier=0).then_inc(pool_const, 1)
            pool.wait_ge(pool_const, 7)

            def fast(n, table):
                s = L[n]

                def step(m, q, h):
                    u, filled, place = unit_of(q, h)
                    c = h % SLOTS
                    pool.wait_ge(s.src_in[u], filled * 16)
                    if past(m, SLOTS):
                        pool.wait_ge(s.msg_ready, m - (SLOTS - 1))
                    pool.sem_inc(may_gather, 1)
                    for g in range(GROUP):
                        i = place * GROUP + g
                        nc.gpsimd.indirect_dma_start(
                            out=gath[c][:, g, :], out_offset=None, in_=table,
                            in_offset=bass.IndirectOffsetOnAxis(ap=src_in[u][:, i:i + 1], axis=0),
                        ).then_inc(s.gathered[c], 16)

                sweep(pool, step)

            def general(n, table):
                s = L[n]
                with pool.Fori(0, TILES) as t:
                    pool.wait_ge(s.g_in, (t + 1) * (16 * G_LOADS[n]))
                    pool.sem_inc(may_gather, 1)
                    nc.gpsimd.indirect_dma_start(
                        out=gath[0][:, 0, :], out_offset=None, in_=table,
                        in_offset=bass.IndirectOffsetOnAxis(ap=g_src[:, 0:1], axis=0)).then_inc(s.g_got, 16)
                    nc.gpsimd.indirect_dma_start(
                        out=g_cur[:, :], out_offset=None, in_=sum_table[n],
                        in_offset=bass.IndirectOffsetOnAxis(ap=g_dst[:, 0:1], axis=0)).then_inc(s.g_got, 16)
                    if n == 1:
                        nc.gpsimd.indirect_dma_start(
                            out=g_v[:, :], out_offset=None, in_=v_table,
                            in_offset=bass.IndirectOffsetOnAxis(ap=g_dst[:, 0:1], axis=0)).then_inc(s.g_got_v, 16)
                    pool.wait_ge(s.g_new, t + 1)
                    pool.sem_inc(may_gather, 1)
                    nc.gpsimd.indirect_dma_start(
                        out=sum_table[n], out_offset=bass.IndirectOffsetOnAxis(ap=g_to[:, 0:1], axis=0),
                        in_=g_new[:, :], in_offset=None).then_inc(s.g_written, 16)

            pool.wait_ge(flag_ready, 1)
            ordered = pool.value_load(flag_i[0:1, 0:1], min_val=0, max_val=1)
            with pool.If(ordered == 1):
                fast(0, x)
            with pool.Else():
                general(0, x)
            pool.wait_ge(u_stored, 16 * (STORES))
            ordered = pool.value_load(flag_i[0:1, 0:1], min_val=0, max_val=1)
            with pool.If(ordered == 1):
                fast(1, u_table)
            with pool.Else():
                general(1, u_table)

        @block.scalar
        def _(act):
            def fast(n):
                s = L[n]

                def edge_features(m, e):
                    act.wait_ge(s.edge_mm, m + 1)
                    if n == 1:
                        if past(m, 2):
                            act.wait_ge(s.pre_mm, m - 1)
                        nc.scalar.activation(edge_h[e][:, :], eh_ps[e][0:F, :], ACT.Relu).then_inc(s.edge_relu, 1)
                    else:
                        nc.scalar.activation(edge_h[e][:, :], eh_ps[e][0:F, :], ACT.Relu,
                                             accum_out=edge_sums[:, 0, ds(m, 1)]).then_inc(s.edge_relu, 1)
                        act.wait_ge(s.edge_relu, m + 1)
                        nc.scalar.activation(edge_h[e][:, :], edge_h[e][:, :], ACT.Square,
                                             accum_out=edge_sums[:, 1, ds(m, 1)]).then_inc(s.edge_sq, 1)

                def step(m, q, h):
                    c = h % SLOTS
                    if not is_last(m):
                        edge_features(m + 1, (h + 1) % 2)
                    act.wait_ge(s.pre_ready, m + 1)
                    if past(m, SLOTS):
                        act.wait_ge(s.seg_mm, m - (SLOTS - 1))
                    nc.scalar.activation(msg[c][:, :, 0:F], gath[c][:, :, :], ACT.Relu).then_inc(s.msg_ready, 1)
                    if n == 1:
                        act.wait_ge(s.msg_ready, m + 1)
                        if past(m, SLOTS):
                            act.wait_ge(s.sq_added, m - (SLOTS - 2))
                        nc.scalar.activation(msg_sq[c][:, :, :], msg[c][:, :, 0:F], ACT.Square
                                             ).then_inc(s.msg_sq_ready, 1)

                edge_features(0, 0)
                sweep(act, step)

            def general(n):
                s = L[n]
                if n == 0:
                    with act.Fori(0, MACROS) as m:
                        act.wait_ge(s.edge_mm, m + 1)
                        nc.scalar.activation(edge_h[0][:, :], eh_ps[0][0:F, :], ACT.Relu,
                                             accum_out=edge_sums[:, 0, ds(m, 1)]).then_inc(s.edge_relu, 1)
                        act.wait_ge(s.edge_relu, m + 1)
                        nc.scalar.activation(edge_h[0][:, :], edge_h[0][:, :], ACT.Square,
                                             accum_out=edge_sums[:, 1, ds(m, 1)]).then_inc(s.edge_sq, 1)
                with act.Fori(0, TILES) as t:
                    if n == 1:
                        act.wait_ge(s.edge_mm, t + 1)
                        nc.scalar.activation(edge_h[0][:, 0:P], eh_ps[0][0:F, 0:P], ACT.Relu).then_inc(s.edge_relu, 1)
                    act.wait_ge(s.pre_ready, t + 1)
                    nc.scalar.activation(msg[0][:, 0, 0:F], gath[0][:, 0, :], ACT.Relu).then_inc(s.msg_ready, 1)
                    if n == 1:
                        act.wait_ge(s.msg_ready, t + 1)
                        nc.scalar.activation(msg_sq[0][:, 0, :], msg[0][:, 0, 0:F], ACT.Square).then_inc(s.msg_sq_ready, 1)

            for i in range(PARTS):
                for k, work in enumerate((work_a, work_b)):
                    if i == 0:
                        act.wait_ge(attr_in[k], 16)
                    else:
                        act.wait_ge(rest_ready[k], i)
                    if i == PARTS - 1 and k == 1:
                        act.wait_ge(part_ready[0], PARTS)
                    nc.scalar.activation(split_parts[k][i], work[:, 0:SPLIT], ACT.Copy).then_inc(part_ready[k], 1)

            act.wait_ge(flag_ready, 1)
            ordered = act.value_load(flag_i[0:1, 0:1], min_val=0, max_val=1)
            with act.If(ordered == 1):
                fast(0)
            with act.Else():
                general(0)
            act.wait_ge(L[0].swept, 1)

            act.wait_ge(loaded_w, 16 * 7)

            def mlp_out(c):
                o, w = CHUNKS[c]
                act.wait_ge(w2_mm, c + 1)
                nc.scalar.activation(work_a[0:F, o:o + w], bank[4 + c % 2][0:F, 0:w], ACT.Identity,
                                     bias=vec[:, B2:B2 + 1], accum_out=chunk_sums[:, c:c + 1]).then_inc(h2_ready, 1)

            for c, (o, w) in enumerate(CHUNKS):
                act.wait_ge(w1_mm, c + 1)
                nc.scalar.activation(work_b[0:F, o:o + w], bank[c % 2][0:F, 0:w], ACT.Relu,
                                     bias=vec[:, B1:B1 + 1]).then_inc(r_ready, 1)
                if c:
                    mlp_out(c - 1)
            mlp_out(NC - 1)
            act.wait_ge(mean0_ready, 1)
            act.wait_ge(h2_ready, NC)
            nc.scalar.activation(work_b[0:F, 0:N], work_a[0:F, 0:N], ACT.Square, bias=st[:, 1:2],
                                 accum_out=st[:, 2:3]).then_inc(var0_ready, 1)
            act.wait_ge(var0_ready, 1)
            nc.scalar.activation(st[:, 3:4], st[:, 2:3], ACT.Sqrt, scale=1.0 / N, bias=eps_s[0:F, :]).then_inc(sd0_ready, 1)
            act.wait_ge(evar_ready, 1)
            nc.scalar.activation(st[:, 14:15], st[:, 13:14], ACT.Sqrt, bias=eps_s[0:F, :]).then_inc(esd_ready, 1)
            act.wait_ge(bn0_ready, 1)
            for c, (o, w) in enumerate(CHUNKS):
                nc.scalar.activation(work_b[0:F, o:o + w], work_a[0:F, o:o + w], ACT.Relu, scale=st[:, 5:6],
                                     bias=st[:, 6:7]).then_inc(y_ready, 1)

            def root(c):
                o, w = CHUNKS[c]
                act.wait_ge(var_mm, c + 1)
                nc.scalar.activation(work_b[0:F, o:o + w], bank[4 + c % 2][0:F, 0:w], ACT.Sqrt,
                                     bias=eps_s[0:F, :]).then_inc(csd_ready, 1)

            for c, (o, w) in enumerate(CHUNKS):
                act.wait_ge(centred, c + 1)
                nc.scalar.activation(work_b[0:F, o:o + w], x1[0:F, o:o + w], ACT.Square).then_inc(csq_ready, 1)
                if c:
                    root(c - 1)
            root(NC - 1)

            act.wait_ge(x1_ready, NC)
            for k in range(0, UV_PAIRS, 2):
                act.wait_ge(uv_mm, k + 1)
                nc.scalar.activation(staged(work_a, k), rows_ps(k, 0), ACT.Copy)
                nc.scalar.activation(staged(work_b, k), rows_ps(k, 1), ACT.Copy).then_inc(even_ready, 1)
            for k in range(STORES):
                act.wait_ge(even_ready, (STORE * (k + 1) + 1) // 2)
                act.wait_ge(odd_ready, STORE * (k + 1) // 2)
                if k >= 2:
                    act.wait_ge(vp_stored[k % 2], 16 * PARTS * (k // 2))
                for i in range(PARTS):
                    if i:
                        act.wait_ge(v_left, (PARTS - 1) * k + i)
                    of = v_rest[:, k % 2, :] if i else work_b[:, k * SC:(k + 1) * SC]
                    nc.scalar.activation(v_bf[:, k % 2, i, :], of, ACT.Copy).then_inc(v_part, 1)

            act.wait_ge(u_stored, 16 * (STORES))
            for c, (o, w) in enumerate(CHUNKS):
                act.wait_ge(nf_mm, c + 1)
                nc.scalar.activation(work_a[0:F, o:o + w], bank[4 + c % 2][0:F, 0:w], ACT.Relu,
                                     bias=vec[:, BNODE:BNODE + 1], accum_out=chunk_sums[:, c:c + 1]).then_inc(nf_ready, 1)
            act.wait_ge(v_stored, 16 * (STORES))
            act.wait_ge(nmean_ready, 1)
            nc.scalar.activation(work_b[0:F, 0:N], work_a[0:F, 0:N], ACT.Square, bias=st[:, 17:18],
                                 accum_out=st[:, 18:19]).then_inc(nsq_ready, 1)

            with act.If(ordered == 1):
                fast(1)
            with act.Else():
                general(1)
            act.wait_ge(L[1].swept, 1)

            act.wait_ge(fvar_ready, 1)
            nc.scalar.activation(st[:, 19:20], st[:, 18:19], ACT.Sqrt, scale=1.0 / N, bias=eps_s[0:F, :]).then_inc(fsd_ready, 1)
            nc.scalar.activation(st[:, 26:27], st[:, 25:26], ACT.Sqrt, bias=eps_s[0:F, :]).then_inc(fsd_ready, 1)
            for k, (t0, nt) in enumerate(FIN):
                act.wait_ge(fin_var, k + 1)
                nc.scalar.activation(sd[:, k % 2, 0:nt], mv[:, k % 2, 0:nt, 1], ACT.Sqrt,
                                     bias=eps_s[:, :]).then_inc(fin_sd, 1)

        @block.vector
        def _(dve):
            chain = [0]

            def link(ins):
                chain[0] += 1
                ins.then_inc(dve_step, 1)
                dve.wait_ge(dve_step, chain[0])

            link(nc.vector.memset(mean_w[:, :], 1.0 / F))
            link(nc.vector.memset(eps_s[:, :], EPS))
            link(nc.vector.memset(spread[:, :], 0.0))
            for s in range(SLOTS):
                link(nc.vector.memset(msg[s][:, :, F:F + 1], 1.0))
            nc.vector.memset(acc[:, :], 0.0).then_inc(L[0].acc_added, 1)
            nc.vector.memset(sq_sum[:, :, :], 0.0).then_inc(L[1].sq_added, 1)

            dve.wait_ge(loaded_idx, 32)
            dve.wait_ge(pool_const, 7)
            nc.vector.tensor_copy(first_f[:, :], first_i[:, :]).then_inc(first_ready, 1)
            link(nc.vector.tensor_copy(part_w[:, :], part[:, :]))
            for k in range(1, PARTS):
                link(nc.vector.tensor_scalar(in_window[:, :], part[:, :], float(k * WINDOW), None, ALU.is_ge))
                link(nc.vector.scalar_tensor_tensor(part_w[:, :], in_window[:, :], -float(WINDOW), part_w[:, :],
                                                    ALU.mult, ALU.add))
            dve.wait_ge(first_spread, 1)
            link(nc.vector.tensor_copy(first_all[:, :], bank[0][:, 0:MACROS]))
            link(nc.vector.tensor_tensor(rel[:, :].rearrange("p (m g) -> p m g", g=GROUP),
                                         dst_i[:, 0:TILES].rearrange("p (m g) -> p m g", g=GROUP),
                                         first_all[:, :].unsqueeze(2).to_broadcast([P, MACROS, GROUP]), ALU.subtract))
            above, inside = (dst_b[k][:, 0:TILES].bitcast(fp32) for k in range(2))
            link(nc.vector.tensor_scalar(above, rel[:, :], 0.0, None, ALU.is_ge))
            nc.vector.scalar_tensor_tensor(inside, rel[:, :], float(WINDOW), above, ALU.is_lt,
                                           ALU.mult, accum_out=in_window[:, :]).then_inc(window_counted, 1)
            dve.wait_ge(window_total, 1)
            link(nc.vector.tensor_scalar(flag_f[:, :], bank[1][0:1, 0:1], float(TILES * P), None, ALU.is_equal))
            dve.wait_ge(window_counted, 1)
            nc.vector.tensor_copy(flag_i[:, :], flag_f[:, :]).then_inc(flag_ready, 1)
            for i in range(PARTS - 1):
                for k, work in enumerate((work_a, work_b)):
                    dve.wait_ge(part_ready[k], i + 1)
                    nc.vector.tensor_tensor(work[:, 0:SPLIT], work[:, 0:SPLIT], split_parts[k][i], ALU.subtract
                                            ).then_inc(rest_ready[k], 1)
            dve.wait_ge(loaded_wedge, 16 * PARTS * PARTS)
            for i in range(PARTS):
                link(nc.vector.tensor_copy(wedge_p[i][:, :], wedge_f[:, :]))
                if i < PARTS - 1:
                    link(nc.vector.tensor_tensor(wedge_f[:, :], wedge_f[:, :], wedge_p[i][:, :], ALU.subtract))
            rows = PARTS * (D1 + 1)
            link(nc.vector.tensor_scalar(third[:, 0:1], part[0:KE, :], float(rows), None, ALU.is_lt))
            link(nc.vector.tensor_scalar(third[:, 2:3], part[0:KE, :], float(2 * rows), None, ALU.is_ge))
            link(nc.vector.tensor_tensor(third[:, 1:2], third[:, 0:1], third[:, 2:3], ALU.add))
            link(nc.vector.tensor_scalar(third[:, 1:2], third[:, 1:2], 0.0, None, ALU.is_equal))
            link(nc.vector.tensor_scalar(wedge_s[:, :], wedge_p[0][:, :], third[:, 0:1], None, ALU.mult))
            link(nc.vector.scalar_tensor_tensor(wedge_s[:, :], wedge_p[1][:, :], third[:, 1:2], wedge_s[:, :],
                                                ALU.mult, ALU.add))
            nc.vector.scalar_tensor_tensor(wedge_s[:, :], wedge_p[2][:, :], third[:, 2:3], wedge_s[:, :],
                                           ALU.mult, ALU.add).then_inc(wedge_ready, 1)
            dve.wait_ge(parts_stored, 16 * 2 * PARTS)
            link(nc.vector.memset(x1[0:F, N:ROWS], 0.0))
            nc.vector.memset(x1[F:F + 1, :], 1.0).then_inc(x1_padded, 1)
            dve.wait_ge(flag_ready, 1)
            ordered = dve.value_load(flag_i[0:1, 0:1], min_val=0, max_val=1)

            def fast(n):
                s = L[n]
                height = F + 1 if n == 0 else F

                def add_sums(m, c):
                    dve.wait_ge(s.seg_mm, m + 1)
                    base = dve.value_load(first_i[0:1, ds(m, 1)], min_val=0, max_val=N - 1)
                    dve.wait_ge(s.acc_added, m + 1)
                    at = acc[0:height, ds(base, WINDOW)]
                    nc.vector.tensor_tensor(at, at, seg_ps[c][0:height, :], ALU.add).then_inc(s.acc_added, 1)
                    if n == 1:
                        dve.wait_ge(s.msg_sq_ready, m + 1)
                        dve.wait_ge(s.sq_added, m + 1)
                        if is_last(m):
                            nc.vector.tensor_tensor(sq_sum[0:TAIL, GROUP - 1, :], sq_sum[0:TAIL, GROUP - 1, :],
                                                    msg_sq[c][0:TAIL, GROUP - 1, :], ALU.add).then_inc(s.sq_added, 1)
                            whole = slice(0, GROUP - 1)
                        else:
                            whole = slice(0, GROUP)
                        nc.vector.tensor_tensor(sq_sum[:, whole, :], sq_sum[:, whole, :], msg_sq[c][:, whole, :],
                                                ALU.add).then_inc(s.sq_added, 1)

                def turned_onehot(m, q, h):
                    u, filled, place = unit_of(q, h)
                    dve.wait_ge(s.dst_in[u], filled * 16)
                    if past(m, SLOTS):
                        dve.wait_ge(s.pre_mm, m - (SLOTS - 1))
                    rows = PARTS * WINDOW
                    nc.vector.tensor_scalar(onehot_t[h % SLOTS][:, :], dst_b[u][0:rows, place * MACRO:(place + 1) * MACRO],
                                            first_all[0:rows, ds(m, 1)], part_w[0:rows, :], ALU.subtract, ALU.is_equal
                                            ).then_inc(s.onehot_t_ready, 1)

                def step(m, q, h):
                    c = h % SLOTS
                    if past(m, SLOTS):
                        dve.wait_ge(s.seg_mm, m - (SLOTS - 1))
                    nc.vector.tensor_tensor(
                        onehot[c][:, :, :], rel[:, ds(m * GROUP, GROUP)].unsqueeze(2).to_broadcast([P, GROUP, WINDOW]),
                        cols[:, :].unsqueeze(1).to_broadcast([P, GROUP, WINDOW]), ALU.is_equal).then_inc(s.onehot_ready, 1)
                    if n == 1 and not is_last(m):
                        turned_onehot(m + 1, q, h + 1)
                    dve.wait_ge(s.pre_mm, m + 1)
                    dve.wait_ge(s.gathered[c], slot_uses(q, h) * (16 * GROUP))
                    nc.vector.tensor_tensor(gath[c][:, :, :], gath[c][:, :, :], pre_ps[c], ALU.add).then_inc(s.pre_ready, 1)
                    if past(m, 1):
                        add_sums(m - 1, (h - 1) % SLOTS)

                if n == 1:
                    turned_onehot(0, 0, 0)
                sweep(dve, step)
                add_sums(MACROS - 1, 0)
                dve.wait_ge(s.edge_relu, MACROS)
                dve.wait_ge(s.msg_ready, MACROS)
                if n == 0:
                    dve.wait_ge(s.edge_sq, MACROS)
                else:
                    dve.wait_ge(s.msg_sq_ready, MACROS)
                    dve.wait_ge(s.onehot_t_ready, MACROS)
                    dve.wait_ge(s.sq_added, MACROS + 2)
                for c in range(SLOTS):
                    uses = 2 * ROUNDS + (c == 0)
                    if n == 0:
                        dve.wait_ge(s.ea32_in[c], 16 * uses)
                    else:
                        dve.wait_ge(s.v_in[c], 16 * PARTS * uses)
                for u in range(2):
                    fills = ROUNDS + (u == 0)
                    dve.wait_ge(s.src_in[u], 16 * fills)
                    dve.wait_ge(s.ea4_in[u], 16 * PARTS * fills)
                    if n == 1:
                        dve.wait_ge(s.dst_in[u], 16 * fills)
                dve.wait_ge(s.acc_added, MACROS + 1)

            def general(n):
                s = L[n]
                dve.wait_ge(s.acc_added, 1)
                nc.vector.memset(work_b[:, :], 0.0).then_inc(s.g_zero, 1)
                own = sem(f"g_dve_{n}")
                STEPS = 7
                with dve.Fori(0, TILES) as t:
                    def then(k, ins):
                        ins.then_inc(own, 1)
                        dve.wait_ge(own, t * STEPS + k)
                    dve.wait_ge(s.g_in, (t + 1) * (16 * G_LOADS[n]))
                    then(1, nc.vector.tensor_copy(g_dst_f[:, :], g_dst[:, :]))
                    then(2, nc.vector.tensor_scalar(g_same[:, :], g_row[:, :], g_dst_f[:, :], None, ALU.is_equal))
                    then(3, nc.vector.tensor_tensor(g_tmp[:, :], g_same[:, :], before[:, :], ALU.mult))
                    then(4, nc.vector.tensor_reduce(g_dup[:, :], g_tmp[:, :], AX.X, ALU.add))
                    then(5, nc.vector.tensor_scalar(g_isfirst[:, :], g_dup[:, :], 0.0, None, ALU.is_equal))
                    then(6, nc.vector.tensor_tensor(g_diff[:, :], g_dst_f[:, :], dump[:, :], ALU.subtract))
                    then(7, nc.vector.scalar_tensor_tensor(g_to_f[:, :], g_diff[:, :], g_isfirst[:, :], dump[:, :],
                                                           ALU.mult, ALU.add))
                    nc.vector.tensor_copy(g_to[:, :], g_to_f[:, :]).then_inc(s.g_selected, 1)
                    nc.vector.tensor_scalar(g_valid[:, :], g_dst_f[:, :], float(N), None, ALU.is_lt).then_inc(s.g_selected, 1)
                    dve.wait_ge(s.pre_mm, t + 1)
                    dve.wait_ge(s.g_got, (t + 1) * 32)
                    if n == 1:
                        dve.wait_ge(s.g_got_v, (t + 1) * 16)
                        nc.vector.tensor_tensor(g_v[:, :], g_v[:, :], pre_ps[0][:, 0, :], ALU.add).then_inc(s.onehot_ready, 1)
                        dve.wait_ge(s.onehot_ready, t + 1)
                        nc.vector.tensor_tensor(gath[0][:, 0, :], gath[0][:, 0, :], g_v[:, :], ALU.add).then_inc(s.pre_ready, 1)
                        dve.wait_ge(s.msg_sq_ready, t + 1)
                        dve.wait_ge(s.sq_added, t + 1)
                        nc.vector.scalar_tensor_tensor(sq_sum[:, 0, :], msg_sq[0][:, 0, :], g_valid[:, :],
                                                       sq_sum[:, 0, :], ALU.mult, ALU.add).then_inc(s.sq_added, 1)
                    else:
                        nc.vector.tensor_tensor(gath[0][:, 0, :], gath[0][:, 0, :], pre_ps[0][:, 0, :], ALU.add
                                                ).then_inc(s.pre_ready, 1)
                    dve.wait_ge(s.g_sum, t + 1)
                    nc.vector.tensor_tensor(g_new[:, :], g_cur[:, :], bank[3][:, 0:F + 1], ALU.add).then_inc(s.g_new, 1)
                height = F + 1 if n == 0 else F
                for i in range(ROWS // P):
                    dve.wait_ge(s.g_turned, i + 1)
                    nc.vector.tensor_copy(acc[0:height, i * P:(i + 1) * P], bank[i % 2][0:height, 0:P]).then_inc(s.g_stored, 1)
                dve.wait_ge(s.g_stored, ROWS // P)
                dve.wait_ge(s.msg_ready, TILES)
                dve.wait_ge(s.g_selected, 2 * TILES)
                dve.wait_ge(s.g_written, 16 * TILES)
                dve.wait_ge(s.g_row_in, 16 * (ROWS // P))
                if n == 0:
                    dve.wait_ge(s.ea4_in[0], 16 * PARTS * MACROS)
                    dve.wait_ge(s.edge_sq, MACROS)
                else:
                    dve.wait_ge(s.edge_relu, TILES)
                    dve.wait_ge(s.sq_added, TILES + 1)

            with dve.If(ordered == 1):
                fast(0)
            with dve.Else():
                general(0)
            nc.vector.memset(st[:, :], 0.0).then_inc(L[0].swept, 1)
            dve.wait_ge(L[0].swept, 1)

            dve.wait_ge(loaded_x, 16)
            for c, (o, w) in enumerate(CHUNKS):
                nc.vector.tensor_tensor(work_a[0:F, o:o + w], x1[0:F, o:o + w], acc[0:F, o:o + w], ALU.add
                                        ).then_inc(h_ready, 1)
            dve.wait_ge(h_ready, NC)
            nc.vector.memset(acc[0:F, :], 0.0).then_inc(L[1].acc_added, 1)
            link(nc.vector.tensor_reduce(st[:, 8:9], edge_sums[:, 0, :], AX.X, ALU.add))
            link(nc.vector.tensor_reduce(st[:, 9:10], edge_sums[:, 1, :], AX.X, ALU.add))
            link(nc.vector.tensor_scalar(st[:, 10:12], st[:, 8:10], 1.0 / E, None, ALU.mult))
            link(nc.vector.tensor_tensor(st[:, 12:13], st[:, 10:11], st[:, 10:11], ALU.mult))
            nc.vector.tensor_tensor(st[:, 13:14], st[:, 11:12], st[:, 12:13], ALU.subtract).then_inc(evar_ready, 1)
            dve.wait_ge(h2_ready, NC)
            link(nc.vector.tensor_reduce(st[:, 0:1], chunk_sums[:, :], AX.X, ALU.add))
            nc.vector.tensor_scalar(st[:, 1:2], st[:, 0:1], -1.0 / N, None, ALU.mult).then_inc(mean0_ready, 1)
            dve.wait_ge(mean0_ready, 1)
            dve.wait_ge(sd0_ready, 1)
            link(nc.vector.reciprocal(st[:, 4:5], st[:, 3:4]))
            link(nc.vector.tensor_tensor(st[:, 5:6], st[:, 4:5], vec[:, GAM0:GAM0 + 1], ALU.mult))
            nc.vector.scalar_tensor_tensor(st[:, 6:7], st[:, 1:2], st[:, 5:6], vec[:, BET0:BET0 + 1],
                                           ALU.mult, ALU.add).then_inc(bn0_ready, 1)
            dve.wait_ge(esd_ready, 1)
            link(nc.vector.reciprocal(st[:, 15:16], st[:, 14:15]))
            link(nc.vector.tensor_tensor(st[:, 16:17], st[:, 15:16], vec[:, GEDGE:GEDGE + 1], ALU.mult))
            nc.vector.tensor_scalar(wc_s[:, :], wmsg_s[:, 2, :], st[:, 16:17], None, ALU.mult).then_inc(wc_ready, 1)
            link(nc.vector.tensor_tensor(st[:, 27:28], st[:, 10:11], st[:, 16:17], ALU.mult))
            nc.vector.tensor_tensor(spread[:, F:F + 1], vec[:, BETEDGE:BETEDGE + 1], st[:, 27:28], ALU.subtract
                                    ).then_inc(eshift_ready, 1)
            dve.wait_ge(uvw_mm, 1)
            nc.vector.tensor_copy(uv_s[:, :, :], bank[3][0:F + 1, 0:2 * F].rearrange("p (k f) -> p k f", k=2)
                                  ).then_inc(uvw_ready, 1)

            dve.wait_ge(bn0_ready, 1)
            for c, (o, w) in enumerate(CHUNKS):
                dve.wait_ge(y_ready, c + 1)
                nc.vector.tensor_tensor(work_a[0:F, o:o + w], work_b[0:F, o:o + w], x1[0:F, o:o + w], ALU.add
                                        ).then_inc(z_ready, 1)

            def normalise(c):
                o, w = CHUNKS[c]
                dve.wait_ge(csd_ready, c + 1)
                link(nc.vector.reciprocal(work_b[0:F, o:o + w], work_b[0:F, o:o + w]))
                nc.vector.tensor_tensor(x1[0:F, o:o + w], x1[0:F, o:o + w], work_b[0:F, o:o + w], ALU.mult
                                        ).then_inc(x1_ready, 1)

            dve.wait_ge(z_ready, NC)
            for c, (o, w) in enumerate(CHUNKS):
                dve.wait_ge(mean_mm, c + 1)
                nc.vector.tensor_tensor(x1[0:F, o:o + w], work_a[0:F, o:o + w], bank[c % 2][0:F, 0:w], ALU.subtract
                                        ).then_inc(centred, 1)
                if c:
                    normalise(c - 1)
            normalise(NC - 1)
            dve.wait_ge(x1_ready, NC)

            for k in range(1, UV_PAIRS, 2):
                dve.wait_ge(uv_mm, k + 1)
                nc.vector.tensor_copy(staged(work_a, k), rows_ps(k, 0))
                nc.vector.tensor_copy(staged(work_b, k), rows_ps(k, 1)).then_inc(odd_ready, 1)
            for k in range(STORES):
                for i in range(PARTS - 1):
                    dve.wait_ge(v_part, PARTS * k + i + 1)
                    of = v_rest[:, k % 2, :] if i else work_b[:, k * SC:(k + 1) * SC]
                    nc.vector.tensor_tensor(v_rest[:, k % 2, :], of, v_bf[:, k % 2, i, :], ALU.subtract).then_inc(v_left, 1)
            dve.wait_ge(u_stored, 16 * (STORES))
            nc.vector.memset(work_a[0:F, N:ROWS], 0.0).then_inc(nf_row, 1)
            nc.vector.memset(work_a[F:F + 1, 0:ROWS], 1.0).then_inc(nf_row, 1)
            dve.wait_ge(nf_ready, NC)
            link(nc.vector.tensor_reduce(st[:, 20:21], chunk_sums[:, :], AX.X, ALU.add))
            nc.vector.tensor_scalar(st[:, 17:18], st[:, 20:21], -1.0 / N, None, ALU.mult).then_inc(nmean_ready, 1)
            dve.wait_ge(nsq_ready, 1)

            with dve.If(ordered == 1):
                fast(1)
            with dve.Else():
                general(1)
            nc.vector.memset(st[:, 30:31], 0.0).then_inc(L[1].swept, 1)
            dve.wait_ge(sq_total, 1)
            link(nc.vector.tensor_copy(st[:, 21:22], bank[7][0:F, 0:1]))

            link(nc.vector.tensor_reduce(st[:, 22:23], acc[0:F, 0:N], AX.X, ALU.add))
            link(nc.vector.tensor_scalar(st[:, 23:24], st[:, 22:23], -1.0 / E, None, ALU.mult))
            link(nc.vector.tensor_tensor(st[:, 24:25], st[:, 23:24], st[:, 23:24], ALU.mult))
            nc.vector.scalar_tensor_tensor(st[:, 25:26], st[:, 21:22], 1.0 / E, st[:, 24:25],
                                           ALU.mult, ALU.subtract).then_inc(fvar_ready, 1)
            dve.wait_ge(fvar_ready, 1)
            dve.wait_ge(fsd_ready, 2)
            link(nc.vector.reciprocal(st[:, 28:29], st[:, 19:20]))
            link(nc.vector.reciprocal(st[:, 29:30], st[:, 26:27]))
            link(nc.vector.tensor_tensor(st[:, 28:29], st[:, 28:29], vec[:, GNODE:GNODE + 1], ALU.mult))
            link(nc.vector.tensor_tensor(st[:, 29:30], st[:, 29:30], vec[:, GMSG:GMSG + 1], ALU.mult))
            link(nc.vector.tensor_scalar(scale_n[:, 0:F], ident[0:F, 0:F], st[:, 28:29], None, ALU.mult))
            link(nc.vector.tensor_scalar(scale_m[:, 0:F], ident[0:F, 0:F], st[:, 29:30], None, ALU.mult))
            link(nc.vector.scalar_tensor_tensor(scale_n[:, F:F + 1], st[:, 17:18], st[:, 28:29],
                                                vec[:, BETNODE:BETNODE + 1], ALU.mult, ALU.add))
            nc.vector.scalar_tensor_tensor(scale_m[:, F:F + 1], st[:, 23:24], st[:, 29:30], vec[:, BETMSG:BETMSG + 1],
                                           ALU.mult, ALU.add).then_inc(scales_ready, 1)
            dve.wait_ge(mats_mm, 1)
            link(nc.vector.tensor_copy(mat_n[:, :], bank[0][0:F + 1, 0:F]))
            nc.vector.tensor_copy(mat_m[:, :], bank[1][0:F + 1, 0:F]).then_inc(mats_ready, 1)

            for k, (t0, nt) in enumerate(FIN):
                b = k % 2
                ps = bank[k % 4][:, 0:GROUP * F].rearrange("p (g f) -> p g f", g=GROUP)
                dve.wait_ge(fin_mm, k + 1)
                for i in range(nt):
                    last = nc.vector.bn_stats(bn6[:, b, i, :], ps[:, i, :])
                link(last)
                for i in range(nt):
                    last = nc.vector.bn_aggr(mv[:, b, i, :], bn6[:, b, i, :])
                last.then_inc(fin_var, 1)
                dve.wait_ge(fin_var, k + 1)
                dve.wait_ge(fin_sd, k + 1)
                link(nc.vector.reciprocal(sd[:, b, 0:nt], sd[:, b, 0:nt]))
                if k >= 2:
                    dve.wait_ge(out_stored[b], 16 * GROUP * (k // 2))
                for i in range(nt):
                    last = nc.vector.tensor_scalar(res[:, b, i, :], ps[:, i, :], mv[:, b, i, 0:1], sd[:, b, i:i + 1],
                                                   ALU.subtract, ALU.mult)
                last.then_inc(fin_ready, 1)

        @block.tensor
        def _(pe):
            pe.wait_ge(pool_const, 7)
            pe.wait_ge(first_ready, 1)
            nc.tensor.matmul(bank[0][:, 0:MACROS], ones[0:1, :], first_f[:, :], start=True, stop=True).then_inc(first_spread, 1)
            pe.wait_ge(window_counted, 1)
            nc.tensor.matmul(bank[1][0:1, 0:1], in_window[:, :], ones[:, 0:1], start=True, stop=True).then_inc(window_total, 1)
            pe.wait_ge(loaded_w, 16 * 7)
            pe.wait_ge(wedge_ready, 1)

            def fast(n):
                s = L[n]
                height = F + 1 if n == 0 else F

                def segments(m, c):
                    pe.wait_ge(s.msg_ready, m + 1)
                    pe.wait_ge(s.onehot_ready, m + 1)
                    if past(m, SLOTS):
                        pe.wait_ge(s.acc_added, m - (SLOTS - 2))
                    for g in range(GROUP):
                        mm = nc.tensor.matmul(seg_ps[c][0:height, :], msg[c][:, g, 0:height], onehot[c][:, g, :],
                                              start=(g == 0), stop=(g == GROUP - 1))
                    mm.then_inc(s.seg_mm, 1)

                def edge_features(m, q, h):
                    u, filled, place = unit_of(q, h)
                    pe.wait_ge(s.ea4_in[u], filled * (16 * PARTS))
                    if past(m, 2):
                        pe.wait_ge(s.edge_relu, m - 1)
                    nc.tensor.matmul(eh_ps[h % 2][0:F, :], wedge_s[:, :], ea4[u][:, place * MACRO:(place + 1) * MACRO],
                                     start=True, stop=True).then_inc(s.edge_mm, 1)

                def step(m, q, h):
                    c = h % SLOTS
                    if past(m, SLOTS):
                        pe.wait_ge(s.pre_ready, m - (SLOTS - 1))
                    if n == 0:
                        pe.wait_ge(s.ea32_in[c], slot_uses(q, h) * 16)
                    else:
                        pe.wait_ge(s.edge_relu, m + 1)
                        pe.wait_ge(s.onehot_t_ready, m + 1)
                        pe.wait_ge(s.v_in[c], slot_uses(q, h) * (16 * PARTS))
                    for g in range(GROUP):
                        tile = slice(g * P, (g + 1) * P)
                        if n == 0:
                            mm = nc.tensor.matmul(pre_ps[c][:, g, :], ea32[c][:, tile], we_s[:, :], start=True, stop=True)
                        else:
                            nc.tensor.matmul(pre_ps[c][:, g, :], edge_h[h % 2][:, tile], wc_s[:, :], start=True, stop=False)
                            mm = nc.tensor.matmul(pre_ps[c][:, g, :], onehot_t[c][:, tile], v_win[c][:, :],
                                                  start=False, stop=True)
                    mm.then_inc(s.pre_mm, 1)
                    if not is_last(m):
                        edge_features(m + 1, q, h + 1)
                    if past(m, 1):
                        segments(m - 1, (h - 1) % SLOTS)

                edge_features(0, 0, 0)
                sweep(pe, step)
                segments(MACROS - 1, 0)

            def general(n):
                s = L[n]
                if n == 0:
                    def edge_features(m):
                        pe.wait_ge(s.ea4_in[0], (m + 1) * (16 * PARTS))
                        nc.tensor.matmul(eh_ps[0][0:F, :], wedge_s[:, :], ea4[0][:, 0:MACRO], start=True, stop=True
                                         ).then_inc(s.edge_mm, 1)

                    edge_features(0)
                    with pe.Fori(1, MACROS) as m:
                        pe.wait_ge(s.edge_sq, m)
                        edge_features(m)
                with pe.Fori(0, TILES) as t:
                    pe.wait_ge(s.g_in, (t + 1) * (16 * G_LOADS[n]))
                    if n == 0:
                        nc.tensor.matmul(pre_ps[0][:, 0, :], ea32[0][:, 0:P], we_s[:, :], start=True, stop=True
                                         ).then_inc(s.pre_mm, 1)
                    else:
                        nc.tensor.matmul(eh_ps[0][0:F, 0:P], wedge_s[:, :], ea4[0][:, 0:P], start=True, stop=True
                                         ).then_inc(s.edge_mm, 1)
                        pe.wait_ge(s.edge_relu, t + 1)
                        nc.tensor.matmul(pre_ps[0][:, 0, :], edge_h[0][:, 0:P], wc_s[:, :], start=True, stop=True
                                         ).then_inc(s.pre_mm, 1)
                    pe.wait_ge(s.msg_ready, t + 1)
                    pe.wait_ge(s.g_selected, (t + 1) * 2)
                    nc.tensor.matmul(bank[3][:, 0:F + 1], g_same[:, :], msg[0][:, 0, :], start=True, stop=True
                                     ).then_inc(s.g_sum, 1)
                for i in range(ROWS // P):
                    pe.wait_ge(s.g_row_in, 16 * (i + 1))
                    if i >= 2:
                        pe.wait_ge(s.g_stored, i - 1)
                    nc.tensor.matmul(bank[i % 2][0:F + 1, 0:P], g_cur[:, :], ident[:, :], start=True, stop=True
                                     ).then_inc(s.g_turned, 1)

            pe.wait_ge(flag_ready, 1)
            ordered = pe.value_load(flag_i[0:1, 0:1], min_val=0, max_val=1)
            with pe.If(ordered == 1):
                fast(0)
            with pe.Else():
                general(0)
            pe.wait_ge(L[0].swept, 1)

            def mlp_second(c):
                o, w = CHUNKS[c]
                pe.wait_ge(r_ready, c + 1)
                if c >= 2:
                    pe.wait_ge(h2_ready, c - 1)
                nc.tensor.matmul(bank[4 + c % 2][0:F, 0:w], w2_s[:, :], work_b[0:F, o:o + w], start=True, stop=True
                                 ).then_inc(w2_mm, 1)

            for c, (o, w) in enumerate(CHUNKS):
                pe.wait_ge(h_ready, c + 1)
                if c >= 2:
                    pe.wait_ge(r_ready, c - 1)
                nc.tensor.matmul(bank[c % 2][0:F, 0:w], w1_s[:, :], work_a[0:F, o:o + w], start=True, stop=True
                                 ).then_inc(w1_mm, 1)
                if c:
                    mlp_second(c - 1)
            mlp_second(NC - 1)
            pe.wait_ge(eshift_ready, 1)
            nc.tensor.matmul(bank[3][0:F + 1, 0:F], ident[0:F, 0:F + 1], wmsg_s[:, 0, :], start=True, stop=True)
            v_part = bank[3][0:F + 1, F:2 * F]
            nc.tensor.matmul(v_part, ident[0:F, 0:F + 1], wmsg_s[:, 1, :], start=True, stop=False)
            nc.tensor.matmul(v_part, spread[:, :], wmsg_s[:, 2, :], start=False, stop=False)
            nc.tensor.matmul(v_part, last_one[:, :], bmsg_s[:, :], start=False, stop=True).then_inc(uvw_mm, 1)

            def variances(c):
                o, w = CHUNKS[c]
                pe.wait_ge(csq_ready, c + 1)
                if c >= 2:
                    pe.wait_ge(csd_ready, c - 1)
                nc.tensor.matmul(bank[4 + c % 2][0:F, 0:w], mean_w[:, :], work_b[0:F, o:o + w], start=True, stop=True
                                 ).then_inc(var_mm, 1)

            for c, (o, w) in enumerate(CHUNKS):
                pe.wait_ge(z_ready, c + 1)
                if c >= 2:
                    pe.wait_ge(centred, c - 1)
                nc.tensor.matmul(bank[c % 2][0:F, 0:w], mean_w[:, :], work_a[0:F, o:o + w], start=True, stop=True
                                 ).then_inc(mean_mm, 1)
                if c:
                    variances(c - 1)
            variances(NC - 1)

            pe.wait_ge(uvw_ready, 1)
            pe.wait_ge(x1_ready, NC)
            for k in range(UV_PAIRS):
                if k >= 3:
                    ready = odd_ready if k % 2 == 0 else even_ready
                    pe.wait_ge(ready, (k - 3) // 2 + 1)
                for t in range(2):
                    mm = nc.tensor.matmul(bank[k % 3][:, t * 2 * F:(t + 1) * 2 * F], x1[0:F + 1, (2 * k + t) * P:(2 * k + t + 1) * P],
                                          uv_s[:, :, :].rearrange("p k f -> p (k f)"), start=True, stop=True)
                mm.then_inc(uv_mm, 1)
            for c, (o, w) in enumerate(CHUNKS):
                if c >= 2:
                    pe.wait_ge(nf_ready, c - 1)
                nc.tensor.matmul(bank[4 + c % 2][0:F, 0:w], wn_s[:, :], x1[0:F, o:o + w], start=True, stop=True
                                 ).then_inc(nf_mm, 1)
            pe.wait_ge(even_ready, (UV_PAIRS + 1) // 2)
            pe.wait_ge(odd_ready, UV_PAIRS // 2)
            pe.wait_ge(nf_ready, NC)
            pe.wait_ge(L[1].acc_added, 1)

            with pe.If(ordered == 1):
                fast(1)
            with pe.Else():
                general(1)
            pe.wait_ge(L[1].swept, 1)

            for g in range(GROUP):
                mm = nc.tensor.matmul(bank[7][0:F, 0:1], sq_sum[:, g, :], ones[:, 0:1], start=(g == 0), stop=(g == GROUP - 1))
            mm.then_inc(sq_total, 1)
            pe.wait_ge(scales_ready, 1)
            nc.tensor.matmul(bank[0][0:F + 1, 0:F], scale_n[:, :], ident[0:F, 0:F], start=True, stop=True)
            nc.tensor.matmul(bank[1][0:F + 1, 0:F], scale_m[:, :], ident[0:F, 0:F], start=True, stop=True).then_inc(mats_mm, 1)
            pe.wait_ge(mats_ready, 1)
            pe.wait_ge(nf_row, 2)
            for k, (t0, nt) in enumerate(FIN):
                if k >= 4:
                    pe.wait_ge(fin_ready, k - 3)
                for i in range(nt):
                    nodes = slice((t0 + i) * P, (t0 + i + 1) * P)
                    to = bank[k % 4][:, i * F:(i + 1) * F]
                    nc.tensor.matmul(to, acc[:, nodes], mat_m[:, :], start=True, stop=False)
                    nc.tensor.matmul(to, work_a[0:F + 1, nodes], mat_n[:, :], start=False, stop=False)
                    mm = nc.tensor.matmul(to, x1[0:F, nodes], ident[0:F, 0:F], start=False, stop=True)
                mm.then_inc(fin_mm, 1)


def kernel(**inputs):
    import numpy as np
    import concourse.bacc as bacc
    from concourse import mybir as _mybir
    from concourse.bass_utils import run_bass_kernel_spmd

    a = {k: np.asarray(v) for k, v in inputs.items()}

    def padded(v, fill):
        out = np.full((EPAD,) + v.shape[1:], fill, v.dtype)
        out[:E] = v
        return out

    def rows(v):
        out = np.zeros((v.shape[1] + 1, EPAD), v.dtype)
        out[:-1, :E] = v.T
        out[-1, :E] = 1
        return out

    src, dst = padded(a["src"], 0), padded(a["dst"], N)
    vectors = ["L0_gnn_b1", "L0_gnn_b2", "L0_gnn_gamma", "L0_gnn_beta", "L1_gnn_b_node", "L1_gnn_g_node",
               "L1_gnn_beta_node", "L1_gnn_g_edge", "L1_gnn_beta_edge", "L1_gnn_g_msg", "L1_gnn_beta_msg"]
    arrays = {
        "x": a["x"],
        "x_t": a["x"].T,
        "src_tiles": src.reshape(-1, P).T,
        "dst_tiles": dst.reshape(-1, P).T,
        "dst_first": dst[:MACROS * MACRO:MACRO].reshape(1, MACROS),
        "dst_row": dst.reshape(1, EPAD),
        "ea32_blocks": rows(a["edge_attr_32"]).reshape(D0 + 1, -1, MACRO).transpose(1, 0, 2),
        "ea4_rows": rows(a["edge_attr_4"]),
        "we_b": np.concatenate([a["L0_gnn_We"], a["L0_gnn_be"][None]]),
        "w1": a["L0_gnn_W1"],
        "w2": a["L0_gnn_W2"],
        "w_node": a["L1_gnn_W_node"],
        "w_edge_b": np.concatenate([a["L1_gnn_W_edge"], a["L1_gnn_b_edge"][None]]),
        "w_msg": a["L1_gnn_W_msg"],
        "b_msg": a["L1_gnn_b_msg"][None],
        "node_vectors": np.stack([a[n] for n in vectors], axis=1),
    }
    arrays = {k: np.ascontiguousarray(v) for k, v in arrays.items()}
    nc = bacc.Bacc("TRN2", target_bir_lowering=False, num_devices=1)
    args = [nc.dram_tensor(k, v.shape, _mybir.dt.from_np(v.dtype), kind="ExternalInput").ap() for k, v in arrays.items()]
    out = nc.dram_tensor("out", (N, F), _mybir.dt.float32, kind="ExternalOutput").ap()
    build(nc, *args, out)
    r = run_bass_kernel_spmd(nc, [arrays], core_ids=[0])
    return r.results[0]["out"]
```

```python
from contextlib import ExitStack

import concourse.bass as bass
from concourse import mybir

N = 6250
E = 206250
F = 96
D0 = 32
D1 = 4
P = 128
EPS = 1e-5
GROUP = 4
MACRO = GROUP * P
TILES = -(-E // P)
MACROS = -(-TILES // GROUP)
SLOTS = 3
UNROLL = 2 * SLOTS
ROUNDS = (MACROS - 1) // UNROLL
UNIT = SLOTS * MACRO
EPAD = -(-MACROS // SLOTS) * UNIT
PARTS = 3
SPLIT = (D1 + 1) * EPAD // P // 2
WINDOW = P - F - 1
NODE_TILES = -(-N // P)
ROWS = (NODE_TILES + 1) * P
CHUNK = 512
CHUNKS = [(c, min(CHUNK, N - c)) for c in range(0, N, CHUNK)]
NC = len(CHUNKS)
STRIP = N // (ROUNDS + 1)
STRIP_ROUND = 2
STRIPS = ROUNDS - STRIP_ROUND
REST = STRIPS * STRIP
COMBINE = 5
COMBINES = -(-NODE_TILES // COMBINE)
FEATURED = NODE_TILES - 1
COMBINED = FEATURED + COMBINES
TAIL = E - (TILES - 1) * P
assert MACROS == UNROLL * ROUNDS + 1 and TILES == MACROS * GROUP and ROWS >= N + 1 + P
assert COMBINED <= ROUNDS and ROWS == COMBINES * COMBINE * P
assert 2 * P * SPLIT == (D1 + 1) * EPAD


def build(nc, x, x_t, src_tiles, dst_tiles, dst_first, dst_row, ea32_blocks, ea4_rows,
          we_b, w1, w2, w_node, w_edge_b, w_msg, b_msg, node_vectors, out):
    fp32, i32, bf16 = mybir.dt.float32, mybir.dt.int32, mybir.dt.bfloat16
    ALU, ACT, AX = mybir.AluOpType, mybir.ActivationFunctionType, mybir.AxisListType
    ds = bass.ds

    u_table = nc.dram_tensor("u_table", [ROWS, F], fp32, kind="Internal").ap()
    v_table = nc.dram_tensor("v_table", [ROWS, F], fp32, kind="Internal").ap()
    ea4_parts = nc.dram_tensor("ea4_parts", [PARTS * (D1 + 1), EPAD], bf16, kind="Internal").ap()
    sum_table = [nc.dram_tensor(f"sum_table{n}", [ROWS, F + 1], fp32, kind="Internal").ap() for n in range(2)]

    ctx = ExitStack()
    with ctx:
        def sb(name, shape, dt=fp32):
            return ctx.enter_context(nc.sbuf_tensor(name, shape, dt))

        def sem(name):
            return ctx.enter_context(nc.semaphore(name))

        UV_PAIRS = ROWS // P // 2
        STORES = (5, 5, 5, 5, 3, 2)
        assert sum(STORES) == UV_PAIRS

        acc = sb("acc", [F + 1, ROWS])
        z = sb("z", [P, ROWS])
        NORMED = ROWS // P * F
        wide_room = sb("wide_room", [P, 2 * ROWS + NORMED])
        work_b = wide_room[:, 0:ROWS]
        work_a = wide_room[:, ROWS:2 * ROWS]
        x1 = wide_room[:, 2 * ROWS:]
        dst_i = sb("dst_i", [P, EPAD // P], i32)
        rel = sb("rel", [P, TILES])
        first_i = sb("first_i", [1, MACROS], i32)
        first_f = sb("first_f", [1, MACROS])
        first_all = sb("first_all", [P, MACROS])
        edge_sums = sb("edge_sums", [F, 2, MACROS])
        sq_sum = sb("sq_sum", [P, GROUP, F])
        src_in = [sb(f"src_in{s}", [P, SLOTS * GROUP], i32) for s in range(2)]
        ea4 = [sb(f"ea4_{s}", [PARTS * PARTS * (D1 + 1), UNIT], bf16) for s in range(2)]
        dst_b = [sb(f"dst_b{s}", [P, max(UNIT, TILES)], i32) for s in range(2)]
        gath = [sb(f"gath{s}", [P, GROUP, F]) for s in range(SLOTS)]
        msg = [sb(f"msg{s}", [P, GROUP, F + 1]) for s in range(SLOTS)]
        msg_sq = [sb(f"msg_sq{s}", [P, GROUP, F]) for s in range(SLOTS)]
        onehot = [sb(f"onehot{s}", [P, GROUP, WINDOW]) for s in range(SLOTS)]
        ea32 = [sb(f"ea32_{s}", [D0 + 1, MACRO]) for s in range(SLOTS)]
        edge_in = [sb(f"edge_in{s}", [P, MACRO]) for s in range(2)]
        edge_w = [sb(f"edge_w{s}", [P, F]) for s in range(SLOTS)]
        window = slice(F, F + WINDOW)
        we_s = sb("we_s", [D0 + 1, F])
        w1_s = sb("w1_s", [F, F])
        w2_s = sb("w2_s", [F, F])
        wn_s = sb("wn_s", [F, F])
        KE = PARTS * PARTS * (D1 + 1)
        wedge_f = sb("wedge_f", [KE, F])
        wedge_s32 = sb("wedge_s32", [D1 + 1, F])
        wedge_p = [sb(f"wedge_p{i}", [KE, F], bf16) for i in range(PARTS)]
        wedge_s = sb("wedge_s", [KE, F], bf16)
        third = sb("third", [KE, PARTS])
        wmsg_s = sb("wmsg_s", [F, 3, F])
        bmsg_s = sb("bmsg_s", [1, F])
        vec = sb("vec", [F, 11])
        B1, B2, GAM0, BET0, BNODE, GNODE, BETNODE, GEDGE, BETEDGE, GMSG, BETMSG = range(11)
        edge_shift = sb("edge_shift", [F, 1])
        msg_const = sb("msg_const", [1, F])
        centre = sb("centre", [F, F])
        zw_s = sb("zw_s", [F, 3 * F])
        cn_s = sb("cn_s", [F, F])
        wide = sb("wide", [F, 2, P])
        b_nodes = sb("b_nodes", [P, F])
        nf_scale = sb("nf_scale", [P, 2, F])
        z_tile = sb("z_tile", [F, P])
        nf_pre = sb("nf_pre", [P, F])
        nf_sq = sb("nf_sq", [P, F])
        nf_sums = sb("nf_sums", [P, 2, F])
        ident = sb("ident", [P, P])
        before = sb("before", [P, P])
        ones = sb("ones", [P, P])
        cols = sb("cols", [P, WINDOW])
        part_w = sb("part_w", [P, 1])
        part = sb("part", [P, 1])
        dump = sb("dump", [P, 1])
        eps_s = sb("eps_s", [P, 1])
        in_window = sb("in_window", [P, 1])
        floor_met = sb("floor_met", [1, 1])
        flag_f = sb("flag_f", [1, 1])
        flag_i = sb("flag_i", [1, 1], i32)
        h_strip = sb("h_strip", [F, STRIP])
        r_strip = sb("r_strip", [F, STRIP])
        floor = sb("floor", [1, ROUNDS + 1, UNROLL])
        h2_stats = sb("h2_stats", [F, (STRIPS + 1) * 6])
        h2_mv = sb("h2_mv", [F, 2])
        st = sb("st", [F, 32])
        scale_m = sb("scale_m", [F, F + 1])
        mat_m = sb("mat_m", [F + 1, F])
        bn6 = sb("bn6", [P, ROWS // P, 6])
        mv = sb("mv", [P, ROWS // P, 2])
        rstd = sb("rstd", [P, ROWS // P])
        shift = sb("shift", [P, ROWS // P])
        res = msg_sq[0:2]
        g_src = sb("g_src", [P, 1], i32)
        g_dst = sb("g_dst", [P, 1], i32)
        g_dst_f = sb("g_dst_f", [P, 1])
        g_dup = sb("g_dup", [P, 1])
        g_isfirst = sb("g_isfirst", [P, 1])
        g_diff = sb("g_diff", [P, 1])
        g_to_f = sb("g_to_f", [P, 1])
        g_to = sb("g_to", [P, 1], i32)
        g_valid = sb("g_valid", [P, 1])
        g_room = [gath[s][:, :, :].rearrange("p g f -> p (g f)") for s in (1, 2)]
        g_row = g_room[0][:, 0:P].bitcast(i32)
        g_same = g_room[0][:, P:2 * P]
        g_tmp = g_room[0][:, 2 * P:3 * P]
        g_cur = g_room[1][:, 0:F + 1]
        g_v = g_room[1][:, F + 1:2 * F + 1]
        g_new = g_room[1][:, 2 * F + 1:3 * F + 2]

        bank = [ctx.enter_context(nc.psum_tensor(f"bank{i}", [P, 512], fp32)) for i in range(8)]
        pre_bank = bank[0:SLOTS]
        pre_ps = [bank[s][:, 0:GROUP * F].rearrange("p (g f) -> p g f", g=GROUP) for s in range(SLOTS)]
        seg_ps = [bank[3 + s][:, 0:WINDOW] for s in range(SLOTS)]
        eh_ps = [bank[6 + s] for s in range(2)]

        loaded_idx = sem("loaded_idx")
        loaded_w = sem("loaded_w")
        loaded_wedge = sem("loaded_wedge")
        edge_row = sem("edge_row")
        ea4_first = [sem(f"ea4_first{u}") for u in range(2)]
        loaded_x = sem("loaded_x")
        pool_const = sem("pool_const")
        dve_step = sem("dve_step")
        first_ready = sem("first_ready")
        first_spread = sem("first_spread")
        floor_counted = sem("floor_counted")
        window_counted = sem("window_counted")
        window_total = sem("window_total")
        flag_ready = sem("flag_ready")
        attr_in = [sem(f"attr_in{k}") for k in range(2)]
        part_ready = [sem(f"part_ready{k}") for k in range(2)]
        rest_ready = [sem(f"rest_ready{k}") for k in range(2)]
        parts_stored = sem("parts_stored")
        wedge_ready = sem("wedge_ready")

        class Layer:

            def __init__(self, n):
                s = lambda name: sem(f"{name}_{n}")
                self.src_in = [s(f"src_in{h}") for h in range(2)]
                self.gathered = [s(f"gathered{h}") for h in range(SLOTS)]
                self.ea4_in = [s(f"ea4_in{h}") for h in range(2)]
                self.onehot_ready = s("onehot_ready")
                self.edge_mm = s("edge_mm")
                self.edge_relu = s("edge_relu")
                self.pre_mm = s("pre_mm")
                self.pre_ready = s("pre_ready")
                self.msg_ready = s("msg_ready")
                self.seg_mm = s("seg_mm")
                self.acc_added = s("acc_added")
                self.swept = s("swept")
                if n == 0:
                    self.ea32_in = [s(f"ea32_in{h}") for h in range(SLOTS)]
                    self.edge_sq = s("edge_sq")
                else:
                    self.dst_in = [s(f"dst_in{h}") for h in range(2)]
                    self.v_in = [s(f"v_in{h}") for h in range(SLOTS)]
                    self.onehot_t_ready = s("onehot_t_ready")
                    self.msg_sq_ready = s("msg_sq_ready")
                    self.sq_added = s("sq_added")
                self.g_in = s("g_in")
                self.g_got = s("g_got")
                self.g_selected = s("g_selected")
                self.g_sum = s("g_sum")
                self.g_new = s("g_new")
                self.g_cleared = s("g_cleared")
                self.g_written = s("g_written")
                self.g_zero = s("g_zero")
                self.g_row_in = s("g_row_in")
                self.g_turned = s("g_turned")
                self.g_stored = s("g_stored")
                if n == 1:
                    self.g_got_v = s("g_got_v")

        L = [Layer(0), Layer(1)]
        G_LOADS = (4, 3 + PARTS)
        may_load = sem("may_load")
        may_gather = sem("may_gather")
        centre_ready = sem("centre_ready")
        centred_mm = sem("centred_mm")
        centred_ready = sem("centred_ready")
        h_ready = sem("h_ready")
        strip_mm = sem("strip_mm")
        may_stats = sem("may_stats")
        strip_counted = sem("strip_counted")
        w1_mm = sem("w1_mm")
        r_ready = sem("r_ready")
        w2_mm = sem("w2_mm")
        h2_ready = sem("h2_ready")
        var0_ready = sem("var0_ready")
        sd0_ready = sem("sd0_ready")
        bn0_ready = sem("bn0_ready")
        y_ready = sem("y_ready")
        z_ready = sem("z_ready")
        evar_ready = sem("evar_ready")
        esd_ready = sem("esd_ready")
        wide_ready = sem("wide_ready")
        const_mm = sem("const_mm")
        const_ready = sem("const_ready")
        const_placed = sem("const_placed")
        zw_mm = sem("zw_mm")
        zvar_ready = sem("zvar_ready")
        zsd_ready = sem("zsd_ready")
        zscale_ready = sem("zscale_ready")
        rows_ready = sem("rows_ready")
        u_stored = sem("u_stored")
        v_stored = sem("v_stored")
        z_tile_ready = sem("z_tile_ready")
        nf_mm = sem("nf_mm")
        nf_pre_ready = sem("nf_pre_ready")
        nf_relu = sem("nf_relu")
        may_square = sem("may_square")
        nf_squared = sem("nf_squared")
        nf_added = sem("nf_added")
        nf_total = sem("nf_total")
        nf_var = sem("nf_var")
        nf_sd = sem("nf_sd")
        nf_vectors = sem("nf_vectors")
        nf_spread = sem("nf_spread")
        nf_scaled = sem("nf_scaled")
        combined = sem("combined")
        sq_total = sem("sq_total")
        half_sum = sem("half_sum")
        fvar_ready = sem("fvar_ready")
        fsd_ready = sem("fsd_ready")
        scales_ready = sem("scales_ready")
        mats_mm = sem("mats_mm")
        mats_ready = sem("mats_ready")
        fin_mm = sem("fin_mm")
        fin_var = sem("fin_var")
        fin_sd = sem("fin_sd")
        fin_scale = sem("fin_scale")
        fin_ready = sem("fin_ready")
        out_stored = [sem(f"out_stored{s}") for s in range(2)]

        z_bf = z[:, :].bitcast(bf16)
        a_bf, b_bf = work_a[:, :].bitcast(bf16), work_b[:, :].bitcast(bf16)
        split_parts = [[a_bf[:, 2 * SPLIT:3 * SPLIT], z_bf[:, 0:SPLIT], z_bf[:, SPLIT:2 * SPLIT]],
                       [b_bf[:, 2 * SPLIT:3 * SPLIT], z_bf[:, 2 * SPLIT:3 * SPLIT], a_bf[:, 0:SPLIT]]]

        attr_parts = ea4_parts.rearrange("(i d) e -> i (d e)", i=PARTS).rearrange("i (p k c) -> i p k c", p=P, k=2)
        ea4_32 = [dst_b[u][0:D1 + 1, 0:UNIT].bitcast(fp32) for u in range(2)]

        FIN = [(i, min(GROUP, NODE_TILES - i)) for i in range(0, NODE_TILES, GROUP)]
        rows_of = lambda i: min(P, N - i * P)

        def sweep(eng, step, spans, after_peeled=None):
            for h in range(UNROLL):
                step(h, 0, h, spans[0][2])
                if after_peeled is not None:
                    after_peeled(h)
            for first, end, node_work, before_it in spans:
                if before_it is not None:
                    before_it()
                with eng.Fori(first, end) as q:
                    for h in range(UNROLL):
                        step(q * UNROLL + h, q, h, node_work)
            step(MACROS - 1, ROUNDS, 0, None)

        def spans_of(n, before=(None, None)):
            if n == 0:
                return [(1, STRIP_ROUND, None, before[0]), (STRIP_ROUND, ROUNDS, "mlp", before[1])]
            return [(1, FEATURED, "features", None), (FEATURED, COMBINED, "combine", before[1]),
                    (COMBINED, ROUNDS, None, None)]

        ZW_BANKS = 8
        ACT_AHEAD = 4
        AHEAD = 3
        LAG = 2
        NODE_STEP = 2

        def past(m, k):
            return not (isinstance(m, int) and m < k)

        def is_last(m):
            return isinstance(m, int) and m == MACROS - 1

        def slot_uses(q, h):
            return q * 2 + (h // SLOTS + 1)

        def unit_of(q, h):
            return h // SLOTS % 2, q + (h // UNROLL + 1), h % SLOTS

        block = ctx.enter_context(nc.Block())

        @block.sync
        def _(sp):
            def load_sources(n, m, u):
                sp.dma_start(src_in[u][:, :], src_tiles[:, ds(m * GROUP, SLOTS * GROUP)]).then_inc(L[n].src_in[u], 16)

            def load_x():
                sp.dma_start(z[0:F, 0:N], x_t).then_inc(loaded_x, 16)

            def load_ea32(m, c):
                sp.dma_start(ea32[c][:, :], ea32_blocks[ds(m, 1), :, :].rearrange("a d e -> (a d) e")
                             ).then_inc(L[0].ea32_in[c], 16)

            sp.dma_start(first_i[:, :], dst_first).then_inc(loaded_idx, 16)
            sp.dma_start(dst_i[:, :], dst_tiles).then_inc(loaded_idx, 16)
            attr = ea4_rows.rearrange("d e -> (d e)").rearrange("(p k c) -> p k c", p=P, k=2)
            for k, work in enumerate((work_a, work_b)):
                sp.dma_start(work[:, 0:SPLIT], attr[:, k, :]).then_inc(attr_in[k], 16)
            for u in range(2):
                load_sources(0, u * SLOTS, u)
            sp.dma_start(wedge_s32[:, :], w_edge_b).then_inc(loaded_w, 16)
            for i in range(PARTS * PARTS):
                sp.dma_start(wedge_f[i * (D1 + 1):(i + 1) * (D1 + 1), :], w_edge_b).then_inc(loaded_wedge, 16)
            for to, of in ((we_s, we_b), (w1_s, w1), (w2_s, w2), (wn_s, w_node),
                           (bmsg_s, b_msg), (vec, node_vectors)):
                sp.dma_start(to[:, :], of).then_inc(loaded_w, 16)
            sp.dma_start(wmsg_s[:, :, :], w_msg.rearrange("(k p) f -> p k f", p=F)).then_inc(loaded_w, 16)
            for c in range(SLOTS):
                load_ea32(c, c)
            sp.wait_ge(window_counted, 1)
            for u in range(2):
                sp.dma_start(ea4_32[u], ea4_rows[:, u * UNIT:(u + 1) * UNIT]).then_inc(ea4_first[u], 16)

            def fast(n):
                s = L[n]

                def load_unit(m, q, h):
                    u = h // SLOTS % 2
                    if past(m, UNROLL):
                        sp.wait_ge(s.pre_ready, m - SLOTS)
                    if past(m, UNROLL):
                        load_sources(n, m, u)
                    if past(m, UNROLL):
                        sp.wait_ge(s.edge_mm, m - SLOTS)
                    if n == 1 or past(m, UNROLL):
                        for i in range(PARTS):
                            rows = slice(i * PARTS * (D1 + 1), (i + 1) * PARTS * (D1 + 1))
                            sp.dma_start(ea4[u][rows, :], ea4_parts[:, ds(m * MACRO, UNIT)]).then_inc(s.ea4_in[u], 16)
                    if n == 1:
                        if past(m, UNROLL):
                            sp.wait_ge(s.onehot_t_ready, m - SLOTS)
                            sp.sem_inc(may_load, 1)
                        sp.dma_start(dst_b[u][window, 0:UNIT], dst_row[:, ds(m * MACRO, UNIT)].to_broadcast([WINDOW, UNIT])
                                     ).then_inc(s.dst_in[u], 16)

                def step(m, q, h, node_work):
                    if h % SLOTS == 0:
                        load_unit(m, q, h)
                    c = h % SLOTS
                    if past(m, SLOTS):
                        sp.wait_ge(s.pre_mm, m - (SLOTS - 1))
                        sp.sem_inc(may_load, 1)
                    if n == 0:
                        if past(m, SLOTS):
                            load_ea32(m, c)
                    else:
                        base = sp.value_load(first_i[0:1, ds(m, 1)], min_val=0, max_val=N - 1)
                        if not past(m, 1):
                            sp.wait_ge(v_stored, 16 * (len(STORES) - 1))
                        sp.dma_start(edge_w[c][window, :], v_table[ds(base, WINDOW), :]).then_inc(s.v_in[c], 16)

                def parts_there():
                    sp.wait_ge(parts_stored, 16 * 2 * PARTS)

                sweep(sp, step, spans_of(n, (parts_there, load_x)) if n == 0 else spans_of(n))

            def general(n):
                s = L[n]
                for u in range(2):
                    sp.wait_ge(s.src_in[u], 16)
                if n == 0:
                    for c in range(SLOTS):
                        sp.wait_ge(s.ea32_in[c], 16)
                    for u in range(2):
                        sp.wait_ge(ea4_first[u], 16)
                    sp.wait_ge(parts_stored, 16 * 2 * PARTS)
                    load_x()
                sp.wait_ge(s.g_zero, 1)
                sp.dma_start(sum_table[n].rearrange("(p t) f -> p (t f)", p=P),
                             work_b[:, 0:ROWS // P * (F + 1)]).then_inc(s.g_cleared, 16)
                sp.wait_ge(s.g_cleared, 16)
                if n == 0:
                    def load_ea4(m):
                        for i in range(PARTS):
                            rows = slice(i * PARTS * (D1 + 1), (i + 1) * PARTS * (D1 + 1))
                            sp.dma_start(ea4[0][rows, 0:MACRO], ea4_parts[:, ds(m * MACRO, MACRO)]).then_inc(s.ea4_in[0], 16)

                    load_ea4(0)
                    with sp.Fori(1, MACROS) as m:
                        sp.wait_ge(s.edge_mm, m)
                        load_ea4(m)
                    sp.wait_ge(s.edge_mm, MACROS)
                with sp.Fori(0, MACROS) as m:
                    for g in range(GROUP):
                        sp.dma_start(g_src[:, :], src_tiles[:, ds(m * GROUP + g, 1)], allow_slow_non_contiguous=True).then_inc(s.g_in, 16)
                        sp.dma_start(g_dst[:, :], dst_tiles[:, ds(m * GROUP + g, 1)], allow_slow_non_contiguous=True).then_inc(s.g_in, 16)
                        sp.dma_start(g_row[:, :], dst_row[:, ds(m * MACRO + g * P, P)].to_broadcast([P, P])
                                     ).then_inc(s.g_in, 16)
                        if n == 0:
                            sp.dma_start(ea32[0][:, 0:P], ea32_blocks[ds(m, 1), :, g * P:(g + 1) * P]
                                         .rearrange("a d e -> (a d) e")).then_inc(s.g_in, 16)
                        else:
                            for i in range(PARTS):
                                rows = slice(i * PARTS * (D1 + 1), (i + 1) * PARTS * (D1 + 1))
                                sp.dma_start(ea4[0][rows, 0:P], ea4_parts[:, ds(m * MACRO + g * P, P)]).then_inc(s.g_in, 16)
                        sp.wait_ge(s.g_written, m * (16 * GROUP) + 16 * (g + 1))
                        sp.sem_inc(may_load, 1)
                sp.wait_ge(s.g_written, 16 * TILES)
                for i in range(ROWS // P):
                    if i:
                        sp.wait_ge(s.g_turned, i)
                    sp.dma_start(g_cur[:, :], sum_table[n][i * P:(i + 1) * P, :]).then_inc(s.g_row_in, 16)

            sp.wait_ge(flag_ready, 1)
            ordered = sp.value_load(flag_i[0:1, 0:1], min_val=0, max_val=1)
            with sp.If(ordered == 1):
                fast(0)
            with sp.Else():
                general(0)
            sp.wait_ge(L[0].swept, 1)

            for u in range(2):
                load_sources(1, u * SLOTS, u)
            def store_rows(work, table, stored, t0, t1):
                sp.dma_start(table[t0 * P:t1 * P, :].rearrange("(t p) f -> p t f", p=P),
                             work[:, t0 * F:t1 * F].rearrange("p (t f) -> p t f", f=F)).then_inc(stored, 16)

            for k, pairs in enumerate(STORES):
                t0, t1 = 2 * sum(STORES[:k]), 2 * sum(STORES[:k + 1])
                sp.wait_ge(rows_ready, t1 // 2)
                store_rows(work_b, u_table, u_stored, t0, t1)
                if k < len(STORES) - 2:
                    store_rows(work_a, v_table, v_stored, t0, t1)
            store_rows(work_a, v_table, v_stored, 2 * sum(STORES[:-2]), ROWS // P)

            sp.wait_ge(const_ready, 1)
            for c in range(SLOTS):
                sp.dma_start(edge_w[c][P - 1:P, :], msg_const[:, :]).then_inc(const_placed, 16)

            sp.wait_ge(flag_ready, 1)
            ordered = sp.value_load(flag_i[0:1, 0:1], min_val=0, max_val=1)
            with sp.If(ordered == 1):
                fast(1)
            with sp.Else():
                general(1)
            sp.wait_ge(L[1].swept, 1)

            for k, (t0, nt) in enumerate(FIN):
                r = rows_of(t0 + nt - 1)
                assert nt == 1 or r == P
                sp.wait_ge(fin_ready, k + 1)
                sp.dma_start(out[t0 * P:(t0 + nt - 1) * P + r, :].rearrange("(i p) f -> p i f", i=nt),
                             res[k % 2][0:r, 0:nt, :]).then_inc(out_stored[k % 2], 16)
            for s2 in range(2):
                sp.wait_ge(out_stored[s2], 16 * ((len(FIN) + 1 - s2) // 2))

        @block.gpsimd
        def _(pool):
            nc.gpsimd.iota(cols[:, :], [[1, WINDOW]], base=0, channel_multiplier=0,
                           allow_small_or_imprecise_dtypes=True).then_inc(pool_const, 1)
            nc.gpsimd.iota(part[:, :], [[0, 1]], base=0, channel_multiplier=1,
                           allow_small_or_imprecise_dtypes=True).then_inc(pool_const, 1)
            nc.gpsimd.iota(dump[:, :], [[0, 1]], base=N + 1, channel_multiplier=1,
                           allow_small_or_imprecise_dtypes=True).then_inc(pool_const, 1)
            nc.gpsimd.iota(floor[:, :, :], [[STRIP, ROUNDS + 1], [0, UNROLL]], base=(1 - STRIP_ROUND) * STRIP,
                           channel_multiplier=0, allow_small_or_imprecise_dtypes=True).then_inc(pool_const, 1)
            nc.gpsimd.memset(ones[:, :], 1.0).then_inc(pool_const, 1)
            pool.wait_ge(pool_const, 5)
            nc.gpsimd.affine_select(out=ident[:, :], in_=ones[:, :], compare_op=ALU.is_equal, fill=0.0, base=0,
                                    pattern=[[1, P]], channel_multiplier=-1).then_inc(pool_const, 1)
            nc.gpsimd.affine_select(out=before[:, :], in_=ones[:, :], compare_op=ALU.is_gt, fill=0.0, base=0,
                                    pattern=[[-1, P]], channel_multiplier=1).then_inc(pool_const, 1)
            pool.wait_ge(pool_const, 7)
            for e in range(2):
                nc.gpsimd.memset(edge_in[e][F:P, :], 1.0).then_inc(edge_row, 1)
            nc.gpsimd.memset(z[0:F, N:ROWS], 0.0).then_inc(z_ready, 1)
            pool.wait_ge(edge_row, 2)
            pool.wait_ge(z_ready, 1)
            nc.gpsimd.memset(acc[:, :], 0.0).then_inc(L[0].acc_added, 2)

            def fast(n, table):
                s = L[n]

                def step(m, q, h, node_work):
                    u, filled, place = unit_of(q, h)
                    c = h % SLOTS
                    pool.wait_ge(s.src_in[u], filled * 16)
                    if past(m, SLOTS):
                        pool.wait_ge(s.msg_ready, m - (SLOTS - 1))
                    pool.sem_inc(may_gather, 1)
                    for g in range(GROUP):
                        i = place * GROUP + g
                        nc.gpsimd.indirect_dma_start(
                            out=gath[c][:, g, :], out_offset=None, in_=table,
                            in_offset=bass.IndirectOffsetOnAxis(ap=src_in[u][:, i:i + 1], axis=0),
                        ).then_inc(s.gathered[c], 16)

                sweep(pool, step, spans_of(n))

            def general(n, table):
                s = L[n]
                with pool.Fori(0, TILES) as t:
                    pool.wait_ge(s.g_in, (t + 1) * (16 * G_LOADS[n]))
                    pool.sem_inc(may_gather, 1)
                    nc.gpsimd.indirect_dma_start(
                        out=gath[0][:, 0, :], out_offset=None, in_=table,
                        in_offset=bass.IndirectOffsetOnAxis(ap=g_src[:, 0:1], axis=0)).then_inc(s.g_got, 16)
                    nc.gpsimd.indirect_dma_start(
                        out=g_cur[:, :], out_offset=None, in_=sum_table[n],
                        in_offset=bass.IndirectOffsetOnAxis(ap=g_dst[:, 0:1], axis=0)).then_inc(s.g_got, 16)
                    if n == 1:
                        nc.gpsimd.indirect_dma_start(
                            out=g_v[:, :], out_offset=None, in_=v_table,
                            in_offset=bass.IndirectOffsetOnAxis(ap=g_dst[:, 0:1], axis=0)).then_inc(s.g_got_v, 16)
                    pool.wait_ge(s.g_new, t + 1)
                    pool.sem_inc(may_gather, 1)
                    nc.gpsimd.indirect_dma_start(
                        out=sum_table[n], out_offset=bass.IndirectOffsetOnAxis(ap=g_to[:, 0:1], axis=0),
                        in_=g_new[:, :], in_offset=None).then_inc(s.g_written, 16)

            pool.wait_ge(flag_ready, 1)
            ordered = pool.value_load(flag_i[0:1, 0:1], min_val=0, max_val=1)
            with pool.If(ordered == 1):
                fast(0, x)
            with pool.Else():
                general(0, x)
            pool.wait_ge(w1_mm, 1)
            nc.gpsimd.memset(acc[0:F, :], 0.0).then_inc(L[1].acc_added, 2)
            pool.wait_ge(u_stored, 16 * len(STORES))
            ordered = pool.value_load(flag_i[0:1, 0:1], min_val=0, max_val=1)
            with pool.If(ordered == 1):
                fast(1, u_table)
            with pool.Else():
                general(1, u_table)

        @block.scalar
        def _(act):
            def attribute_part(k, i):
                if i == 0:
                    act.wait_ge(attr_in[k], 16)
                else:
                    act.wait_ge(rest_ready[k], i)
                if i == PARTS - 1 and k == 1:
                    act.wait_ge(part_ready[0], PARTS)
                work = (work_a, work_b)[k]
                nc.scalar.activation(split_parts[k][i], work[:, 0:SPLIT], ACT.Copy).then_inc(part_ready[k], 1)
                act.wait_ge(part_ready[k], i + 1)
                nc.scalar.dma_start(attr_parts[i, :, k, :], split_parts[k][i]).then_inc(parts_stored, 16)

            def later_parts(h):
                if h < 2 * (PARTS - 1):
                    attribute_part(h % 2, h // 2 + 1)

            def fast(n):
                s = L[n]

                def edge_features(m, e):
                    act.wait_ge(s.edge_mm, m + 1)
                    if n == 1:
                        if past(m, 2):
                            act.wait_ge(s.pre_mm, m - 1)
                        nc.scalar.activation(edge_in[e][0:F, :], eh_ps[e][0:F, :], ACT.Relu).then_inc(s.edge_relu, 1)
                    else:
                        nc.scalar.activation(edge_in[e][0:F, :], eh_ps[e][0:F, :], ACT.Relu,
                                             accum_out=edge_sums[:, 0, ds(m, 1)]).then_inc(s.edge_relu, 1)
                        act.wait_ge(s.edge_relu, m + 1)
                        nc.scalar.activation(edge_in[e][0:F, :], edge_in[e][0:F, :], ACT.Square,
                                             accum_out=edge_sums[:, 1, ds(m, 1)]).then_inc(s.edge_sq, 1)

                def step(m, q, h, node_work):
                    c = h % SLOTS
                    if not is_last(m):
                        edge_features(m + 1, (h + 1) % 2)
                    act.wait_ge(s.pre_ready, m + 1)
                    if past(m, SLOTS):
                        act.wait_ge(s.seg_mm, m - (SLOTS - 1))
                    nc.scalar.activation(msg[c][:, :, 0:F], gath[c][:, :, :], ACT.Relu).then_inc(s.msg_ready, 1)
                    if n == 1:
                        act.wait_ge(s.msg_ready, m + 1)
                        if past(m, SLOTS):
                            act.wait_ge(s.sq_added, m - (SLOTS - 2))
                        nc.scalar.activation(msg_sq[c][:, :, :], msg[c][:, :, 0:F], ACT.Square
                                             ).then_inc(s.msg_sq_ready, 1)
                    if node_work == "features":
                        if h == NODE_STEP - 1:
                            node_tile(q, q + 1)
                        if h == NODE_STEP:
                            node_features(q, q + 1)

                if n == 1:
                    act.wait_ge(v_stored, 16 * (len(STORES) - 1))
                    node_tile(NODE_TILES - 1, 0)
                    node_features(NODE_TILES - 1, 0)
                edge_features(0, 0)
                sweep(act, step, spans_of(n, (None, node_scale if n == 1 else None)),
                      later_parts if n == 0 else None)

            def node_tile(t, done):
                if not isinstance(done, int) or done:
                    act.wait_ge(nf_pre_ready, done)
                nc.scalar.activation(z_tile[:, :], z[0:F, ds(t * P, P)], ACT.Copy).then_inc(z_tile_ready, 1)

            def node_features(t, done):
                act.wait_ge(nf_pre_ready, done + 1)
                nc.scalar.activation(work_a[:, ds(t * F, F)], nf_pre[:, :], ACT.Relu).then_inc(nf_relu, 1)
                act.wait_ge(nf_relu, done + 1)
                act.wait_ge(nf_added, done * 2 + 2)
                act.sem_inc(may_square, 1)
                nc.scalar.activation(nf_sq[:, :], work_a[:, ds(t * F, F)], ACT.Square).then_inc(nf_squared, 1)

            def node_scale():
                act.wait_ge(nf_var, 1)
                nc.scalar.activation(st[:, 19:20], st[:, 18:19], ACT.Sqrt, bias=eps_s[0:F, :]).then_inc(nf_sd, 1)

            def general(n):
                s = L[n]
                if n == 1:
                    act.wait_ge(v_stored, 16 * (len(STORES) - 1))
                    node_tile(NODE_TILES - 1, 0)
                    node_features(NODE_TILES - 1, 0)
                    with act.Fori(0, FEATURED) as t:
                        node_tile(t, t + 1)
                        node_features(t, t + 1)
                    node_scale()
                if n == 0:
                    for h in range(UNROLL):
                        later_parts(h)
                    with act.Fori(0, MACROS) as m:
                        act.wait_ge(s.edge_mm, m + 1)
                        nc.scalar.activation(edge_in[0][0:F, :], eh_ps[0][0:F, :], ACT.Relu,
                                             accum_out=edge_sums[:, 0, ds(m, 1)]).then_inc(s.edge_relu, 1)
                        act.wait_ge(s.edge_relu, m + 1)
                        nc.scalar.activation(edge_in[0][0:F, :], edge_in[0][0:F, :], ACT.Square,
                                             accum_out=edge_sums[:, 1, ds(m, 1)]).then_inc(s.edge_sq, 1)
                with act.Fori(0, TILES) as t:
                    if n == 1:
                        act.wait_ge(s.edge_mm, t + 1)
                        nc.scalar.activation(edge_in[0][0:F, 0:P], eh_ps[0][0:F, 0:P], ACT.Relu).then_inc(s.edge_relu, 1)
                    act.wait_ge(s.pre_ready, t + 1)
                    nc.scalar.activation(msg[0][:, 0, 0:F], gath[0][:, 0, :], ACT.Relu).then_inc(s.msg_ready, 1)
                    if n == 1:
                        act.wait_ge(s.msg_ready, t + 1)
                        nc.scalar.activation(msg_sq[0][:, 0, :], msg[0][:, 0, 0:F], ACT.Square).then_inc(s.msg_sq_ready, 1)

            attribute_part(0, 0)
            attribute_part(1, 0)

            act.wait_ge(flag_ready, 1)
            ordered = act.value_load(flag_i[0:1, 0:1], min_val=0, max_val=1)
            with act.If(ordered == 1):
                fast(0)
            with act.Else():
                general(0)
            act.wait_ge(L[0].swept, 1)

            act.wait_ge(loaded_w, 16 * 8)
            act.wait_ge(evar_ready, 1)
            nc.scalar.activation(st[:, 14:15], st[:, 13:14], ACT.Sqrt, bias=eps_s[0:F, :]).then_inc(esd_ready, 1)

            act.wait_ge(w1_mm, 1)
            nc.scalar.activation(work_b[0:F, REST:N], bank[0][0:F, 0:N - REST], ACT.Relu, bias=vec[:, B1:B1 + 1]
                                 ).then_inc(r_ready, 1)
            act.wait_ge(w2_mm, 1)
            nc.scalar.activation(work_a[0:F, REST:N], bank[4][0:F, 0:N - REST], ACT.Identity, bias=vec[:, B2:B2 + 1]
                                 ).then_inc(h2_ready, 1)
            act.wait_ge(var0_ready, 1)
            nc.scalar.activation(st[:, 3:4], h2_mv[:, 1:2], ACT.Sqrt, bias=eps_s[0:F, :]).then_inc(sd0_ready, 1)
            act.wait_ge(h2_ready, STRIPS + 1)
            act.wait_ge(bn0_ready, 1)

            def batch_normed(c):
                o, w = CHUNKS[c]
                nc.scalar.activation(work_a[0:F, o:o + w], work_a[0:F, o:o + w], ACT.Relu, scale=st[:, 5:6],
                                     bias=st[:, 6:7]).then_inc(y_ready, 1)

            def normed(k):
                act.wait_ge(zscale_ready, k + 1)
                for t in (2 * k, 2 * k + 1):
                    rows = wide_room[:, t * F:(t + 1) * F]
                    to = bass.AP(tensor=rows.tensor, offset=rows.offset, ap=[rows.ap[0], [ROWS, 3], [1, F]])
                    last = nc.scalar.activation(to, bank[t % ZW_BANKS][:, 0:3 * F].rearrange("p (k f) -> p k f", k=3), ACT.Copy,
                                                scale=rstd[:, t:t + 1])
                last.then_inc(rows_ready, 1)

            for c in range(0, ACT_AHEAD, 2):
                batch_normed(c)
            for k in range(UV_PAIRS):
                if k % 4 == 0 and k // 2 + ACT_AHEAD < NC:
                    batch_normed(k // 2 + ACT_AHEAD)
                act.wait_ge(zvar_ready, k + 1)
                nc.scalar.activation(rstd[:, 2 * k:2 * k + 2], mv[:, 2 * k:2 * k + 2, 1], ACT.Sqrt,
                                     bias=eps_s[:, :]).then_inc(zsd_ready, 1)
                if k:
                    normed(k - 1)
            normed(UV_PAIRS - 1)

            with act.If(ordered == 1):
                fast(1)
            with act.Else():
                general(1)
            act.wait_ge(L[1].swept, 1)

            nc.scalar.activation(work_a[0:F, 0:N - N // 2], acc[0:F, N // 2:N], ACT.Copy,
                                 accum_out=st[:, 31:32]).then_inc(half_sum, 1)
            act.wait_ge(fvar_ready, 1)
            nc.scalar.activation(st[:, 26:27], st[:, 25:26], ACT.Sqrt, bias=eps_s[0:F, :]).then_inc(fsd_ready, 1)

            def finished(k):
                t0, nt = FIN[k]
                act.wait_ge(fin_scale, k + 1)
                if k >= 2:
                    act.wait_ge(out_stored[k % 2], 16 * (k // 2))
                for i in range(nt):
                    t = t0 + i
                    last = nc.scalar.activation(res[k % 2][:, i, :], x1[:, t * F:(t + 1) * F], ACT.Identity,
                                                scale=rstd[:, t:t + 1], bias=shift[:, t:t + 1])
                last.then_inc(fin_ready, 1)

            for k, (t0, nt) in enumerate(FIN):
                act.wait_ge(fin_var, k + 1)
                nc.scalar.activation(rstd[:, t0:t0 + nt], mv[:, t0:t0 + nt, 1], ACT.Sqrt,
                                     bias=eps_s[:, :]).then_inc(fin_sd, 1)
                if k >= LAG:
                    finished(k - LAG)
            for k in range(len(FIN) - LAG, len(FIN)):
                finished(k)

        @block.vector
        def _(dve):
            chain = [0]

            def link(ins):
                chain[0] += 1
                ins.then_inc(dve_step, 1)
                dve.wait_ge(dve_step, chain[0])

            def attribute_rest(k, i):
                work = (work_a, work_b)[k]
                dve.wait_ge(part_ready[k], i + 1)
                nc.vector.tensor_tensor(work[:, 0:SPLIT], work[:, 0:SPLIT], split_parts[k][i], ALU.subtract
                                        ).then_inc(rest_ready[k], 1)

            def edge_weight_parts():
                dve.wait_ge(loaded_wedge, 16 * PARTS * PARTS)
                for i in range(PARTS):
                    link(nc.vector.tensor_copy(wedge_p[i][:, :], wedge_f[:, :]))
                    if i < PARTS - 1:
                        link(nc.vector.tensor_tensor(wedge_f[:, :], wedge_f[:, :], wedge_p[i][:, :], ALU.subtract))
                rows = PARTS * (D1 + 1)
                link(nc.vector.tensor_scalar(third[:, 0:1], part[0:KE, :], float(rows), None, ALU.is_lt))
                link(nc.vector.tensor_scalar(third[:, 2:3], part[0:KE, :], float(2 * rows), None, ALU.is_ge))
                link(nc.vector.tensor_tensor(third[:, 1:2], third[:, 0:1], third[:, 2:3], ALU.add))
                link(nc.vector.tensor_scalar(third[:, 1:2], third[:, 1:2], 0.0, None, ALU.is_equal))
                link(nc.vector.tensor_scalar(wedge_s[:, :], wedge_p[0][:, :], third[:, 0:1], None, ALU.mult))
                link(nc.vector.scalar_tensor_tensor(wedge_s[:, :], wedge_p[1][:, :], third[:, 1:2], wedge_s[:, :],
                                                    ALU.mult, ALU.add))
                nc.vector.scalar_tensor_tensor(wedge_s[:, :], wedge_p[2][:, :], third[:, 2:3], wedge_s[:, :],
                                               ALU.mult, ALU.add).then_inc(wedge_ready, 1)

            def later_rests(h):
                if h < 2 * (PARTS - 1) - 1:
                    attribute_rest((h + 1) % 2, (h + 1) // 2)
                if h == 2 * (PARTS - 1) - 1:
                    edge_weight_parts()

            link(nc.vector.memset(eps_s[:, :], EPS))
            for s in range(SLOTS):
                link(nc.vector.memset(msg[s][:, :, F:F + 1], 1.0))
            nc.vector.memset(sq_sum[:, :, :], 0.0).then_inc(L[1].sq_added, 1)
            nc.vector.memset(nf_sums[:, :, :], 0.0).then_inc(nf_added, 2)

            dve.wait_ge(loaded_idx, 32)
            dve.wait_ge(pool_const, 7)
            nc.vector.tensor_copy(first_f[:, :], first_i[:, :]).then_inc(first_ready, 1)
            link(nc.vector.tensor_scalar(part_w[:, :], part[:, :], float(F), None, ALU.subtract))
            nc.vector.scalar_tensor_tensor(floor[:, :, :].rearrange("p r h -> p (r h)")[:, 0:MACROS], first_f[:, :], 0.0,
                                           floor[:, :, :].rearrange("p r h -> p (r h)")[:, 0:MACROS], ALU.add, ALU.is_ge,
                                           accum_out=floor_met[:, :]).then_inc(floor_counted, 1)
            dve.wait_ge(first_spread, 1)
            link(nc.vector.tensor_copy(first_all[:, :], bank[0][:, 0:MACROS]))
            link(nc.vector.tensor_tensor(rel[:, :].rearrange("p (m g) -> p m g", g=GROUP),
                                         dst_i[:, 0:TILES].rearrange("p (m g) -> p m g", g=GROUP),
                                         first_all[:, :].unsqueeze(2).to_broadcast([P, MACROS, GROUP]), ALU.subtract))
            above, inside = (dst_b[k][:, 0:TILES].bitcast(fp32) for k in range(2))
            link(nc.vector.tensor_scalar(above, rel[:, :], 0.0, None, ALU.is_ge))
            nc.vector.scalar_tensor_tensor(inside, rel[:, :], float(WINDOW), above, ALU.is_lt,
                                           ALU.mult, accum_out=in_window[:, :]).then_inc(window_counted, 1)
            dve.wait_ge(window_total, 1)
            link(nc.vector.tensor_scalar(flag_f[:, :], bank[1][0:1, 0:1], float(TILES * P), None, ALU.is_equal))
            dve.wait_ge(window_counted, 1)
            dve.wait_ge(floor_counted, 1)
            link(nc.vector.scalar_tensor_tensor(flag_f[:, :], floor_met[:, :], float(MACROS), flag_f[:, :],
                                                ALU.is_equal, ALU.mult))
            nc.vector.tensor_copy(flag_i[:, :], flag_f[:, :]).then_inc(flag_ready, 1)
            nc.vector.tensor_scalar(centre[:, :], ident[0:F, 0:F], 1.0 / F, None, ALU.subtract).then_inc(centre_ready, 1)
            dve.wait_ge(centre_ready, 1)
            link(nc.vector.tensor_copy(zw_s[:, 2 * F:3 * F], centre[:, :]))
            dve.wait_ge(centred_mm, 1)
            link(nc.vector.tensor_copy(zw_s[:, 0:2 * F], bank[2][0:F, 0:2 * F]))
            nc.vector.tensor_copy(cn_s[:, :], bank[2][0:F, 2 * F:3 * F]).then_inc(centred_ready, 1)
            attribute_rest(0, 0)
            dve.wait_ge(flag_ready, 1)
            ordered = dve.value_load(flag_i[0:1, 0:1], min_val=0, max_val=1)

            def fast(n):
                s = L[n]
                height = F + 1 if n == 0 else F

                def add_sums(m, c):
                    dve.wait_ge(s.seg_mm, m + 1)
                    base = dve.value_load(first_i[0:1, ds(m, 1)], min_val=0, max_val=N - 1)
                    dve.wait_ge(s.acc_added, m + 2)
                    at = acc[0:height, ds(base, WINDOW)]
                    nc.vector.tensor_tensor(at, at, seg_ps[c][0:height, :], ALU.add).then_inc(s.acc_added, 1)
                    if n == 1:
                        dve.wait_ge(s.msg_sq_ready, m + 1)
                        dve.wait_ge(s.sq_added, m + 1)
                        if is_last(m):
                            nc.vector.tensor_tensor(sq_sum[0:TAIL, GROUP - 1, :], sq_sum[0:TAIL, GROUP - 1, :],
                                                    msg_sq[c][0:TAIL, GROUP - 1, :], ALU.add).then_inc(s.sq_added, 1)
                            whole = slice(0, GROUP - 1)
                        else:
                            whole = slice(0, GROUP)
                        nc.vector.tensor_tensor(sq_sum[:, whole, :], sq_sum[:, whole, :], msg_sq[c][:, whole, :],
                                                ALU.add).then_inc(s.sq_added, 1)

                def turned_onehot(m, q, h):
                    u, filled, place = unit_of(q, h)
                    dve.wait_ge(s.dst_in[u], filled * 16)
                    if past(m, 2):
                        dve.wait_ge(s.pre_mm, m - 1)
                    nc.vector.tensor_scalar(edge_in[h % 2][window, :], dst_b[u][window, place * MACRO:(place + 1) * MACRO],
                                            first_all[window, ds(m, 1)], part_w[window, :], ALU.subtract, ALU.is_equal
                                            ).then_inc(s.onehot_t_ready, 1)

                def step(m, q, h, node_work):
                    c = h % SLOTS
                    if past(m, SLOTS):
                        dve.wait_ge(s.seg_mm, m - (SLOTS - 1))
                    nc.vector.tensor_tensor(
                        onehot[c][:, :, :], rel[:, ds(m * GROUP, GROUP)].unsqueeze(2).to_broadcast([P, GROUP, WINDOW]),
                        cols[:, :].unsqueeze(1).to_broadcast([P, GROUP, WINDOW]), ALU.is_equal).then_inc(s.onehot_ready, 1)
                    if n == 1 and not is_last(m):
                        turned_onehot(m + 1, q, h + 1)
                    dve.wait_ge(s.pre_mm, m + 1)
                    if node_work == "features" and h == NODE_STEP:
                        node_pre(q, q + 1, pre_bank[c][:, GROUP * F:(GROUP + 1) * F])
                    if node_work == "mlp":
                        product = pre_bank[c][0:F, GROUP * F:GROUP * F + STRIP]
                        if h == 1:
                            strip_hidden(product)
                        elif h == 2:
                            strip_out(q - STRIP_ROUND, product)
                    dve.wait_ge(s.gathered[c], slot_uses(q, h) * (16 * GROUP))
                    nc.vector.tensor_tensor(gath[c][:, :, :], gath[c][:, :, :], pre_ps[c], ALU.add).then_inc(s.pre_ready, 1)
                    if past(m, 1):
                        add_sums(m - 1, (h - 1) % SLOTS)
                    if node_work == "mlp":
                        if h == 0:
                            dve.wait_ge(s.acc_added, m + 2)
                            strip_state(q - STRIP_ROUND)
                        elif h == 3:
                            strip_statistics(q - STRIP_ROUND)
                    if h == NODE_STEP + 1:
                        if node_work == "features":
                            node_sums(q, q + 1)
                        elif node_work == "combine":
                            combine(q - FEATURED)

                if n == 1:
                    short_tile()
                    turned_onehot(0, 0, 0)
                sweep(dve, step, spans_of(n, (None, node_scale if n == 1 else before_strips)), later_rests if n == 0 else None)
                add_sums(MACROS - 1, 0)
                dve.wait_ge(s.edge_relu, MACROS)
                dve.wait_ge(s.msg_ready, MACROS)
                if n == 0:
                    dve.wait_ge(s.edge_sq, MACROS)
                    dve.wait_ge(strip_counted, STRIPS)
                else:
                    dve.wait_ge(s.msg_sq_ready, MACROS)
                    dve.wait_ge(s.onehot_t_ready, MACROS)
                    dve.wait_ge(s.sq_added, MACROS + 2)
                for c in range(SLOTS):
                    uses = 2 * ROUNDS + (c == 0)
                    if n == 0:
                        dve.wait_ge(s.ea32_in[c], 16 * uses)
                    else:
                        dve.wait_ge(s.v_in[c], 16 * uses)
                for u in range(2):
                    fills = ROUNDS + (u == 0)
                    dve.wait_ge(s.src_in[u], 16 * fills)
                    dve.wait_ge(s.ea4_in[u], 16 * PARTS * (fills - 1 if n == 0 else fills))
                    if n == 1:
                        dve.wait_ge(s.dst_in[u], 16 * fills)
                dve.wait_ge(s.acc_added, MACROS + 2)

            def before_strips():
                dve.wait_ge(loaded_x, 16)
                dve.wait_ge(loaded_w, 16 * 8)
                dve.wait_ge(parts_stored, 16 * 2 * PARTS)

            def strip_state(i):
                at = ds(i * STRIP, STRIP)
                nc.vector.tensor_tensor(h_strip[:, :], acc[0:F, at], z[0:F, at], ALU.add).then_inc(h_ready, 1)

            def strip_hidden(ps):
                nc.vector.tensor_scalar(r_strip[:, :], ps, vec[:, B1:B1 + 1], 0.0, ALU.add, ALU.max).then_inc(r_ready, 1)

            def strip_out(i, ps):
                nc.vector.tensor_scalar(work_a[0:F, ds(i * STRIP, STRIP)], ps, vec[:, B2:B2 + 1], None, ALU.add
                                        ).then_inc(h2_ready, 1)

            def strip_statistics(i):
                dve.wait_ge(h2_ready, i + 1)
                dve.sem_inc(may_stats, 1)
                nc.vector.bn_stats(h2_stats[:, ds(i * 6, 6)], work_a[0:F, ds(i * STRIP, STRIP)]).then_inc(strip_counted, 1)

            def node_pre(t, done, ps):
                dve.wait_ge(nf_relu, done)
                nc.vector.scalar_tensor_tensor(nf_pre[:, :], ps, rstd[:, ds(t, 1)], b_nodes[:, :], ALU.mult, ALU.add
                                               ).then_inc(nf_pre_ready, 1)

            def node_sums(t, done, rows=P):
                dve.wait_ge(nf_squared, done + 1)
                dve.wait_ge(nf_added, done * 2 + 2)
                nc.vector.tensor_tensor(nf_sums[0:rows, 0, :], nf_sums[0:rows, 0, :], work_a[0:rows, ds(t * F, F)], ALU.add
                                        ).then_inc(nf_added, 1)
                nc.vector.tensor_tensor(nf_sums[0:rows, 1, :], nf_sums[0:rows, 1, :], nf_sq[0:rows, :], ALU.add
                                        ).then_inc(nf_added, 1)

            def short_tile():
                dve.wait_ge(nf_mm, 1)
                nc.vector.scalar_tensor_tensor(nf_pre[:, :], bank[6][:, 0:F], rstd[:, NODE_TILES - 1:NODE_TILES],
                                               b_nodes[:, :], ALU.mult, ALU.add).then_inc(nf_pre_ready, 1)
                node_sums(NODE_TILES - 1, 0, rows_of(NODE_TILES - 1))

            def node_scale():
                dve.wait_ge(nf_total, 1)
                link(nc.vector.tensor_copy(st[:, 0:2], bank[0][0:F, 0:2]))
                link(nc.vector.tensor_scalar(st[:, 10:12], st[:, 0:2], 1.0 / N, None, ALU.mult))
                link(nc.vector.tensor_tensor(st[:, 17:18], st[:, 10:11], st[:, 10:11], ALU.mult))
                nc.vector.tensor_tensor(st[:, 18:19], st[:, 11:12], st[:, 17:18], ALU.subtract).then_inc(nf_var, 1)
                dve.wait_ge(nf_sd, 1)
                link(nc.vector.reciprocal(st[:, 20:21], st[:, 19:20]))
                link(nc.vector.tensor_tensor(st[:, 28:29], st[:, 20:21], vec[:, GNODE:GNODE + 1], ALU.mult))
                link(nc.vector.tensor_tensor(st[:, 24:25], st[:, 10:11], st[:, 28:29], ALU.mult))
                link(nc.vector.tensor_tensor(st[:, 27:28], vec[:, BETNODE:BETNODE + 1], st[:, 24:25], ALU.subtract))
                link(nc.vector.tensor_copy(wide[:, 0, :], st[:, 28:29].to_broadcast([F, P])))
                nc.vector.tensor_copy(wide[:, 1, :], st[:, 27:28].to_broadcast([F, P])).then_inc(nf_vectors, 1)
                dve.wait_ge(nf_spread, 1)
                nc.vector.tensor_copy(nf_scale[:, :, :], bank[0][:, 0:2 * F].rearrange("p (k f) -> p k f", k=2)
                                      ).then_inc(nf_scaled, 1)
                dve.wait_ge(nf_scaled, 1)

            def combine(i):
                at = ds(i * (COMBINE * F), COMBINE * F)
                nf = work_a[:, at].rearrange("p (t f) -> p t f", f=F)
                x1_at = x1[:, at].rearrange("p (t f) -> p t f", f=F)
                per_feature = lambda k: nf_scale[:, k, :].unsqueeze(1).to_broadcast([P, COMBINE, F])
                nc.vector.tensor_tensor(nf, nf, per_feature(0), ALU.mult).then_inc(combined, 1)
                nc.vector.tensor_tensor(x1_at, x1_at, per_feature(1), ALU.add).then_inc(combined, 1)
                dve.wait_ge(combined, i * 3 + 2)
                nc.vector.tensor_tensor(x1_at, x1_at, nf, ALU.add).then_inc(combined, 1)

            def general(n):
                s = L[n]
                if n == 1:
                    short_tile()
                    with dve.Fori(0, FEATURED) as t:
                        dve.wait_ge(nf_mm, t + 2)
                        node_pre(t, t + 1, bank[6][:, 0:F])
                        node_sums(t, t + 1)
                    node_scale()
                    with dve.Fori(0, COMBINES) as i:
                        combine(i)
                    dve.wait_ge(u_stored, 16 * len(STORES))
                else:
                    for h in range(UNROLL):
                        later_rests(h)
                    dve.wait_ge(parts_stored, 16 * 2 * PARTS)
                dve.wait_ge(s.acc_added, 2)
                nc.vector.memset(work_b[:, :], 0.0).then_inc(s.g_zero, 1)
                own = sem(f"g_dve_{n}")
                STEPS = 7
                with dve.Fori(0, TILES) as t:
                    def then(k, ins):
                        ins.then_inc(own, 1)
                        dve.wait_ge(own, t * STEPS + k)
                    dve.wait_ge(s.g_in, (t + 1) * (16 * G_LOADS[n]))
                    then(1, nc.vector.tensor_copy(g_dst_f[:, :], g_dst[:, :]))
                    then(2, nc.vector.tensor_scalar(g_same[:, :], g_row[:, :], g_dst_f[:, :], None, ALU.is_equal))
                    then(3, nc.vector.tensor_tensor(g_tmp[:, :], g_same[:, :], before[:, :], ALU.mult))
                    then(4, nc.vector.tensor_reduce(g_dup[:, :], g_tmp[:, :], AX.X, ALU.add))
                    then(5, nc.vector.tensor_scalar(g_isfirst[:, :], g_dup[:, :], 0.0, None, ALU.is_equal))
                    then(6, nc.vector.tensor_tensor(g_diff[:, :], g_dst_f[:, :], dump[:, :], ALU.subtract))
                    then(7, nc.vector.scalar_tensor_tensor(g_to_f[:, :], g_diff[:, :], g_isfirst[:, :], dump[:, :],
                                                           ALU.mult, ALU.add))
                    nc.vector.tensor_copy(g_to[:, :], g_to_f[:, :]).then_inc(s.g_selected, 1)
                    nc.vector.tensor_scalar(g_valid[:, :], g_dst_f[:, :], float(N), None, ALU.is_lt).then_inc(s.g_selected, 1)
                    dve.wait_ge(s.pre_mm, t + 1)
                    dve.wait_ge(s.g_got, (t + 1) * 32)
                    if n == 1:
                        dve.wait_ge(s.g_got_v, (t + 1) * 16)
                        nc.vector.tensor_tensor(g_v[:, :], g_v[:, :], pre_ps[0][:, 0, :], ALU.add).then_inc(s.onehot_ready, 1)
                        dve.wait_ge(s.onehot_ready, t + 1)
                        nc.vector.tensor_tensor(gath[0][:, 0, :], gath[0][:, 0, :], g_v[:, :], ALU.add).then_inc(s.pre_ready, 1)
                        dve.wait_ge(s.msg_sq_ready, t + 1)
                        dve.wait_ge(s.sq_added, t + 1)
                        nc.vector.scalar_tensor_tensor(sq_sum[:, 0, :], msg_sq[0][:, 0, :], g_valid[:, :],
                                                       sq_sum[:, 0, :], ALU.mult, ALU.add).then_inc(s.sq_added, 1)
                    else:
                        nc.vector.tensor_tensor(gath[0][:, 0, :], gath[0][:, 0, :], pre_ps[0][:, 0, :], ALU.add
                                                ).then_inc(s.pre_ready, 1)
                    dve.wait_ge(s.g_sum, t + 1)
                    nc.vector.tensor_tensor(g_new[:, :], g_cur[:, :], bank[3][:, 0:F + 1], ALU.add).then_inc(s.g_new, 1)
                height = F + 1 if n == 0 else F
                for i in range(ROWS // P):
                    dve.wait_ge(s.g_turned, i + 1)
                    nodes = acc[0:height, i * P:(i + 1) * P]
                    nc.vector.tensor_tensor(nodes, nodes, bank[i % 2][0:height, 0:P], ALU.add).then_inc(s.g_stored, 1)
                dve.wait_ge(s.g_stored, ROWS // P)
                if n == 0:
                    before_strips()
                    with dve.Fori(0, STRIPS) as i:
                        strip_state(i)
                        dve.wait_ge(strip_mm, i * 2 + 1)
                        strip_hidden(bank[6][0:F, 0:STRIP])
                        dve.wait_ge(strip_mm, i * 2 + 2)
                        strip_out(i, bank[7][0:F, 0:STRIP])
                        strip_statistics(i)
                    dve.wait_ge(strip_counted, STRIPS)
                dve.wait_ge(s.msg_ready, TILES)
                dve.wait_ge(s.g_selected, 2 * TILES)
                dve.wait_ge(s.g_written, 16 * TILES)
                dve.wait_ge(s.g_row_in, 16 * (ROWS // P))
                if n == 0:
                    dve.wait_ge(s.ea4_in[0], 16 * PARTS * MACROS)
                    dve.wait_ge(s.edge_sq, MACROS)
                else:
                    dve.wait_ge(s.edge_relu, TILES)
                    dve.wait_ge(s.sq_added, TILES + 1)

            before_branch = chain[0]
            with dve.If(ordered == 1):
                fast(0)
            after_branch, chain[0] = chain[0], before_branch
            with dve.Else():
                general(0)
            assert chain[0] == after_branch
            nc.vector.memset(st[:, :], 0.0).then_inc(L[0].swept, 1)
            dve.wait_ge(L[0].swept, 1)

            rest = acc[0:F, REST:N]
            nc.vector.tensor_tensor(rest, rest, z[0:F, REST:N], ALU.add).then_inc(h_ready, 1)
            link(nc.vector.tensor_reduce(st[:, 8:9], edge_sums[:, 0, :], AX.X, ALU.add))
            link(nc.vector.tensor_reduce(st[:, 9:10], edge_sums[:, 1, :], AX.X, ALU.add))
            link(nc.vector.tensor_scalar(st[:, 10:12], st[:, 8:10], 1.0 / E, None, ALU.mult))
            link(nc.vector.tensor_tensor(st[:, 12:13], st[:, 10:11], st[:, 10:11], ALU.mult))
            nc.vector.tensor_tensor(st[:, 13:14], st[:, 11:12], st[:, 12:13], ALU.subtract).then_inc(evar_ready, 1)
            dve.wait_ge(h2_ready, STRIPS + 1)
            link(nc.vector.bn_stats(h2_stats[:, STRIPS * 6:(STRIPS + 1) * 6], work_a[0:F, REST:N]))
            nc.vector.bn_aggr(h2_mv[:, :], h2_stats[:, :].rearrange("p (i s) -> p i s", s=6)).then_inc(var0_ready, 1)
            dve.wait_ge(var0_ready, 1)
            dve.wait_ge(sd0_ready, 1)
            link(nc.vector.reciprocal(st[:, 4:5], st[:, 3:4]))
            link(nc.vector.tensor_tensor(st[:, 5:6], st[:, 4:5], vec[:, GAM0:GAM0 + 1], ALU.mult))
            link(nc.vector.tensor_tensor(st[:, 0:1], h2_mv[:, 0:1], st[:, 5:6], ALU.mult))
            nc.vector.tensor_tensor(st[:, 6:7], vec[:, BET0:BET0 + 1], st[:, 0:1], ALU.subtract).then_inc(bn0_ready, 1)
            def residual(c):
                o, w = CHUNKS[c]
                at = work_a[0:F, o:o + w]
                if c % 2 == 0:
                    dve.wait_ge(y_ready, c // 2 + 1)
                    nc.vector.tensor_tensor(z[0:F, o:o + w], at, z[0:F, o:o + w], ALU.add).then_inc(z_ready, 1)
                else:
                    link(nc.vector.tensor_scalar(at, at, st[:, 5:6], st[:, 6:7], ALU.mult, ALU.add))
                    nc.vector.scalar_tensor_tensor(z[0:F, o:o + w], at, 0.0, z[0:F, o:o + w], ALU.max, ALU.add
                                                   ).then_inc(z_ready, 1)

            def scales(k):
                t = slice(2 * k, 2 * k + 2)
                dve.wait_ge(zsd_ready, k + 1)
                nc.vector.reciprocal(rstd[:, t], rstd[:, t]).then_inc(zscale_ready, 1)

            dve.wait_ge(bn0_ready, 1)
            for c in range(AHEAD):
                residual(c)
            for k in range(UV_PAIRS):
                if k % 2 == 0 and k // 2 + AHEAD < NC:
                    residual(k // 2 + AHEAD)
                dve.wait_ge(zw_mm, 2 * k + 2)
                for t in (2 * k, 2 * k + 1):
                    last = nc.vector.bn_stats(bn6[:, t, :], bank[t % ZW_BANKS][:, 2 * F:3 * F])
                link(last)
                for t in (2 * k, 2 * k + 1):
                    last = nc.vector.bn_aggr(mv[:, t, :], bn6[:, t, :])
                last.then_inc(zvar_ready, 1)
                if k:
                    scales(k - 1)
            scales(UV_PAIRS - 1)
            dve.wait_ge(esd_ready, 1)
            link(nc.vector.reciprocal(st[:, 15:16], st[:, 14:15]))
            link(nc.vector.tensor_tensor(st[:, 16:17], st[:, 15:16], vec[:, GEDGE:GEDGE + 1], ALU.mult))
            for c in range(SLOTS):
                link(nc.vector.tensor_scalar(edge_w[c][0:F, :], wmsg_s[:, 2, :], st[:, 16:17], None, ALU.mult))
            link(nc.vector.tensor_tensor(st[:, 27:28], st[:, 10:11], st[:, 16:17], ALU.mult))
            link(nc.vector.tensor_tensor(edge_shift[:, :], vec[:, BETEDGE:BETEDGE + 1], st[:, 27:28], ALU.subtract))
            nc.vector.tensor_copy(wide[:, 0, :], vec[:, BNODE:BNODE + 1].to_broadcast([F, P])).then_inc(wide_ready, 1)
            dve.wait_ge(const_mm, 1)
            nc.vector.tensor_copy(msg_const[:, :], bank[7][0:1, 0:F]).then_inc(const_ready, 1)
            link(nc.vector.tensor_copy(b_nodes[:, :], bank[7][:, F:2 * F]))
            dve.wait_ge(zscale_ready, UV_PAIRS)
            before_branch = chain[0]
            with dve.If(ordered == 1):
                fast(1)
            after_branch, chain[0] = chain[0], before_branch
            with dve.Else():
                general(1)
            assert chain[0] == after_branch
            nc.vector.memset(st[:, 30:31], 0.0).then_inc(L[1].swept, 1)
            dve.wait_ge(sq_total, 1)
            link(nc.vector.tensor_copy(st[:, 21:22], bank[7][0:F, 0:1]))

            link(nc.vector.tensor_reduce(st[:, 22:23], acc[0:F, 0:N // 2], AX.X, ALU.add))
            dve.wait_ge(half_sum, 1)
            link(nc.vector.tensor_tensor(st[:, 22:23], st[:, 22:23], st[:, 31:32], ALU.add))
            link(nc.vector.tensor_scalar(st[:, 23:24], st[:, 22:23], -1.0 / E, None, ALU.mult))
            link(nc.vector.tensor_tensor(st[:, 24:25], st[:, 23:24], st[:, 23:24], ALU.mult))
            nc.vector.scalar_tensor_tensor(st[:, 25:26], st[:, 21:22], 1.0 / E, st[:, 24:25],
                                           ALU.mult, ALU.subtract).then_inc(fvar_ready, 1)
            dve.wait_ge(fvar_ready, 1)
            dve.wait_ge(fsd_ready, 1)
            link(nc.vector.reciprocal(st[:, 29:30], st[:, 26:27]))
            link(nc.vector.tensor_tensor(st[:, 29:30], st[:, 29:30], vec[:, GMSG:GMSG + 1], ALU.mult))
            link(nc.vector.tensor_scalar(scale_m[:, 0:F], ident[0:F, 0:F], st[:, 29:30], None, ALU.mult))
            nc.vector.scalar_tensor_tensor(scale_m[:, F:F + 1], st[:, 23:24], st[:, 29:30], vec[:, BETMSG:BETMSG + 1],
                                           ALU.mult, ALU.add).then_inc(scales_ready, 1)
            dve.wait_ge(mats_mm, 1)
            nc.vector.tensor_copy(mat_m[:, :], bank[1][0:F + 1, 0:F]).then_inc(mats_ready, 1)

            def final_scales(k):
                t0, nt = FIN[k]
                t = slice(t0, t0 + nt)
                dve.wait_ge(fin_sd, k + 1)
                link(nc.vector.reciprocal(rstd[:, t], rstd[:, t]))
                nc.vector.scalar_tensor_tensor(shift[:, t], mv[:, t, 0], -1.0, rstd[:, t], ALU.mult, ALU.mult
                                               ).then_inc(fin_scale, 1)

            for k, (t0, nt) in enumerate(FIN):
                at = x1[:, t0 * F:(t0 + nt) * F]
                dve.wait_ge(fin_mm, k + 1)
                link(nc.vector.tensor_tensor(at, at, bank[2 + k % 4][:, 0:nt * F], ALU.add))
                for i in range(nt):
                    last = nc.vector.bn_stats(bn6[:, t0 + i, :], x1[:, (t0 + i) * F:(t0 + i + 1) * F])
                link(last)
                for i in range(nt):
                    last = nc.vector.bn_aggr(mv[:, t0 + i, :], bn6[:, t0 + i, :])
                last.then_inc(fin_var, 1)
                if k >= LAG:
                    final_scales(k - LAG)
            for k in range(len(FIN) - LAG, len(FIN)):
                final_scales(k)

        @block.tensor
        def _(pe):
            pe.wait_ge(pool_const, 7)
            pe.wait_ge(first_ready, 1)
            nc.tensor.matmul(bank[0][:, 0:MACROS], ones[0:1, :], first_f[:, :], start=True, stop=True).then_inc(first_spread, 1)
            pe.wait_ge(window_counted, 1)
            nc.tensor.matmul(bank[1][0:1, 0:1], in_window[:, :], ones[:, 0:1], start=True, stop=True).then_inc(window_total, 1)
            pe.wait_ge(loaded_w, 16 * 8)
            pe.wait_ge(centre_ready, 1)
            nc.tensor.matmul(bank[2][0:F, 0:2 * F], centre[:, :], wmsg_s[:, 0:2, :].rearrange("p k f -> p (k f)"),
                             start=True, stop=True)
            nc.tensor.matmul(bank[2][0:F, 2 * F:3 * F], centre[:, :], wn_s[:, :], start=True, stop=True).then_inc(centred_mm, 1)
            pe.wait_ge(centred_ready, 1)

            def fast(n):
                s = L[n]
                height = F + 1 if n == 0 else F

                def segments(m, c):
                    pe.wait_ge(s.msg_ready, m + 1)
                    pe.wait_ge(s.onehot_ready, m + 1)
                    if past(m, SLOTS):
                        pe.wait_ge(s.acc_added, m - (SLOTS - 2))
                    for g in range(GROUP):
                        mm = nc.tensor.matmul(seg_ps[c][0:height, :], msg[c][:, g, 0:height], onehot[c][:, g, :],
                                              start=(g == 0), stop=(g == GROUP - 1))
                    mm.then_inc(s.seg_mm, 1)

                def edge_features(m, q, h):
                    u, filled, place = unit_of(q, h)
                    if past(m, 2):
                        pe.wait_ge(s.edge_relu, m - 1)
                    macro = slice(place * MACRO, (place + 1) * MACRO)
                    if n == 0 and not past(m, UNROLL):
                        pe.wait_ge(ea4_first[u], 16)
                        nc.tensor.matmul(eh_ps[h % 2][0:F, :], wedge_s32[:, :], ea4_32[u][:, macro],
                                         start=True, stop=True).then_inc(s.edge_mm, 1)
                        return
                    if n == 0:
                        if not past(m, UNROLL + 1):
                            pe.wait_ge(wedge_ready, 1)
                        filled = filled - 1
                    pe.wait_ge(s.ea4_in[u], filled * (16 * PARTS))
                    nc.tensor.matmul(eh_ps[h % 2][0:F, :], wedge_s[:, :], ea4[u][:, macro],
                                     start=True, stop=True).then_inc(s.edge_mm, 1)

                def step(m, q, h, node_work):
                    c = h % SLOTS
                    if past(m, SLOTS):
                        pe.wait_ge(s.pre_ready, m - (SLOTS - 1))
                    if n == 0:
                        pe.wait_ge(s.ea32_in[c], slot_uses(q, h) * 16)
                    else:
                        pe.wait_ge(s.edge_relu, m + 1)
                        pe.wait_ge(s.onehot_t_ready, m + 1)
                        pe.wait_ge(s.v_in[c], slot_uses(q, h) * 16)
                    if node_work == "features" and h == NODE_STEP:
                        node_matmul(q + 1, pre_bank[c][:, GROUP * F:(GROUP + 1) * F])
                    if node_work == "mlp" and h in (1, 2):
                        strip_matmul(q - STRIP_ROUND, h - 1, pre_bank[c][0:F, GROUP * F:GROUP * F + STRIP])
                    for g in range(GROUP):
                        tile = slice(g * P, (g + 1) * P)
                        if n == 0:
                            mm = nc.tensor.matmul(pre_ps[c][:, g, :], ea32[c][:, tile], we_s[:, :], start=True, stop=True)
                        else:
                            mm = nc.tensor.matmul(pre_ps[c][:, g, :], edge_in[h % 2][:, tile], edge_w[c][:, :], start=True, stop=True)
                    mm.then_inc(s.pre_mm, 1)
                    if not is_last(m):
                        edge_features(m + 1, q, h + 1)
                    if past(m, 1):
                        segments(m - 1, (h - 1) % SLOTS)

                if n == 1:
                    node_matmul(0, bank[6][:, 0:F]).then_inc(nf_mm, 1)
                    pe.wait_ge(nf_pre_ready, 1)
                edge_features(0, 0, 0)
                sweep(pe, step, spans_of(n, (None, node_scale if n == 1 else None)))
                segments(MACROS - 1, 0)

            def strip_matmul(i, second, to):
                pe.wait_ge(r_ready if second else h_ready, i + 1)
                return nc.tensor.matmul(to, (w2_s if second else w1_s)[:, :], (r_strip if second else h_strip)[:, :],
                                        start=True, stop=True)

            def node_matmul(done, to):
                pe.wait_ge(z_tile_ready, done + 1)
                return nc.tensor.matmul(to, z_tile[:, :], cn_s[:, :], start=True, stop=True)

            def node_scale(in_loop=True):
                pe.wait_ge(nf_added, 2 * (NODE_TILES + 1))
                if in_loop:
                    pe.wait_ge(L[1].pre_ready, FEATURED * UNROLL - (SLOTS - 1))
                for k in range(2):
                    mm = nc.tensor.matmul(bank[0][0:F, k:k + 1], nf_sums[:, k, :], ones[:, 0:1], start=True, stop=True)
                mm.then_inc(nf_total, 1)
                pe.wait_ge(nf_vectors, 1)
                for k in range(2):
                    mm = nc.tensor.matmul(bank[0][:, k * F:(k + 1) * F], wide[:, k, :], ident[0:F, 0:F], start=True, stop=True)
                mm.then_inc(nf_spread, 1)
                pe.wait_ge(nf_scaled, 1)

            def general(n):
                s = L[n]
                if n == 1:
                    node_matmul(0, bank[6][:, 0:F]).then_inc(nf_mm, 1)
                    with pe.Fori(0, FEATURED) as t:
                        pe.wait_ge(nf_pre_ready, t + 1)
                        node_matmul(t + 1, bank[6][:, 0:F]).then_inc(nf_mm, 1)
                    node_scale(False)
                if n == 0:
                    def edge_features(m):
                        pe.wait_ge(s.ea4_in[0], (m + 1) * (16 * PARTS))
                        nc.tensor.matmul(eh_ps[0][0:F, :], wedge_s[:, :], ea4[0][:, 0:MACRO], start=True, stop=True
                                         ).then_inc(s.edge_mm, 1)

                    pe.wait_ge(wedge_ready, 1)
                    edge_features(0)
                    with pe.Fori(1, MACROS) as m:
                        pe.wait_ge(s.edge_sq, m)
                        edge_features(m)
                with pe.Fori(0, TILES) as t:
                    pe.wait_ge(s.g_in, (t + 1) * (16 * G_LOADS[n]))
                    if n == 0:
                        nc.tensor.matmul(pre_ps[0][:, 0, :], ea32[0][:, 0:P], we_s[:, :], start=True, stop=True
                                         ).then_inc(s.pre_mm, 1)
                    else:
                        nc.tensor.matmul(eh_ps[0][0:F, 0:P], wedge_s[:, :], ea4[0][:, 0:P], start=True, stop=True
                                         ).then_inc(s.edge_mm, 1)
                        pe.wait_ge(s.edge_relu, t + 1)
                        nc.tensor.matmul(pre_ps[0][:, 0, :], edge_in[0][0:F, 0:P], edge_w[0][0:F, :], start=True, stop=False)
                        nc.tensor.matmul(pre_ps[0][:, 0, :], ones[0:1, :], msg_const[:, :], start=False, stop=True
                                         ).then_inc(s.pre_mm, 1)
                    pe.wait_ge(s.msg_ready, t + 1)
                    pe.wait_ge(s.g_selected, (t + 1) * 2)
                    nc.tensor.matmul(bank[3][:, 0:F + 1], g_same[:, :], msg[0][:, 0, :], start=True, stop=True
                                     ).then_inc(s.g_sum, 1)
                for i in range(ROWS // P):
                    pe.wait_ge(s.g_row_in, 16 * (i + 1))
                    if i >= 2:
                        pe.wait_ge(s.g_stored, i - 1)
                    nc.tensor.matmul(bank[i % 2][0:F + 1, 0:P], g_cur[:, :], ident[:, :], start=True, stop=True
                                     ).then_inc(s.g_turned, 1)
                if n == 0:
                    with pe.Fori(0, STRIPS) as i:
                        for second in range(2):
                            strip_matmul(i, second, bank[6 + second][0:F, 0:STRIP]).then_inc(strip_mm, 1)

            pe.wait_ge(flag_ready, 1)
            ordered = pe.value_load(flag_i[0:1, 0:1], min_val=0, max_val=1)
            with pe.If(ordered == 1):
                fast(0)
            with pe.Else():
                general(0)
            pe.wait_ge(L[0].swept, 1)

            pe.wait_ge(h_ready, STRIPS + 1)
            nc.tensor.matmul(bank[0][0:F, 0:N - REST], w1_s[:, :], acc[0:F, REST:N], start=True, stop=True).then_inc(w1_mm, 1)
            pe.wait_ge(r_ready, STRIPS + 1)
            nc.tensor.matmul(bank[4][0:F, 0:N - REST], w2_s[:, :], work_b[0:F, REST:N], start=True, stop=True
                             ).then_inc(w2_mm, 1)
            pe.wait_ge(h2_ready, STRIPS + 1)
            for t in range(ROWS // P):
                pe.wait_ge(z_ready, min(-(-(t + 1) * P // CHUNK), NC) + 1)
                if t >= ZW_BANKS:
                    pe.wait_ge(rows_ready, (t - ZW_BANKS) // 2 + 1)
                nc.tensor.matmul(bank[t % ZW_BANKS][:, 0:3 * F], z[0:F, t * P:(t + 1) * P], zw_s[:, :], start=True, stop=True
                                 ).then_inc(zw_mm, 1)
            pe.wait_ge(rows_ready, UV_PAIRS)
            pe.wait_ge(wide_ready, 1)
            nc.tensor.matmul(bank[7][0:1, 0:F], edge_shift[:, :], wmsg_s[:, 2, :], start=True, stop=False)
            nc.tensor.matmul(bank[7][0:1, 0:F], ones[0:1, 0:1], bmsg_s[:, :], start=False, stop=True)
            nc.tensor.matmul(bank[7][:, F:2 * F], wide[:, 0, :], ident[0:F, 0:F], start=True, stop=True).then_inc(const_mm, 1)
            pe.wait_ge(const_placed, 16 * SLOTS)
            pe.wait_ge(edge_row, 2)
            pe.wait_ge(L[1].acc_added, 2)

            with pe.If(ordered == 1):
                fast(1)
            with pe.Else():
                general(1)
            pe.wait_ge(L[1].swept, 1)

            for g in range(GROUP):
                mm = nc.tensor.matmul(bank[7][0:F, 0:1], sq_sum[:, g, :], ones[:, 0:1], start=(g == 0), stop=(g == GROUP - 1))
            mm.then_inc(sq_total, 1)
            pe.wait_ge(scales_ready, 1)
            nc.tensor.matmul(bank[1][0:F + 1, 0:F], scale_m[:, :], ident[0:F, 0:F], start=True, stop=True).then_inc(mats_mm, 1)
            pe.wait_ge(mats_ready, 1)
            for k, (t0, nt) in enumerate(FIN):
                if k >= 4:
                    pe.wait_ge(fin_var, k - 3)
                for i in range(nt):
                    nodes = slice((t0 + i) * P, (t0 + i + 1) * P)
                    mm = nc.tensor.matmul(bank[2 + k % 4][:, i * F:(i + 1) * F], acc[:, nodes], mat_m[:, :], start=True, stop=True)
                mm.then_inc(fin_mm, 1)


def kernel(**inputs):
    import numpy as np
    import concourse.bacc as bacc
    from concourse import mybir as _mybir
    from concourse.bass_utils import run_bass_kernel_spmd

    a = {k: np.asarray(v) for k, v in inputs.items()}

    def padded(v, fill):
        out = np.full((EPAD,) + v.shape[1:], fill, v.dtype)
        out[:E] = v
        return out

    def rows(v):
        out = np.zeros((v.shape[1] + 1, EPAD), v.dtype)
        out[:-1, :E] = v.T
        out[-1, :E] = 1
        return out

    src, dst = padded(a["src"], 0), padded(a["dst"], N)
    vectors = ["L0_gnn_b1", "L0_gnn_b2", "L0_gnn_gamma", "L0_gnn_beta", "L1_gnn_b_node", "L1_gnn_g_node",
               "L1_gnn_beta_node", "L1_gnn_g_edge", "L1_gnn_beta_edge", "L1_gnn_g_msg", "L1_gnn_beta_msg"]
    arrays = {
        "x": a["x"],
        "x_t": a["x"].T,
        "src_tiles": src.reshape(-1, P).T,
        "dst_tiles": dst.reshape(-1, P).T,
        "dst_first": dst[:MACROS * MACRO:MACRO].reshape(1, MACROS),
        "dst_row": dst.reshape(1, EPAD),
        "ea32_blocks": rows(a["edge_attr_32"]).reshape(D0 + 1, -1, MACRO).transpose(1, 0, 2),
        "ea4_rows": rows(a["edge_attr_4"]),
        "we_b": np.concatenate([a["L0_gnn_We"], a["L0_gnn_be"][None]]),
        "w1": a["L0_gnn_W1"],
        "w2": a["L0_gnn_W2"],
        "w_node": a["L1_gnn_W_node"],
        "w_edge_b": np.concatenate([a["L1_gnn_W_edge"], a["L1_gnn_b_edge"][None]]),
        "w_msg": a["L1_gnn_W_msg"],
        "b_msg": a["L1_gnn_b_msg"][None],
        "node_vectors": np.stack([a[n] for n in vectors], axis=1),
    }
    arrays = {k: np.ascontiguousarray(v) for k, v in arrays.items()}
    nc = bacc.Bacc("TRN2", target_bir_lowering=False, num_devices=1)
    args = [nc.dram_tensor(k, v.shape, _mybir.dt.from_np(v.dtype), kind="ExternalInput").ap() for k, v in arrays.items()]
    out = nc.dram_tensor("out", (N, F), _mybir.dt.float32, kind="ExternalOutput").ap()
    build(nc, *args, out)
    r = run_bass_kernel_spmd(nc, [arrays], core_ids=[0])
    return r.results[0]["out"]
```
